# Optimizing a Trainium2 kernel written in Bass

```python
import numpy as np
import jax
import jax.numpy as jnp

def _softmax(x, axis=-1):
    return jax.nn.softmax(x, axis=axis)

def _gelu(x):
    return jax.nn.gelu(x, approximate=True)

def _silu(x):
    return jax.nn.silu(x)

def _sigmoid(x):
    return jax.nn.sigmoid(x)

def _layernorm(x, axis=-1, eps=1e-05):
    m = jnp.mean(x, axis=axis, keepdims=True)
    v = jnp.var(x, axis=axis, keepdims=True)
    return (x - m) / jnp.sqrt(v + eps)

def _scatter_add(tgt, idx, src, axis=0):
    return tgt.at[idx].add(src)

def _segment_sum(src, seg, n):
    return jax.ops.segment_sum(src, seg, n)
kernel_name = 'mk_audio_tower_d4_tok_audfeat256_r4_e63757'

def setup_inputs(seed: int=0):
    np.random.seed(seed)
    _w = jnp.asarray

    def _rec_inputs():
        import jax
        import jax.numpy as jnp
        _rk = jax.random.key(seed)
        x = -5.07413e-05 + 0.999912 * jax.random.normal(jax.random.fold_in(_rk, 1), (32, 256, 64), jnp.float32)
        return x
    x = _rec_inputs()

    def _L0_tok_setup():
        import jax, jax.numpy as jnp
        from jax import lax
        import numpy as np
        B, T, C, K, STRIDE = (16, 4000, 64, 5, 2)
        EPS = 0.001
        key = jax.random.key(seed)
        k0, k1, k2, k3 = jax.random.split(key, 4)
        x = jax.random.normal(k0, (B, T, C), dtype=jnp.float32)
        w = jax.random.normal(k1, (K, 1, C), dtype=jnp.float32) * 0.1
        b = jax.random.normal(k2, (C,), dtype=jnp.float32) * 0.01
        gamma = jnp.ones((C,), dtype=jnp.float32)
        beta = jnp.zeros((C,), dtype=jnp.float32)
        alpha = jnp.full((C,), 0.25, dtype=jnp.float32) + 0.01 * jax.random.normal(k3, (C,), dtype=jnp.float32)
        return {'x': x, 'w': w, 'b': b, 'gamma': gamma, 'beta': beta, 'alpha': alpha}
    _L0_tok_all = _L0_tok_setup()
    _L0_tok_in = {k: v for k, v in _L0_tok_all.items() if k in ('w', 'b', 'gamma', 'beta', 'alpha')}
    del _L0_tok_all

    def _L0_attn_setup():
        import jax, jax.numpy as jnp
        import numpy as np
        F = 64
        key = jax.random.key(seed)
        ks = jax.random.split(key, 6)
        s = 1.0 / np.sqrt(F)
        x = jax.random.normal(ks[0], (16, 256, F), dtype=jnp.float32)
        W_alpha = jax.random.uniform(ks[1], (F, F), minval=-s, maxval=s, dtype=jnp.float32)
        W_beta = jax.random.uniform(ks[2], (F, F), minval=-s, maxval=s, dtype=jnp.float32)
        W_unary = jax.random.uniform(ks[3], (F, F), minval=-s, maxval=s, dtype=jnp.float32)
        b_unary = jax.random.uniform(ks[4], (F,), minval=-s, maxval=s, dtype=jnp.float32)
        W_r = jax.random.uniform(ks[5], (F, F), minval=-s, maxval=s, dtype=jnp.float32)
        return {'x': x, 'W_alpha': W_alpha, 'W_beta': W_beta, 'W_unary': W_unary, 'b_unary': b_unary, 'W_r': W_r}
    _L0_attn_all = _L0_attn_setup()
    _L0_attn_in = {k: v for k, v in _L0_attn_all.items() if k in ('W_alpha', 'W_beta', 'W_unary', 'b_unary', 'W_r')}
    del _L0_attn_all

    def _L0_ffn_setup():
        import jax, jax.numpy as jnp
        import numpy as np
        NUM_EXPERTS = 8
        TOP_K = 2
        B, S, D = (8, 2048, 64)

        def _moe(tokens, router_w, w1, b1, w2, b2):
            N = tokens.shape[0]
            E = router_w.shape[0]
            logits = tokens.astype(jnp.float32) @ router_w.astype(jnp.float32).T
            probs = jax.nn.softmax(logits, axis=-1)
            rw, re = jax.lax.top_k(probs, TOP_K)
            if TOP_K > 1:
                rw = rw / jnp.maximum(rw.sum(-1, keepdims=True), 1e-12)
            rw = rw.astype(tokens.dtype)
            combine = jnp.zeros((N, E), tokens.dtype).at[jnp.arange(N)[:, None], re].set(rw)
            out = tokens
            for e in range(E):
                h = jax.nn.gelu(tokens @ w1[e] + b1[e], approximate=False)
                y = h @ w2[e] + b2[e]
                out = out + combine[:, e:e + 1] * y
            return out
        key = jax.random.key(seed)
        ks = jax.random.split(key, 4)
        scale = 1.0 / np.sqrt(D).astype(np.float32)
        return {'input_embeddings': jax.random.normal(ks[0], (B, S, D), jnp.float32), 'router_w': jax.random.normal(ks[1], (NUM_EXPERTS, D), jnp.float32) * scale, 'w1': jax.random.normal(ks[2], (NUM_EXPERTS, D, D), jnp.float32) * scale, 'b1': jnp.zeros((NUM_EXPERTS, D), jnp.float32), 'w2': jax.random.normal(ks[3], (NUM_EXPERTS, D, D), jnp.float32) * scale, 'b2': jnp.zeros((NUM_EXPERTS, D), jnp.float32)}
    _L0_ffn_all = _L0_ffn_setup()
    _L0_ffn_in = {k: v for k, v in _L0_ffn_all.items() if k in ('router_w', 'w1', 'b1', 'w2', 'b2')}
    del _L0_ffn_all

    def _L1_attn_setup():
        import jax, jax.numpy as jnp
        import numpy as np
        key = jax.random.key(seed)
        k1, k2 = jax.random.split(key)
        B, N, F = (4, 1024, 64)
        nodes = jax.random.normal(k1, (B, N, F), dtype=jnp.float32)
        limit = np.sqrt(6.0 / (F + F)).astype(np.float32)
        W = jax.random.uniform(k2, (F, F), dtype=jnp.float32, minval=-limit, maxval=limit)
        return {'nodes': nodes, 'W': W}
    _L1_attn_all = _L1_attn_setup()
    _L1_attn_in = {k: v for k, v in _L1_attn_all.items() if k in ('W',)}
    del _L1_attn_all

    def _L1_ffn_setup():
        import jax, jax.numpy as jnp
        import numpy as np
        E = 8
        K = 2
        D = 64
        H = 128
        DOUT = 64
        EPS = 1e-05
        key = jax.random.key(seed)
        ks = jax.random.split(key, 9)
        s = 0.02
        return {'x': jax.random.normal(ks[0], (4, 2048, D), jnp.float32), 'gamma': 1.0 + 0.05 * jax.random.normal(ks[1], (D,), jnp.float32), 'beta': 0.05 * jax.random.normal(ks[2], (D,), jnp.float32), 'Wr': 0.01 * jax.random.normal(ks[3], (D, E), jnp.float32), 'br': jnp.zeros((E,), jnp.float32), 'W1': s * jax.random.normal(ks[4], (E, D, H), jnp.float32), 'b1': s * jax.random.normal(ks[5], (E, H), jnp.float32), 'W2': s * jax.random.normal(ks[6], (E, H, DOUT), jnp.float32), 'b2': s * jax.random.normal(ks[7], (E, DOUT), jnp.float32)}
    _L1_ffn_all = _L1_ffn_setup()
    _L1_ffn_in = {k: v for k, v in _L1_ffn_all.items() if k in ('gamma', 'beta', 'Wr', 'br', 'W1', 'b1', 'W2', 'b2')}
    del _L1_ffn_all

    def _L2_attn_setup():
        import jax, jax.numpy as jnp
        import numpy as np
        H, D = (8, 32)
        EPS = 1e-05
        key = jax.random.key(seed)
        ks = jax.random.split(key, 4)
        B, N, C = (2, 512, 64)
        inner = H * D
        return {'node_features': jax.random.normal(ks[0], (B, N, C), jnp.float32), 'ln_gamma': jnp.ones((C,), jnp.float32), 'ln_beta': jnp.zeros((C,), jnp.float32), 'W_qkv': jax.random.normal(ks[1], (3 * inner, C), jnp.float32) * 0.02, 'W_gate': jax.random.normal(ks[2], (inner, C), jnp.float32) * 0.02, 'b_gate': jnp.ones((inner,), jnp.float32), 'W_final': jax.random.normal(ks[3], (C, inner), jnp.float32) * 0.02, 'b_final': jnp.zeros((C,), jnp.float32)}
    _L2_attn_all = _L2_attn_setup()
    _L2_attn_in = {k: v for k, v in _L2_attn_all.items() if k in ('ln_gamma', 'ln_beta', 'W_qkv', 'W_gate', 'b_gate', 'W_final', 'b_final')}
    del _L2_attn_all

    def _L2_ffn_setup():
        import jax, jax.numpy as jnp
        import numpy as np
        INPUT_WIDTH = 64
        DEPTH = 7
        OUTPUT_WIDTH = 64
        N_NODES = 2 ** (DEPTH + 1) - 1
        key = jax.random.key(seed)
        k_x, k_w1, k_w2 = jax.random.split(key, 3)
        init1 = 1.0 / np.sqrt(INPUT_WIDTH)
        x = jax.random.normal(k_x, (2, 256, INPUT_WIDTH), dtype=jnp.float32)
        w1s = jax.random.uniform(k_w1, (N_NODES, INPUT_WIDTH), jnp.float32, -init1, init1)
        b1s = jnp.zeros((N_NODES,), jnp.float32)
        w2s = jax.random.uniform(k_w2, (N_NODES, INPUT_WIDTH, OUTPUT_WIDTH), jnp.float32, -init1, init1)
        b2s = jnp.zeros((N_NODES, OUTPUT_WIDTH), jnp.float32)
        return {'x': x, 'w1s': w1s, 'b1s': b1s, 'w2s': w2s, 'b2s': b2s}
    _L2_ffn_all = _L2_ffn_setup()
    _L2_ffn_in = {k: v for k, v in _L2_ffn_all.items() if k in ('w1s', 'b1s', 'w2s', 'b2s')}
    del _L2_ffn_all

    def _L3_attn_setup():
        import jax, jax.numpy as jnp
        import numpy as np
        key = jax.random.key(seed)
        k1, k2, k3 = jax.random.split(key, 3)
        b, n_t, n, n_h = (8, 256, 64, 8)
        s = jax.random.normal(k1, (b, n_t, n), dtype=jnp.float32)
        Q = jax.random.normal(k2, (n_h, n, n), dtype=jnp.float32) * 0.02
        E = jax.random.normal(k3, (n_h, n, n), dtype=jnp.float32) * 0.02
        return {'s': s, 'Q': Q, 'E': E}
    _L3_attn_all = _L3_attn_setup()
    _L3_attn_in = {k: v for k, v in _L3_attn_all.items() if k in ('Q', 'E')}
    del _L3_attn_all

    def _L3_ffn_setup():
        import jax, jax.numpy as jnp
        import numpy as np
        DIM = 64
        HEADS = 8
        NUM_KEYS = 64
        NUM_KV = NUM_KEYS ** 2
        PK_TOPK = 16
        FINAL_TOPK = 16
        DIM_KEY = DIM // 2
        P = 2

        def _pk(x, Wq_pk, pk_keys):
            b, n, _ = x.shape
            q = (x @ Wq_pk).reshape(b, n, P, HEADS, DIM_KEY).transpose(2, 0, 1, 3, 4)
            sim = jnp.einsum('pbnhd,pkhd->pbnhk', q, pk_keys)
            scores, idx = jax.lax.top_k(sim, PK_TOPK)
            idx0 = idx[0]
            idx1 = idx[1] * NUM_KEYS
            index = (idx0[..., :, None] + idx1[..., None, :]).reshape(b, n, HEADS, PK_TOPK * PK_TOPK)
            score = (scores[0][..., :, None] + scores[1][..., None, :]).reshape(b, n, HEADS, PK_TOPK * PK_TOPK)
            final_scores, pk_idx = jax.lax.top_k(score, FINAL_TOPK)
            final_indices = jnp.take_along_axis(index, pk_idx, axis=-1)
            final_scores = jax.nn.softmax(final_scores, axis=-1)
            return (final_scores, final_indices)
        key = jax.random.key(seed)
        ks = jax.random.split(key, 7)
        b, n = (2, 256)
        std = 0.02
        x = jax.random.normal(ks[0], (b, n, DIM), dtype=jnp.float32)
        Wq_pk = jax.random.normal(ks[1], (DIM, P * HEADS * DIM_KEY), dtype=jnp.float32) * std
        pk_keys = jax.random.normal(ks[2], (P, NUM_KEYS, HEADS, DIM_KEY), dtype=jnp.float32) * std
        Wq = jax.random.normal(ks[3], (DIM, HEADS * DIM), dtype=jnp.float32) * std
        keys_table = jax.random.normal(ks[4], (NUM_KV * HEADS, DIM), dtype=jnp.float32) * std
        values_table = jax.random.normal(ks[5], (NUM_KV * HEADS, DIM), dtype=jnp.float32) * std
        Wo = jax.random.normal(ks[6], (DIM * HEADS, DIM), dtype=jnp.float32) * std
        return {'x': x, 'Wq_pk': Wq_pk, 'pk_keys': pk_keys, 'Wq': Wq, 'keys_table': keys_table, 'values_table': values_table, 'Wo': Wo}
    _L3_ffn_all = _L3_ffn_setup()
    _L3_ffn_in = {k: v for k, v in _L3_ffn_all.items() if k in ('Wq_pk', 'pk_keys', 'Wq', 'keys_table', 'values_table', 'Wo')}
    del _L3_ffn_all
    return {'x': x, 'L0_tok_w': _L0_tok_in['w'], 'L0_tok_b': _L0_tok_in['b'], 'L0_tok_gamma': _L0_tok_in['gamma'], 'L0_tok_beta': _L0_tok_in['beta'], 'L0_tok_alpha': _L0_tok_in['alpha'], 'L0_attn_W_alpha': _L0_attn_in['W_alpha'], 'L0_attn_W_beta': _L0_attn_in['W_beta'], 'L0_attn_W_unary': _L0_attn_in['W_unary'], 'L0_attn_b_unary': _L0_attn_in['b_unary'], 'L0_attn_W_r': _L0_attn_in['W_r'], 'L0_ffn_router_w': _L0_ffn_in['router_w'], 'L0_ffn_w1': _L0_ffn_in['w1'], 'L0_ffn_b1': _L0_ffn_in['b1'], 'L0_ffn_w2': _L0_ffn_in['w2'], 'L0_ffn_b2': _L0_ffn_in['b2'], 'L1_attn_W': _L1_attn_in['W'], 'L1_ffn_gamma': _L1_ffn_in['gamma'], 'L1_ffn_beta': _L1_ffn_in['beta'], 'L1_ffn_Wr': _L1_ffn_in['Wr'], 'L1_ffn_br': _L1_ffn_in['br'], 'L1_ffn_W1': _L1_ffn_in['W1'], 'L1_ffn_b1': _L1_ffn_in['b1'], 'L1_ffn_W2': _L1_ffn_in['W2'], 'L1_ffn_b2': _L1_ffn_in['b2'], 'L2_attn_ln_gamma': _L2_attn_in['ln_gamma'], 'L2_attn_ln_beta': _L2_attn_in['ln_beta'], 'L2_attn_W_qkv': _L2_attn_in['W_qkv'], 'L2_attn_W_gate': _L2_attn_in['W_gate'], 'L2_attn_b_gate': _L2_attn_in['b_gate'], 'L2_attn_W_final': _L2_attn_in['W_final'], 'L2_attn_b_final': _L2_attn_in['b_final'], 'L2_ffn_w1s': _L2_ffn_in['w1s'], 'L2_ffn_b1s': _L2_ffn_in['b1s'], 'L2_ffn_w2s': _L2_ffn_in['w2s'], 'L2_ffn_b2s': _L2_ffn_in['b2s'], 'L3_attn_Q': _L3_attn_in['Q'], 'L3_attn_E': _L3_attn_in['E'], 'L3_ffn_Wq_pk': _L3_ffn_in['Wq_pk'], 'L3_ffn_pk_keys': _L3_ffn_in['pk_keys'], 'L3_ffn_Wq': _L3_ffn_in['Wq'], 'L3_ffn_keys_table': _L3_ffn_in['keys_table'], 'L3_ffn_values_table': _L3_ffn_in['values_table'], 'L3_ffn_Wo': _L3_ffn_in['Wo']}

def reference(x, L0_tok_w, L0_tok_b, L0_tok_gamma, L0_tok_beta, L0_tok_alpha, L0_attn_W_alpha, L0_attn_W_beta, L0_attn_W_unary, L0_attn_b_unary, L0_attn_W_r, L0_ffn_router_w, L0_ffn_w1, L0_ffn_b1, L0_ffn_w2, L0_ffn_b2, L1_attn_W, L1_ffn_gamma, L1_ffn_beta, L1_ffn_Wr, L1_ffn_br, L1_ffn_W1, L1_ffn_b1, L1_ffn_W2, L1_ffn_b2, L2_attn_ln_gamma, L2_attn_ln_beta, L2_attn_W_qkv, L2_attn_W_gate, L2_attn_b_gate, L2_attn_W_final, L2_attn_b_final, L2_ffn_w1s, L2_ffn_b1s, L2_ffn_w2s, L2_ffn_b2s, L3_attn_Q, L3_attn_E, L3_ffn_Wq_pk, L3_ffn_pk_keys, L3_ffn_Wq, L3_ffn_keys_table, L3_ffn_values_table, L3_ffn_Wo):
    import jax
    import jax.numpy as jnp

    def _L0_tok_ref(x, w, b, gamma, beta, alpha):
        import jax, jax.numpy as jnp
        from jax import lax
        import numpy as np
        B, T, C, K, STRIDE = (16, 4000, 64, 5, 2)
        EPS = 0.001
        y = lax.conv_general_dilated(x, w, window_strides=(STRIDE,), padding='SAME', dimension_numbers=('NWC', 'WIO', 'NWC'), feature_group_count=C) + b
        mean = jnp.mean(y, axis=(1, 2), keepdims=True)
        var = jnp.var(y, axis=(1, 2), keepdims=True)
        yn = (y - mean) * lax.rsqrt(var + EPS) * gamma + beta
        return jnp.where(yn > 0, yn, alpha * yn)

    def _L0_attn_ref(x, W_alpha, W_beta, W_unary, b_unary, W_r):
        import jax, jax.numpy as jnp
        import numpy as np
        F = 64
        B, N, _ = x.shape
        alpha = jnp.einsum('bnf,gf->bng', x, W_alpha)
        beta = jnp.einsum('bnf,gf->bng', x, W_beta)
        unary = jnp.einsum('bnf,gf->bng', x, W_unary) + b_unary
        scores = jnp.einsum('bif,bjf->bij', alpha, beta)
        scores = scores * (1.0 - jnp.eye(N, dtype=x.dtype))
        att = jnp.einsum('bij,bjf->bif', scores, unary) / N
        out = jnp.einsum('bif,gf->big', att, W_r) + x
        return out

    def _L0_ffn_ref(input_embeddings, router_w, w1, b1, w2, b2):
        import jax, jax.numpy as jnp
        import numpy as np
        NUM_EXPERTS = 8
        TOP_K = 2
        B, S, D = (8, 2048, 64)

        def _moe(tokens, router_w, w1, b1, w2, b2):
            N = tokens.shape[0]
            E = router_w.shape[0]
            logits = tokens.astype(jnp.float32) @ router_w.astype(jnp.float32).T
            probs = jax.nn.softmax(logits, axis=-1)
            rw, re = jax.lax.top_k(probs, TOP_K)
            if TOP_K > 1:
                rw = rw / jnp.maximum(rw.sum(-1, keepdims=True), 1e-12)
            rw = rw.astype(tokens.dtype)
            combine = jnp.zeros((N, E), tokens.dtype).at[jnp.arange(N)[:, None], re].set(rw)
            out = tokens
            for e in range(E):
                h = jax.nn.gelu(tokens @ w1[e] + b1[e], approximate=False)
                y = h @ w2[e] + b2[e]
                out = out + combine[:, e:e + 1] * y
            return out
        b, s, d = input_embeddings.shape
        tokens = input_embeddings.reshape(b * s, d)
        return _moe(tokens, router_w, w1, b1, w2, b2).reshape(b, s, d)

    def _L1_attn_ref(nodes, W):
        import jax, jax.numpy as jnp
        import numpy as np
        F = nodes.shape[-1]
        norm_const = 1.0 / jnp.sqrt(jnp.asarray(F, dtype=nodes.dtype))
        x = jnp.einsum('bnf,fg->bng', nodes, W)
        prods = jnp.einsum('bnf,bmf->bnm', x, nodes)
        att_scores = jax.nn.softmax(prods * norm_const, axis=-1)
        messgs = jnp.einsum('bnm,bmf->bnf', att_scores, nodes)
        return messgs

    def _L1_ffn_ref(x, gamma, beta, Wr, br, W1, b1, W2, b2):
        import jax, jax.numpy as jnp
        import numpy as np
        E = 8
        K = 2
        D = 64
        H = 128
        DOUT = 64
        EPS = 1e-05
        mu = jnp.mean(x, axis=-1, keepdims=True)
        var = jnp.mean(jnp.square(x - mu), axis=-1, keepdims=True)
        xn = (x - mu) * jax.lax.rsqrt(var + EPS) * gamma + beta
        logits = jnp.einsum('bsd,de->bse', xn, Wr) + br
        top_vals, top_idx = jax.lax.top_k(logits, K)
        w = jax.nn.softmax(top_vals, axis=-1)
        w_full = jnp.einsum('bsk,bske->bse', w, jax.nn.one_hot(top_idx, E, dtype=w.dtype))
        y = jnp.zeros(x.shape[:-1] + (DOUT,), x.dtype)
        for e in range(E):
            h = jax.nn.gelu(jnp.einsum('bsd,dh->bsh', xn, W1[e]) + b1[e], approximate=False)
            y_e = jnp.einsum('bsh,hd->bsd', h, W2[e]) + b2[e]
            y = y + y_e * w_full[..., e, None]
        return y

    def _L2_attn_ref(node_features, ln_gamma, ln_beta, W_qkv, W_gate, b_gate, W_final, b_final):
        import jax, jax.numpy as jnp
        import numpy as np
        H, D = (8, 32)
        EPS = 1e-05
        x = node_features
        B, N, _ = x.shape
        mu = jnp.mean(x, axis=-1, keepdims=True)
        var = jnp.mean(jnp.square(x - mu), axis=-1, keepdims=True)
        normed = (x - mu) / jnp.sqrt(var + EPS) * ln_gamma + ln_beta
        qkv = normed @ W_qkv.T
        q, k, v = jnp.split(qkv, 3, axis=-1)

        def to_heads(t):
            return t.reshape(B, N, H, D).transpose(0, 2, 1, 3)
        q, k, v = (to_heads(q), to_heads(k), to_heads(v))
        gate = jax.nn.sigmoid(to_heads(x @ W_gate.T + b_gate))
        scores = jnp.einsum('bhid,bhjd->bhij', q, k) * D ** (-0.5)
        attn = jax.nn.softmax(scores, axis=-1)
        out = jnp.einsum('bhij,bhid->bhjd', attn, v) * gate
        out = out.transpose(0, 2, 1, 3).reshape(B, N, H * D)
        return x + out @ W_final.T + b_final

    def _L2_ffn_ref(x, w1s, b1s, w2s, b2s):
        import jax, jax.numpy as jnp
        import numpy as np
        INPUT_WIDTH = 64
        DEPTH = 7
        OUTPUT_WIDTH = 64
        N_NODES = 2 ** (DEPTH + 1) - 1
        B, S, D = x.shape
        flat_x = x.reshape(B * S, D)
        T = flat_x.shape[0]
        current = jnp.zeros((T,), dtype=jnp.int32)
        all_nodes = []
        all_logits = []
        for _ in range(DEPTH + 1):
            all_nodes.append(current)
            score = jnp.einsum('td,td->t', flat_x, w1s[current]) + b1s[current]
            all_logits.append(score)
            choice = ((jnp.sign(score) + 1.0) / 2.0).astype(jnp.int32)
            current = current * 2 + choice + 1
        logits = jnp.stack(all_logits, axis=1)
        path_weights = jax.nn.gelu(jnp.abs(logits), approximate=False)
        out = jnp.zeros((T, OUTPUT_WIDTH), dtype=x.dtype)
        for i in range(DEPTH + 1):
            nodes_i = all_nodes[i]
            t_i = jnp.einsum('td,tdo->to', flat_x, w2s[nodes_i]) + b2s[nodes_i]
            out = out + t_i * path_weights[:, i][:, None]
        return out.reshape(B, S, OUTPUT_WIDTH)

    def _L3_attn_ref(s, Q, E):
        import jax, jax.numpy as jnp
        import numpy as np
        n_t = s.shape[1]
        qs = jnp.einsum('bti,hij->bhtj', s, Q)
        Omega = jnp.einsum('bhtj,buj->bhtu', qs, s)
        mask = jnp.tril(jnp.ones((n_t, n_t), dtype=s.dtype))
        Omega = Omega * mask
        es = jnp.einsum('hij,buj->bhui', E, s)
        r = jnp.einsum('bhtu,bhui->bti', Omega, es)
        return r

    def _L3_ffn_ref(x, Wq_pk, pk_keys, Wq, keys_table, values_table, Wo):
        import jax, jax.numpy as jnp
        import numpy as np
        DIM = 64
        HEADS = 8
        NUM_KEYS = 64
        NUM_KV = NUM_KEYS ** 2
        PK_TOPK = 16
        FINAL_TOPK = 16
        DIM_KEY = DIM // 2
        P = 2

        def _pk(x, Wq_pk, pk_keys):
            b, n, _ = x.shape
            q = (x @ Wq_pk).reshape(b, n, P, HEADS, DIM_KEY).transpose(2, 0, 1, 3, 4)
            sim = jnp.einsum('pbnhd,pkhd->pbnhk', q, pk_keys)
            scores, idx = jax.lax.top_k(sim, PK_TOPK)
            idx0 = idx[0]
            idx1 = idx[1] * NUM_KEYS
            index = (idx0[..., :, None] + idx1[..., None, :]).reshape(b, n, HEADS, PK_TOPK * PK_TOPK)
            score = (scores[0][..., :, None] + scores[1][..., None, :]).reshape(b, n, HEADS, PK_TOPK * PK_TOPK)
            final_scores, pk_idx = jax.lax.top_k(score, FINAL_TOPK)
            final_indices = jnp.take_along_axis(index, pk_idx, axis=-1)
            final_scores = jax.nn.softmax(final_scores, axis=-1)
            return (final_scores, final_indices)
        b, n, d = x.shape
        q = (x @ Wq).reshape(b, n, HEADS, DIM) * DIM ** (-0.5)
        kv_scores, indices = _pk(x, Wq_pk, pk_keys)
        offsets = jnp.arange(HEADS, dtype=indices.dtype) * NUM_KV
        ind = indices + offsets[None, None, :, None]
        k = jnp.einsum('bnhk,bnhkd->bnhd', kv_scores, keys_table[ind])
        v = jnp.einsum('bnhk,bnhkd->bnhd', kv_scores, values_table[ind])
        sim = jnp.einsum('bihd,bjhd->bhij', q, k)
        neg = -jnp.finfo(sim.dtype).max
        causal = jnp.tril(jnp.ones((n, n), dtype=bool))
        sim = jnp.where(causal, sim, neg)
        attn = jax.nn.softmax(sim, axis=-1)
        out = jnp.einsum('bhij,bjhd->bhid', attn, v)
        out = out.transpose(0, 2, 1, 3).reshape(b, n, HEADS * DIM)
        return out @ Wo
    h = _L0_tok_ref(x, L0_tok_w, L0_tok_b, L0_tok_gamma, L0_tok_beta, L0_tok_alpha)
    h = h + _L0_attn_ref(_layernorm(h, axis=-1), L0_attn_W_alpha, L0_attn_W_beta, L0_attn_W_unary, L0_attn_b_unary, L0_attn_W_r)
    h = h + _L0_ffn_ref(_layernorm(h, axis=-1), L0_ffn_router_w, L0_ffn_w1, L0_ffn_b1, L0_ffn_w2, L0_ffn_b2)
    h = h + _L1_attn_ref(_layernorm(h, axis=-1), L1_attn_W)
    h = h + _L1_ffn_ref(_layernorm(h, axis=-1), L1_ffn_gamma, L1_ffn_beta, L1_ffn_Wr, L1_ffn_br, L1_ffn_W1, L1_ffn_b1, L1_ffn_W2, L1_ffn_b2)
    h = h + _L2_attn_ref(_layernorm(h, axis=-1), L2_attn_ln_gamma, L2_attn_ln_beta, L2_attn_W_qkv, L2_attn_W_gate, L2_attn_b_gate, L2_attn_W_final, L2_attn_b_final)
    h = h + _L2_ffn_ref(_layernorm(h, axis=-1), L2_ffn_w1s, L2_ffn_b1s, L2_ffn_w2s, L2_ffn_b2s)
    h = h + _L3_attn_ref(_layernorm(h, axis=-1), L3_attn_Q, L3_attn_E)
    h = h + _L3_ffn_ref(_layernorm(h, axis=-1), L3_ffn_Wq_pk, L3_ffn_pk_keys, L3_ffn_Wq, L3_ffn_keys_table, L3_ffn_values_table, L3_ffn_Wo)
    return h

_drawn_inputs = setup_inputs


def setup_inputs(seed=0):
    import zlib

    import numpy as np

    out = dict(_drawn_inputs(seed))
    spreads = {'L0_tok_gamma': (1.0, 0.2),
     'L0_tok_beta': (0.0, 0.1),
     'L0_ffn_b1': (0.0, 0.1),
     'L0_ffn_b2': (0.0, 0.1),
     'L1_ffn_br': (0.0, 0.278),
     'L2_attn_ln_gamma': (1.0, 0.6),
     'L2_attn_ln_beta': (0.0, 0.8),
     'L2_attn_b_gate': (1.0, 0.6),
     'L2_attn_b_final': (0.0, 0.1),
     'L2_ffn_b1s': (0.0, 0.1),
     'L2_ffn_b2s': (0.0, 0.1)}
    factors = {'L1_ffn_gamma': 8.0,
     'L1_ffn_beta': 7.97,
     'L1_ffn_b1': 7.359,
     'L2_attn_W_gate': 8.0,
     'L2_attn_W_final': 2.768,
     'L3_ffn_Wq_pk': 64.0,
     'L3_ffn_pk_keys': 64.0,
     'L3_ffn_Wq': 64.0,
     'L3_ffn_keys_table': 64.0,
     'L3_ffn_values_table': 64.0,
     'L3_ffn_Wo': 64.0}
    for name, (base, spread) in spreads.items():
        noise = np.random.default_rng([zlib.crc32(name.encode()), seed]).standard_normal(out[name].shape)
        drawn = base * np.exp(spread * noise) if base else spread * noise
        out[name] = jnp.asarray(drawn.astype(out[name].dtype))
    for name, factor in factors.items():
        out[name] = (out[name] * factor).astype(out[name].dtype)
    return out
```

```python
from contextlib import ExitStack

import numpy as np

import concourse.bass as bass
from concourse import mybir

ALU = mybir.AluOpType
ACT = mybir.ActivationFunctionType
AX = mybir.AxisListType
F32 = mybir.dt.float32

SEQS, T_IN, F = 32, 256, 64
T = T_IN // 2
TAPS = 5
GS = 4
GROUPS = SEQS // GS
TOK = GS * T
FB = F + 1
EXPERTS = 8
H2, D2 = 8, 32
NODES = 255
TREE_DEPTH = 7
PER = 8
HEADS = 8
KEYS = 64
TOPK = 16
CHUNKS = KEYS * KEYS // 128
DK = 32
BANKS = 8
LOWEST = -3.0e38
LN_EPS = 1e-5
TOK_EPS = 1e-3


def pack_columns():
    return {
        "ident": (128, 128), "mean128": (128, 128), "off_diag": (128, 128), "upper": (128, 128),
        "causal": (128, 128),
        "tok_w": (128, TAPS * F), "tok_b": (128, F), "tok_gamma": (128, F), "tok_beta": (128, F),
        "tok_alpha": (128, F),
        "wa": (F, F), "wb": (F, F), "wu": (FB, F), "wr": (F, F),
        "m0_router": (FB, EXPERTS), "m0_w1": (FB, EXPERTS * F), "m0_w2": (128, EXPERTS * F),
        "m0_b2": (1, EXPERTS * F),
        "a1_w": (F, F),
        "m1_gamma": (128, F), "m1_beta": (128, F),
        "m1_router": (FB, EXPERTS), "m1_w1": (FB, EXPERTS * 128), "m1_w2": (128, EXPERTS * F),
        "m1_b2": (1, EXPERTS * F),
        "a2_gamma": (128, F), "a2_beta": (128, F),
        "a2_wq": (F, H2 * D2), "a2_wk": (F, H2 * D2), "a2_wv": (F, H2 * D2),
        "a2_wg": (FB, H2 * D2), "a2_wf": (128, 2 * F), "a2_bf": (128, F),
        "tree_w1": (FB, NODES + 1),
        "a3_q": (F, HEADS * F), "a3_e": (F, HEADS * F),
    }


def lay_out(inp):
    f = np.float32
    rows = lambda v: np.broadcast_to(np.asarray(v).reshape(1, -1), (128, np.asarray(v).size))
    below = lambda w, b: np.concatenate([w, np.asarray(b).reshape(1, -1)], 0)
    zero = lambda n: np.zeros((1, n), f)
    r = np.arange(128)
    d = {"ident": np.eye(128, dtype=f), "mean128": np.full((128, 128), 1 / 128, f),
         "off_diag": (1 - np.eye(128, dtype=f)) / f(T),
         "upper": (r[:, None] <= r[None, :]).astype(f),
         "causal": np.where(r[:, None] >= r[None, :], f(0), f(LOWEST)).astype(f)}
    d["tok_w"] = rows(inp["L0_tok_w"][:, 0, :])
    for k in ("b", "gamma", "beta", "alpha"):
        d["tok_" + k] = rows(inp["L0_tok_" + k])
    d["wa"], d["wb"], d["wr"] = inp["L0_attn_W_alpha"].T, inp["L0_attn_W_beta"].T, inp["L0_attn_W_r"].T
    d["wu"] = below(inp["L0_attn_W_unary"].T, inp["L0_attn_b_unary"])
    d["m0_router"] = np.concatenate([inp["L0_ffn_router_w"].T, zero(EXPERTS)], 0)
    d["m0_w1"] = below(inp["L0_ffn_w1"].transpose(1, 0, 2).reshape(F, -1), inp["L0_ffn_b1"])
    w2 = np.zeros((2, F, EXPERTS // 2, 2, F), f)
    for e in range(EXPERTS):
        w2[e % 2, :, e // 2, e % 2, :] = inp["L0_ffn_w2"][e]
    d["m0_w2"] = w2.reshape(128, EXPERTS * F)
    d["m0_b2"] = inp["L0_ffn_b2"].reshape(1, -1)
    d["a1_w"] = inp["L1_attn_W"]
    d["m1_gamma"], d["m1_beta"] = rows(inp["L1_ffn_gamma"]), rows(inp["L1_ffn_beta"])
    d["m1_router"] = below(inp["L1_ffn_Wr"], inp["L1_ffn_br"])
    d["m1_w1"] = below(inp["L1_ffn_W1"].transpose(1, 0, 2).reshape(F, -1), inp["L1_ffn_b1"])
    d["m1_w2"] = inp["L1_ffn_W2"].transpose(1, 0, 2).reshape(128, -1)
    d["m1_b2"] = inp["L1_ffn_b2"].reshape(1, -1)
    d["a2_gamma"], d["a2_beta"] = rows(inp["L2_attn_ln_gamma"]), rows(inp["L2_attn_ln_beta"])
    w = inp["L2_attn_W_qkv"].T
    d["a2_wq"], d["a2_wk"], d["a2_wv"] = w[:, :256], w[:, 256:512], w[:, 512:]
    d["a2_wg"] = below(inp["L2_attn_W_gate"].T, inp["L2_attn_b_gate"])
    d["a2_wf"] = inp["L2_attn_W_final"].T.reshape(2, 128, F).transpose(1, 0, 2).reshape(128, -1)
    d["a2_bf"] = rows(inp["L2_attn_b_final"])
    d["tree_w1"] = np.concatenate([below(inp["L2_ffn_w1s"].T, inp["L2_ffn_b1s"]), np.zeros((FB, 1), f)], 1)
    d["a3_q"] = inp["L3_attn_Q"].transpose(1, 0, 2).reshape(F, -1)
    d["a3_e"] = inp["L3_attn_E"].transpose(2, 0, 1).reshape(F, -1)
    cols = pack_columns()
    pack = np.zeros((128, sum(c for _, c in cols.values())), f)
    at = 0
    for name, (nr, nc_) in cols.items():
        assert d[name].shape == (nr, nc_), (name, d[name].shape)
        pack[:nr, at:at + nc_] = d[name]
        at += nc_

    x = np.concatenate([np.zeros((SEQS, 1, F), f), inp["x"], np.zeros((SEQS, 2, F), f)], 1)
    win = np.stack([x[:, k:k + 2 * T:2, :] for k in range(TAPS)], 2)
    win = win.reshape(GROUPS, GS, T, TAPS * F).transpose(0, 2, 1, 3)
    tree_w2 = np.concatenate([inp["L2_ffn_w2s"].transpose(1, 0, 2).reshape(F, -1),
                              inp["L2_ffn_b2s"].reshape(1, -1)], 0)
    head = np.zeros((HEADS, F, 320), f)
    wq_pk = inp["L3_ffn_Wq_pk"].reshape(F, 2, HEADS, DK)
    for h in range(HEADS):
        head[h, :, 0:64] = wq_pk[:, :, h, :].reshape(F, 64)
        for p in range(2):
            head[h, p * DK:(p + 1) * DK, 64 + p * KEYS:64 + (p + 1) * KEYS] = inp["L3_ffn_pk_keys"][p, :, h, :].T
        head[h, :, 192:256] = inp["L3_ffn_Wq"][:, h * F:(h + 1) * F]
        head[h, :, 256:320] = inp["L3_ffn_Wo"][h * F:(h + 1) * F, :]
    table = np.concatenate([inp["L3_ffn_keys_table"], inp["L3_ffn_values_table"]], 1)
    table = table.reshape(HEADS, CHUNKS, 128, 2 * F).transpose(0, 2, 1, 3).reshape(HEADS, 128, CHUNKS * 2 * F)
    sel = np.zeros((2, KEYS, CHUNKS, 2, KEYS), f)
    for c in range(CHUNKS):
        for j in range(2):
            sel[0, :, c, j, :] = np.eye(KEYS)
            sel[1, 2 * c + j, c, j, :] = 1
    sel = sel.reshape(128, CHUNKS * 128)
    arrays = {"pack": pack, "win": win.reshape(GROUPS, T, GS * TAPS * F), "tree_w2": tree_w2, "head": head,
              "table": table, "sel": sel}
    return {k: np.ascontiguousarray(v) for k, v in arrays.items()}


class Memory:
    pass


def spread(ap, axis, n):
    ap = ap.unsqueeze(axis)
    shape = list(ap.shape)
    shape[axis] = n
    return ap.to_broadcast(shape)


def chain_of(eng, sem):
    count = [0]

    def link(ins):
        count[0] += 1
        ins.then_inc(sem, 1)
        eng.wait_ge(sem, count[0])
    return link


class Norm:

    def __init__(self, m, name, src, dst, turned, bank=0, eps=LN_EPS):
        self.m, self.src, self.dst, self.turned, self.bank, self.eps = m, src, dst, turned, bank, eps
        self.var, self.std = m.sem(f"{name}_var"), m.sem(f"{name}_std")
        if turned is not None:
            self.normed, self.inps, self.ready = (m.sem(f"{name}_{x}") for x in ("normed", "turned_in_psum", "turned"))

    def dve_normalize(self, v, link):
        m = self.m
        for b in range(GS):
            last = v.bn_stats(m.stats[:, b, :], self.src[:, b, :])
        link(last)
        for b in range(GS):
            last = v.bn_aggr(m.moments[:, b, :], m.stats[:, b, :])
        link(last)
        v.tensor_scalar(m.var[:], m.moments[:, :, 1], self.eps, None, ALU.add).then_inc(self.var, 1)
        v.wait_ge(self.std, 1)
        link(v.reciprocal(m.rstd[:], m.std[:]))
        for b in range(GS):
            last = v.tensor_scalar(self.dst[:, b, :], self.src[:, b, :], m.moments[:, b, 0:1],
                                   m.rstd[:, b:b + 1], ALU.subtract, ALU.mult)
        return last

    def act_root(self, a):
        a.wait_ge(self.var, 1)
        a.activation(self.m.std[:], self.m.var[:], ACT.Sqrt).then_inc(self.std, 1)

    def pe_turn(self, pe):
        pe.wait_ge(self.normed, 1)
        for b in range(GS):
            last = pe.transpose(self.m.ps[0:F, self.bank, b * T:(b + 1) * T], self.dst[:, b, :], self.m.w["ident"])
        last.then_inc(self.inps, 1)

    def act_copy(self, a):
        a.wait_ge(self.inps, 1)
        a.copy(self.turned[0:F, :], self.m.ps[0:F, self.bank, :]).then_inc(self.ready, 1)


def layer0_tokens(nc, m, g):
    loaded, parts, sums, var, std, own = (m.sem("tok_" + x) for x in (
        "window_loaded", "partial_moments", "moments_in_psum", "var", "std", "dve"))
    with nc.Block() as block:
        @block.sync
        def _(sp):
            sp.dma_start(m.window[:].rearrange("p b k -> p (b k)"), m.dram["win"][g]).then_inc(loaded, 16)

        @block.vector
        def _(v):
            link = chain_of(v, own)
            v.wait_ge(loaded, 16)
            link(v.tensor_tensor(m.window[:], m.window[:], spread(m.w["tok_w"], 1, GS), ALU.mult))
            link(v.tensor_reduce(m.n[:], m.window[:].rearrange("p b (k f) -> p b f k", k=TAPS), AX.X, ALU.add))
            link(v.tensor_tensor(m.n[:], m.n[:], spread(m.w["tok_b"], 1, GS), ALU.add))
            for b in range(GS):
                last = v.bn_stats(m.stats[:, b, :], m.n[:, b, :])
            link(last)
            for b in range(GS):
                last = v.bn_aggr(m.moments[:, b, :], m.stats[:, b, :])
            link(last)
            link(v.tensor_copy(m.small[:, 0:GS], m.moments[:, :, 0]))
            link(v.tensor_tensor(m.small[:, GS:2 * GS], m.small[:, 0:GS], m.small[:, 0:GS], ALU.mult))
            v.tensor_tensor(m.small[:, GS:2 * GS], m.small[:, GS:2 * GS], m.moments[:, :, 1], ALU.add).then_inc(parts, 1)
            v.wait_ge(sums, 1)
            link(v.tensor_copy(m.small[:, 0:2 * GS], m.ps[:, 0, 0:2 * GS]))
            link(v.tensor_tensor(m.small[:, 2 * GS:3 * GS], m.small[:, 0:GS], m.small[:, 0:GS], ALU.mult))
            link(v.tensor_tensor(m.var[:], m.small[:, GS:2 * GS], m.small[:, 2 * GS:3 * GS], ALU.subtract))
            v.tensor_scalar(m.var[:], m.var[:], TOK_EPS, None, ALU.add).then_inc(var, 1)
            v.wait_ge(std, 1)
            link(v.reciprocal(m.rstd[:], m.std[:]))
            for b in range(GS):
                last = v.tensor_scalar(m.n[:, b, :], m.n[:, b, :], m.small[:, b:b + 1], m.rstd[:, b:b + 1],
                                       ALU.subtract, ALU.mult)
            link(last)
            link(v.tensor_tensor(m.n[:], m.n[:], spread(m.w["tok_gamma"], 1, GS), ALU.mult))
            link(v.tensor_tensor(m.n[:], m.n[:], spread(m.w["tok_beta"], 1, GS), ALU.add))
            link(v.scalar_tensor_tensor(m.n2[:], m.n[:], 0.0, spread(m.w["tok_alpha"], 1, GS), ALU.min, ALU.mult))
            link(v.scalar_tensor_tensor(m.h[:], m.n[:], 0.0, m.n2[:], ALU.max, ALU.add))

        @block.tensor
        def _(pe):
            pe.wait_ge(parts, 1)
            pe.matmul(m.ps[:, 0, 0:2 * GS], m.w["mean128"], m.small[:, 0:2 * GS], start=True, stop=True).then_inc(sums, 1)

        @block.scalar
        def _(a):
            a.wait_ge(var, 1)
            a.activation(m.std[:], m.var[:], ACT.Sqrt).then_inc(std, 1)


def layer0_attention(nc, m, g):
    norm = Norm(m, "l0a", m.h, m.n, m.nT)
    proj, copied, scored, masked, mixed, mixed_sb, out, own = (m.sem("l0a_" + x) for x in (
        "projected", "projections_copied", "scores", "scores_masked", "mixed", "mixed_copied", "out", "dve"))
    aT, bT = m.big[0:F, 0, :], m.big[0:F, 1, :]
    un, sT, mixT = m.big[:, 2, 0:GS * F], m.big[:, 3, :], m.big[0:F, 4, :]
    with nc.Block() as block:
        @block.tensor
        def _(pe):
            norm.pe_turn(pe)
            pe.wait_ge(norm.ready, 1)
            pe.matmul(m.ps[0:F, 1, :], m.w["wa"], m.nT[0:F, :], start=True, stop=True)
            pe.matmul(m.ps[0:F, 2, :], m.w["wb"], m.nT[0:F, :], start=True, stop=True)
            for b in range(GS):
                last = pe.matmul(m.ps[:, 3, b * F:(b + 1) * F], m.nT[:, b * T:(b + 1) * T], m.w["wu"], start=True, stop=True)
            last.then_inc(proj, 1)
            pe.wait_ge(copied, 3)
            for b in range(GS):
                at = slice(b * T, (b + 1) * T)
                last = pe.matmul(m.ps[:, 4, at], bT[:, at], aT[:, at], start=True, stop=True)
            last.then_inc(scored, 1)
            pe.wait_ge(masked, 1)
            for b in range(GS):
                at = slice(b * T, (b + 1) * T)
                last = pe.matmul(m.ps[0:F, 5, at], un[:, b * F:(b + 1) * F], sT[:, at], start=True, stop=True)
            last.then_inc(mixed, 1)
            pe.wait_ge(mixed_sb, 1)
            for b in range(GS):
                last = pe.matmul(m.ps[:, 6, b * F:(b + 1) * F], mixT[:, b * T:(b + 1) * T], m.w["wr"], start=True, stop=True)
            last.then_inc(out, 1)

        @block.scalar
        def _(a):
            norm.act_root(a)
            norm.act_copy(a)
            a.wait_ge(proj, 1)
            a.copy(aT, m.ps[0:F, 1, :]).then_inc(copied, 1)
            a.copy(bT, m.ps[0:F, 2, :]).then_inc(copied, 1)
            a.wait_ge(mixed, 1)
            a.copy(mixT, m.ps[0:F, 5, :]).then_inc(mixed_sb, 1)

        @block.vector
        def _(v):
            link = chain_of(v, own)
            norm.dve_normalize(v, link).then_inc(norm.normed, 1)
            v.wait_ge(proj, 1)
            v.tensor_copy(un, m.ps[:, 3, 0:GS * F]).then_inc(copied, 1)
            v.wait_ge(scored, 1)
            v.tensor_tensor(sT.rearrange("p (b t) -> p b t", b=GS), m.ps[:, 4, :].rearrange("p (b t) -> p b t", b=GS),
                            spread(m.w["off_diag"], 1, GS), ALU.mult).then_inc(masked, 1)
            v.wait_ge(norm.normed, 1)
            link(v.tensor_tensor(m.h[:], m.h[:], m.n[:], ALU.add))
            v.wait_ge(out, 1)
            link(v.tensor_tensor(m.h[:], m.h[:], m.ps[:, 6, 0:GS * F].rearrange("p (b f) -> p b f", b=GS), ALU.add))


def mixture(nc, m, which):
    name = f"l{which}m"
    units = (4, 8)[which]
    norm = Norm(m, name, m.h, m.n, m.nT, bank=0)
    if which:
        norm.src, norm.dst = m.n, m.n2
        first = Norm(m, name + "_first", m.h, m.n, None)
    logits, shifted, exped, hidden, acted, out, folded, own = (m.sem(f"{name}_{x}") for x in (
        "logits", "logits_shifted", "exp", "hidden", "gelu", "expert_outputs", "outputs_folded", "dve"))
    w1, w2, b2 = (m.w[f"m{which}_{x}"] for x in ("w1", "w2", "b2"))
    lg, mx, wt, tmp = (m.gate[:, i] for i in range(4))
    act = m.big
    with nc.Block() as block:
        @block.tensor
        def _(pe):
            norm.pe_turn(pe)
            pe.wait_ge(norm.ready, 1)
            for b in range(GS):
                last = pe.matmul(m.ps[:, 1, b * EXPERTS:(b + 1) * EXPERTS], m.nT[:, b * T:(b + 1) * T],
                                 m.w[f"m{which}_router"], start=True, stop=True)
            last.then_inc(logits, 1)
            for u in range(units):
                if u >= 2:
                    pe.wait_ge(acted, u - 1)
                pe.matmul(m.ps[:, 2 + u % 2, :], w1[:, u * 128:(u + 1) * 128], m.nT[:], start=True, stop=True).then_inc(hidden, 1)
            pe.wait_ge(acted, units)
            wide = EXPERTS * F // units
            for b in range(GS):
                pe.matmul(m.ps[:, 4 + b, :], m.ones[0:1, :], b2, start=True, stop=False)
                for u in range(units):
                    last = pe.matmul(m.ps[:, 4 + b, u * wide:(u + 1) * wide], act[:, u, b * T:(b + 1) * T],
                                     w2[:, u * wide:(u + 1) * wide], start=False, stop=u == units - 1)
                last.then_inc(out, 1)

        @block.scalar
        def _(a):
            if which:
                first.act_root(a)
            norm.act_root(a)
            norm.act_copy(a)
            a.wait_ge(shifted, 1)
            a.activation(tmp, tmp, ACT.Exp).then_inc(exped, 1)
            for u in range(units):
                a.wait_ge(hidden, u + 1)
                a.activation(act[:, u, :], m.ps[:, 2 + u % 2, :], ACT.Gelu).then_inc(acted, 1)

        @block.vector
        def _(v):
            link = chain_of(v, own)
            if which:
                link(first.dve_normalize(v, link))
                link(norm.dve_normalize(v, link))
                link(v.tensor_tensor(m.n2[:], m.n2[:], spread(m.w["m1_gamma"], 1, GS), ALU.mult))
                v.tensor_tensor(m.n2[:], m.n2[:], spread(m.w["m1_beta"], 1, GS), ALU.add).then_inc(norm.normed, 1)
            else:
                norm.dve_normalize(v, link).then_inc(norm.normed, 1)
                v.wait_ge(norm.normed, 1)
                link(v.tensor_tensor(m.h[:], m.h[:], m.n[:], ALU.add))
            v.wait_ge(logits, 1)
            link(v.tensor_copy(lg, m.ps[:, 1, 0:GS * EXPERTS].rearrange("p (b e) -> p b e", b=GS)))
            for b in range(GS):
                last = v.max(mx[:, b, :], lg[:, b, :])
            link(last)
            v.tensor_tensor(tmp, lg, mx[:, :, 0:1].to_broadcast([128, GS, EXPERTS]), ALU.subtract).then_inc(shifted, 1)
            link(v.tensor_tensor(wt, lg, mx[:, :, 1:2].to_broadcast([128, GS, EXPERTS]), ALU.is_ge))
            v.wait_ge(exped, 1)
            link(v.tensor_tensor(wt, wt, tmp, ALU.mult))
            link(v.tensor_reduce(m.small[:, 0:GS], wt, AX.X, ALU.add))
            link(v.reciprocal(m.small[:, 0:GS], m.small[:, 0:GS]))
            link(v.tensor_tensor(wt, wt, spread(m.small[:, 0:GS], 2, EXPERTS), ALU.mult))
            for b in range(GS):
                v.wait_ge(out, b + 1)
                link(v.tensor_tensor(m.wide[:, b % 2, :].rearrange("p (e f) -> p e f", e=EXPERTS),
                                     m.ps[:, 4 + b, :].rearrange("p (e f) -> p e f", e=EXPERTS),
                                     spread(wt[:, b, :], 2, F), ALU.mult))
                link(v.tensor_reduce(m.n2[:, b, :], m.wide[:, b % 2, :].rearrange("p (e f) -> p f e", e=EXPERTS),
                                     AX.X, ALU.add))
            link(v.tensor_tensor(m.h[:], m.h[:], m.n2[:], ALU.add))


def layer0_mixture(nc, m, g):
    mixture(nc, m, 0)


def layer1_mixture(nc, m, g):
    mixture(nc, m, 1)


def layer1_attention(nc, m, g):
    norm = Norm(m, "l1a", m.h, m.n, m.nT)
    proj, copied, scored, maxed, exped, turned, turned_sb, out, own = (m.sem("l1a_" + x) for x in (
        "projected", "projection_copied", "scores", "max", "exp", "probs_turned", "probs_copied", "out", "dve"))
    xT, p, pT = m.big[0:F, 0, :], m.big[:, 1, :], m.big[:, 2, :]
    mx, total = m.small[:, 0:GS], m.small[:, GS:2 * GS]
    scale = F ** -0.5
    with nc.Block() as block:
        @block.tensor
        def _(pe):
            norm.pe_turn(pe)
            pe.wait_ge(norm.ready, 1)
            pe.matmul(m.ps[0:F, 1, :], m.w["a1_w"], m.nT[0:F, :], start=True, stop=True).then_inc(proj, 1)
            pe.wait_ge(copied, 1)
            for b in range(GS):
                at = slice(b * T, (b + 1) * T)
                last = pe.matmul(m.ps[:, 2, at], xT[:, at], m.nT[0:F, at], start=True, stop=True)
            last.then_inc(scored, 1)
            for b in range(GS):
                at = slice(b * T, (b + 1) * T)
                pe.wait_ge(exped, b + 1)
                last = pe.transpose(m.ps[:, 3, at], p[:, at], m.w["ident"])
            last.then_inc(turned, 1)
            pe.wait_ge(turned_sb, 1)
            for b in range(GS):
                last = pe.matmul(m.ps[:, 4, b * F:(b + 1) * F], pT[:, b * T:(b + 1) * T], m.n[:, b, :], start=True, stop=True)
            last.then_inc(out, 1)

        @block.scalar
        def _(a):
            norm.act_root(a)
            norm.act_copy(a)
            a.wait_ge(proj, 1)
            a.copy(xT, m.ps[0:F, 1, :]).then_inc(copied, 1)
            a.wait_ge(maxed, 1)
            for b in range(GS):
                at = slice(b * T, (b + 1) * T)
                a.activation(p[:, at], m.ps[:, 2, at], ACT.Exp, bias=mx[:, b:b + 1], scale=scale,
                             accum_out=total[:, b:b + 1]).then_inc(exped, 1)
            a.wait_ge(turned, 1)
            a.copy(pT, m.ps[:, 3, :]).then_inc(turned_sb, 1)

        @block.vector
        def _(v):
            link = chain_of(v, own)
            norm.dve_normalize(v, link).then_inc(norm.normed, 1)
            v.wait_ge(scored, 1)
            link(v.tensor_reduce(mx, m.ps[:, 2, :].rearrange("p (b t) -> p b t", b=GS), AX.X, ALU.max))
            v.tensor_scalar(mx, mx, -scale, None, ALU.mult).then_inc(maxed, 1)
            v.wait_ge(exped, GS)
            link(v.reciprocal(m.rstd[:], total))
            v.wait_ge(out, 1)
            for b in range(GS):
                last = v.scalar_tensor_tensor(m.h[:, b, :], m.ps[:, 4, b * F:(b + 1) * F], m.rstd[:, b:b + 1],
                                              m.h[:, b, :], ALU.mult, ALU.add)
            link(last)


def layer2_attention(nc, m, g):
    norm = Norm(m, "l2a", m.h, m.n, m.nT, bank=0)
    norm2 = Norm(m, "l2a_own", m.n, m.n2, m.mT, bank=1)
    proj, copied, gated, scored, maxed, exped, vready, mixed, ogated, out, own = (m.sem("l2a_" + x) for x in (
        "projected", "projections_copied", "gate_tanh", "scores", "max", "exp", "values_scaled", "mixed", "gated",
        "out", "dve"))
    qT, kT, gT, og = m.big[:, 0:2, :], m.big[:, 2:4, :], m.big[:, 4:6, :], m.big[:, 6:8, :]
    scale = D2 ** -0.5
    pr = m.probs
    mx, total, rinv = (m.small[:, 16 * i:16 * (i + 1)] for i in range(3))
    with nc.Block() as block:
        @block.tensor
        def _(pe):
            norm.pe_turn(pe)
            norm2.pe_turn(pe)
            pe.wait_ge(norm.ready, 1)
            pe.wait_ge(norm2.ready, 1)
            for s in range(2):
                at = slice(s * 128, (s + 1) * 128)
                pe.matmul(m.ps[:, s, :], m.w["a2_wq"][:, at], m.mT[0:F, :], start=True, stop=True)
                pe.matmul(m.ps[:, 2 + s, :], m.w["a2_wk"][:, at], m.mT[0:F, :], start=True, stop=True)
                pe.matmul(m.ps[:, 4 + s, :], m.w["a2_wg"][:, at], m.nT[:], start=True, stop=True)
            for b in range(GS):
                last = pe.matmul(m.ps[:, 6 + b // 2, (b % 2) * 256:(b % 2 + 1) * 256], m.mT[0:F, b * T:(b + 1) * T],
                                 m.w["a2_wv"], start=True, stop=True)
            last.then_inc(proj, 1)
            pe.wait_ge(copied, 3)
            pe.wait_ge(gated, 1)
            for pair in range(2):
                for r in range(4):
                    rows = slice(32 * r, 32 * r + 32)
                    for b in range(2):
                        at = slice((2 * pair + b) * T, (2 * pair + b + 1) * T)
                        for s in range(2):
                            last = pe.matmul(m.ps[:, 4 * pair + r, (2 * b + s) * T:(2 * b + s + 1) * T],
                                             qT[rows, s, at], kT[rows, s, at], start=True, stop=True)
                last.then_inc(scored, 1)
            for pair in range(2):
                pe.wait_ge(exped, 16 * (pair + 1))
                pe.wait_ge(vready, pair + 1)
                for b in range(2):
                    bb = 2 * pair + b
                    for s in range(2):
                        for r in range(4):
                            col = (4 * s + r) * D2
                            last = pe.matmul(m.ps[32 * r:32 * r + 32, s, bb * T:(bb + 1) * T],
                                             m.values[:, bb, col:col + D2], pr[:, pair, r, b, s, :], start=True, stop=True)
                last.then_inc(mixed, 1)
            pe.wait_ge(ogated, 2)
            for b in range(GS):
                for s in range(2):
                    last = pe.matmul(m.ps[:, 2, b * F:(b + 1) * F], og[:, s, b * T:(b + 1) * T],
                                     m.w["a2_wf"][:, s * F:(s + 1) * F], start=s == 0, stop=s == 1)
            last.then_inc(out, 1)

        @block.scalar
        def _(a):
            norm.act_root(a)
            norm.act_copy(a)
            norm2.act_root(a)
            norm2.act_copy(a)
            a.wait_ge(proj, 1)
            a.activation(gT, m.ps[:, 4:6, :], ACT.Tanh, scale=0.5).then_inc(gated, 1)
            a.copy(qT, m.ps[:, 0:2, :]).then_inc(copied, 1)
            for pair in range(2):
                a.wait_ge(maxed, pair + 1)
                for i in range(16):
                    r, b, s = i // 4, i // 2 % 2, i % 2
                    a.activation(pr[:, pair, r, b, s, :], m.ps[:, 4 * pair + r, (i % 4) * T:(i % 4 + 1) * T], ACT.Exp,
                                 bias=m.l2max[:, pair, i:i + 1], scale=scale,
                                 accum_out=m.l2sum[:, pair, i:i + 1]).then_inc(exped, 1)

        @block.vector
        def _(v):
            link = chain_of(v, own)
            norm.dve_normalize(v, link).then_inc(norm.normed, 1)
            v.wait_ge(norm.normed, 1)
            link(norm2.dve_normalize(v, link))
            link(v.tensor_tensor(m.n2[:], m.n2[:], spread(m.w["a2_gamma"], 1, GS), ALU.mult))
            v.tensor_tensor(m.n2[:], m.n2[:], spread(m.w["a2_beta"], 1, GS), ALU.add).then_inc(norm2.normed, 1)
            link(v.tensor_tensor(m.h[:], m.h[:], m.n[:], ALU.add))
            link(v.tensor_tensor(m.h[:], m.h[:], spread(m.w["a2_bf"], 1, GS), ALU.add))
            v.wait_ge(proj, 1)
            v.tensor_copy(kT, m.ps[:, 2:4, :]).then_inc(copied, 1)
            v.tensor_copy(m.values[:].rearrange("p b c -> p (b c)"), m.ps[:, 6:8, :].rearrange("p k c -> p (k c)")).then_inc(copied, 1)
            v.wait_ge(gated, 1)
            link(v.tensor_scalar(gT, gT, 0.5, 0.5, ALU.mult, ALU.add))
            for pair in range(2):
                v.wait_ge(scored, pair + 1)
                link(v.tensor_reduce(m.l2max[:, pair, :],
                                     m.ps[:, 4 * pair:4 * pair + 4, :].rearrange("p r (c t) -> p r c t", t=T), AX.X, ALU.max))
                v.tensor_scalar(m.l2max[:, pair, :], m.l2max[:, pair, :], -scale, None, ALU.mult).then_inc(maxed, 1)
            v.wait_ge(copied, 3)
            for pair in range(2):
                v.wait_ge(exped, 16 * (pair + 1))
                link(v.reciprocal(rinv, m.l2sum[:, pair, :]))
                for b in range(2):
                    vals = m.values[:, 2 * pair + b, :].rearrange("p (s r d) -> p s r d", s=2, r=4)
                    by = rinv.rearrange("p (r b s) -> p b s r", r=4, b=2)[:, b]
                    last = v.tensor_tensor(vals, vals, spread(by, 3, D2), ALU.mult)
                last.then_inc(vready, 1)
                v.wait_ge(vready, pair + 1)
            v.wait_ge(mixed, 2)
            for s in range(2):
                v.tensor_tensor(og[:, s, :], m.ps[:, s, :], gT[:, s, :], ALU.mult).then_inc(ogated, 1)
            v.wait_ge(out, 1)
            link(v.tensor_tensor(m.h[:], m.h[:], m.ps[:, 2, 0:GS * F].rearrange("p (b f) -> p b f", b=GS), ALU.add))


def layer2_tree(nc, m, g):
    norm = Norm(m, "l2t", m.h, m.n, m.nT)
    scored, absed, acted, product, weighted, summed, own = (m.sem("l2t_" + x) for x in (
        "scores", "abs", "gelu", "products", "weighted", "summed", "dve"))
    right, ind, gate = m.tree[:, 0], m.tree[:, 1], m.tree[:, 2]
    scores = m.ps[:, 0:2, :].rearrange("p k (b n) -> p (k b) n", b=2)
    steps = [(b, c) for b in range(GS) for c in range((NODES + 1) // PER // 2)]
    with nc.Block() as block:
        @block.tensor
        def _(pe):
            norm.pe_turn(pe)
            pe.wait_ge(norm.ready, 1)
            for b in range(GS):
                last = pe.matmul(m.ps[:, b // 2, (b % 2) * 256:(b % 2 + 1) * 256], m.nT[:, b * T:(b + 1) * T],
                                 m.w["tree_w1"], start=True, stop=True)
            last.then_inc(scored, 1)
            for i, (b, c) in enumerate(steps):
                if i >= 3:
                    pe.wait_ge(weighted, i - 2)
                for k in range(2):
                    n = min(PER, NODES - (2 * c + k) * PER) * F
                    at = (2 * c + k) * PER * F
                    last = pe.matmul(m.ps[:, 2 + 2 * (i % 3) + k, 0:n], m.nT[:, b * T:(b + 1) * T],
                                     m.tree_w2[:, at:at + n], start=True, stop=True)
                last.then_inc(product, 1)

        @block.scalar
        def _(a):
            norm.act_root(a)
            norm.act_copy(a)
            a.wait_ge(scored, 1)
            a.activation(gate, scores, ACT.Abs).then_inc(absed, 1)
            a.wait_ge(absed, 1)
            a.activation(gate, gate, ACT.Gelu).then_inc(acted, 1)

        @block.vector
        def _(v):
            link = chain_of(v, own)
            norm.dve_normalize(v, link).then_inc(norm.normed, 1)
            v.wait_ge(absed, 1)
            link(v.tensor_scalar(right, scores, 0.0, None, ALU.is_gt))
            link(v.memset(ind[:, :, 0:1], 1.0))
            for level in range(TREE_DEPTH):
                lo, n = 2 ** level - 1, 2 ** level
                kids = ind[:, :, 2 * lo + 1:2 * lo + 1 + 2 * n].rearrange("p b (n k) -> p b n k", k=2)
                link(v.tensor_tensor(kids[:, :, :, 1], ind[:, :, lo:lo + n], right[:, :, lo:lo + n], ALU.mult))
                link(v.tensor_tensor(kids[:, :, :, 0], ind[:, :, lo:lo + n], kids[:, :, :, 1], ALU.subtract))
            v.wait_ge(acted, 1)
            link(v.tensor_tensor(gate[:, :, 0:NODES], gate[:, :, 0:NODES], ind[:, :, 0:NODES], ALU.mult))
            for i, (b, c) in enumerate(steps):
                n = min(2 * PER, NODES - 2 * c * PER)
                v.wait_ge(product, i + 1)
                if i >= 3:
                    v.wait_ge(summed, i - 2)
                v.tensor_tensor(m.weighted[:, i % 3, 0:n, :],
                                m.ps[:, 2 + 2 * (i % 3):4 + 2 * (i % 3), :].rearrange("p k (n f) -> p (k n) f", f=F)[:, 0:n, :],
                                spread(gate[:, b, 2 * c * PER:2 * c * PER + n], 2, F), ALU.mult).then_inc(weighted, 1)
            v.wait_ge(summed, len(steps))
            for b in range(GS):
                last = v.tensor_reduce(m.n2[:, b, :], m.summed[:, b].rearrange("p n f -> p f n"), AX.X, ALU.add)
            link(last)
            link(v.tensor_tensor(m.h[:], m.h[:], m.n2[:], ALU.add))

        @block.gpsimd
        def _(pool):
            for i, (b, c) in enumerate(steps):
                n = min(2 * PER, NODES - 2 * c * PER)
                pool.wait_ge(weighted, i + 1)
                if c:
                    pool.wait_ge(summed, i)
                    pool.tensor_tensor(m.summed[:, b, 0:n, :], m.summed[:, b, 0:n, :], m.weighted[:, i % 3, 0:n, :],
                                       ALU.add).then_inc(summed, 1)
                else:
                    pool.tensor_copy(m.summed[:, b], m.weighted[:, i % 3]).then_inc(summed, 1)


def layer3_attention(nc, m, g):
    norm = Norm(m, "l3a", m.h, m.n, m.nT)
    proj, copied, evals, ecopied, omega, masked, out, own = (m.sem("l3a_" + x) for x in (
        "queries", "queries_copied", "values", "values_copied", "omega", "omega_masked", "out", "dve"))
    qT = m.big
    with nc.Block() as block:
        @block.tensor
        def _(pe):
            norm.pe_turn(pe)
            pe.wait_ge(norm.ready, 1)
            for h in range(HEADS):
                if h >= 2:
                    pe.wait_ge(copied, h - 1)
                pe.matmul(m.ps[0:F, 1 + h % 2, :], m.w["a3_q"][:, h * F:(h + 1) * F], m.nT[0:F, :], start=True, stop=True).then_inc(proj, 1)
            pe.wait_ge(copied, HEADS)
            for b in range(GS):
                nb = m.nT[0:F, b * T:(b + 1) * T]
                if b >= 1:
                    pe.wait_ge(ecopied, b)
                pe.matmul(m.ps[:, 3, :], nb, m.w["a3_e"], start=True, stop=True).then_inc(evals, 1)
                for half in range(2):
                    i = 2 * b + half
                    if i >= 2:
                        pe.wait_ge(masked, i - 1)
                    pe.matmul(m.ps[:, 4 + half, :], nb, qT[0:F, 4 * half:4 * half + 4, b * T:(b + 1) * T], start=True,
                              stop=True).then_inc(omega, 1)
                pe.wait_ge(ecopied, b + 1)
                for half in range(2):
                    pe.wait_ge(masked, 2 * b + half + 1)
                    for k in range(4):
                        h = 4 * half + k
                        last = pe.matmul(m.ps[:, 6, b * F:(b + 1) * F], m.omega[:, half, k * T:(k + 1) * T],
                                         m.evals[:, b % 2, h * F:(h + 1) * F], start=h == 0, stop=h == HEADS - 1)
                last.then_inc(out, 1)

        @block.scalar
        def _(a):
            norm.act_root(a)
            norm.act_copy(a)
            for h in range(HEADS):
                a.wait_ge(proj, h + 1)
                a.copy(qT[0:F, h, :], m.ps[0:F, 1 + h % 2, :]).then_inc(copied, 1)
            for b in range(GS):
                a.wait_ge(evals, b + 1)
                if b >= 2:
                    a.wait_ge(out, b - 1)
                a.copy(m.evals[:, b % 2, :], m.ps[:, 3, :]).then_inc(ecopied, 1)

        @block.vector
        def _(v):
            link = chain_of(v, own)
            norm.dve_normalize(v, link).then_inc(norm.normed, 1)
            for b in range(GS):
                for half in range(2):
                    v.wait_ge(omega, 2 * b + half + 1)
                    if b >= 1:
                        v.wait_ge(out, b)
                    v.tensor_tensor(m.omega[:, half, :].rearrange("p (k t) -> p k t", t=T),
                                    m.ps[:, 4 + half, :].rearrange("p (k t) -> p k t", t=T),
                                    spread(m.w["upper"], 1, 4), ALU.mult).then_inc(masked, 1)
            v.wait_ge(out, GS)
            link(v.tensor_tensor(m.h[:], m.h[:], m.ps[:, 6, 0:GS * F].rearrange("p (b f) -> p b f", b=GS), ALU.add))


def layer3_input(nc, m, g):
    norm = Norm(m, "l3i", m.h, m.n, m.nT)
    own, kept = m.sem("l3i_dve"), m.sem("l3i_kept")
    with nc.Block() as block:
        @block.tensor
        def _(pe):
            norm.pe_turn(pe)

        @block.scalar
        def _(a):
            norm.act_root(a)
            a.wait_ge(norm.inps, 1)
            a.copy(m.nT_all[:, bass.ts(g, TOK)], m.ps[0:F, 0, :]).then_inc(kept, 1)
            a.wait_ge(kept, 1)

        @block.vector
        def _(v):
            link = chain_of(v, own)
            norm.dve_normalize(v, link).then_inc(norm.normed, 1)
            link(v.tensor_copy(m.h_all[:, bass.ts(g, GS * F)], m.h[:].rearrange("p b f -> p (b f)")))


LAYERS = [layer0_tokens, layer0_attention, layer0_mixture, layer1_attention, layer1_mixture,
          layer2_attention, layer2_tree, layer3_attention]


def load_head(nc, m, h):
    loaded = m.sem("head_loaded")
    with nc.Block() as block:
        @block.sync
        def _(sp):
            sp.dma_start(m.table[:], m.dram["table"][h]).then_inc(loaded, 16)
            sp.dma_start(m.head[:], m.dram["head"][h]).then_inc(loaded, 16)
            sp.wait_ge(loaded, 32)


def stairs():
    return [(0, 1, 16), (1, 1, 8), (2, 2, 5), (4, 4, 3), (8, 8, 1)]


def memory_and_attention(nc, m, g):
    names = ("input", "query_in_psum", "query", "scores_in_psum", "scores", "best", "threshold", "exp16", "limits",
             "scores_turned", "scores_copied", "spread_in_psum", "sum", "exp", "weights", "table_product", "kv",
             "kv_turned", "values", "attn_scores", "attn_max", "attn_exp", "probs_turned", "probs_copied", "mixed",
             "mixed_copied", "out")
    s = {n: m.sem("pk_" + n) for n in names}
    own = m.sem("pk_dve")
    wq_pk, keys, wq, wo = m.head[:, 0:64], m.head[:, 64:192], m.head[:, 192:256], m.head[:, 256:320]
    x, qT, aT = m.big[0:F, 0, :], m.big[0:F, 1, :], m.big[0:F, 2, :]
    sc, scT, kvT = m.big[:, 3, :], m.big[:, 4, :], m.big[:, 5, :]
    probs, probsT, mixT = m.big[:, 6, :], m.big[:, 7, :], m.big[0:F, 3, :]
    floor, rinv = m.floor[:, 0, :], m.floor[:, 1, :]
    cand = m.cand
    scb = sc.rearrange("p (b s k) -> p b s k", b=GS, s=2)
    v16, top = m.v16, m.top
    scale = F ** -0.5
    with nc.Block() as block:
        @block.tensor
        def _(pe):
            pe.wait_ge(s["input"], 1)
            pe.matmul(m.ps[0:F, 0, :], wq_pk, x, start=True, stop=True)
            pe.matmul(m.ps[0:F, 1, :], wq, x, start=True, stop=True).then_inc(s["query_in_psum"], 1)
            pe.wait_ge(s["query"], 2)
            for b in range(GS):
                last = pe.matmul(m.ps[:, 2, b * 128:(b + 1) * 128], qT[:, b * T:(b + 1) * T], keys, start=True, stop=True)
            last.then_inc(s["scores_in_psum"], 1)
            pe.wait_ge(s["limits"], 1)
            for b in range(GS):
                at = slice(b * T, (b + 1) * T)
                last = pe.transpose(m.ps[:, 3, at], sc[:, at], m.w["ident"])
            last.then_inc(s["scores_turned"], 1)
            for b in range(GS):
                at = slice(b * T, (b + 1) * T)
                for i in range(2):
                    last = pe.matmul(m.ps[:, i, at], m.limit[:, i, b:b + 1].to_broadcast([128, 128]), m.w["ident"],
                                     start=True, stop=True)
            last.then_inc(s["spread_in_psum"], 1)
            pe.wait_ge(s["scores_copied"], 3)
            for c in range(CHUNKS + 2):
                if c < CHUNKS:
                    if c >= 4:
                        pe.wait_ge(s["weights"], c - 3)
                    pe.matmul(m.ps[:, 4 + c % 4, :], m.sel[:, c * 128:(c + 1) * 128], scT, start=True, stop=True).then_inc(s["sum"], 1)
                if c >= 2:
                    k = c - 2
                    pe.wait_ge(s["weights"], k + 1)
                    pe.matmul(m.ps[:, 2, :], m.table[:, k * 128:(k + 1) * 128], m.wts[:, k % 3, :], start=k == 0,
                              stop=k == CHUNKS - 1).then_inc(s["table_product"], 1)
            pe.wait_ge(s["kv"], 1)
            for b in range(GS):
                at = slice(b * T, (b + 1) * T)
                pe.transpose(m.ps[:, 0, at], kvT[:, at], m.w["ident"])
                last = pe.matmul(m.ps[:, 1, at], aT[:, at], kvT[0:F, at], start=True, stop=True)
            last.then_inc(s["attn_scores"], 1)
            for b in range(GS):
                at = slice(b * T, (b + 1) * T)
                pe.wait_ge(s["attn_exp"], b + 1)
                last = pe.transpose(m.ps[:, 3, at], probs[:, at], m.w["ident"])
            last.then_inc(s["probs_turned"], 1)
            pe.wait_ge(s["probs_copied"], 1)
            pe.wait_ge(s["values"], 1)
            for b in range(GS):
                at = slice(b * T, (b + 1) * T)
                last = pe.matmul(m.ps[0:F, 4, at], m.vals[:, b, :], probsT[:, at], start=True, stop=True)
            last.then_inc(s["mixed"], 1)
            pe.wait_ge(s["mixed_copied"], 1)
            for b in range(GS):
                last = pe.matmul(m.ps[:, 5, b * F:(b + 1) * F], mixT[:, b * T:(b + 1) * T], wo, start=True, stop=True)
            last.then_inc(s["out"], 1)

        @block.scalar
        def _(a):
            a.copy(x, m.nT_all[:, bass.ts(g, TOK)]).then_inc(s["input"], 1)
            a.wait_ge(s["query_in_psum"], 1)
            a.copy(qT, m.ps[0:F, 0, :]).then_inc(s["query"], 1)
            a.copy(aT, m.ps[0:F, 1, :]).then_inc(s["query"], 1)
            a.wait_ge(s["scores_in_psum"], 1)
            a.copy(sc, m.ps[:, 2, :]).then_inc(s["scores"], 1)
            a.wait_ge(s["threshold"], 1)
            a.activation(m.e16[:], m.d16[:], ACT.Exp).then_inc(s["exp16"], 1)
            a.wait_ge(s["scores_turned"], 1)
            a.copy(scT, m.ps[:, 3, :]).then_inc(s["scores_copied"], 1)
            for c in range(CHUNKS):
                a.wait_ge(s["sum"], c + 1)
                if c >= 3:
                    a.wait_ge(s["weights"], c - 2)
                a.activation(m.exps[:, c % 3, :], m.ps[:, 4 + c % 4, :], ACT.Exp).then_inc(s["exp"], 1)
            a.wait_ge(s["attn_max"], 1)
            for b in range(GS):
                at = slice(b * T, (b + 1) * T)
                a.activation(probs[:, at], m.msk[:, at], ACT.Exp, bias=m.amax[:, b:b + 1], scale=scale,
                             accum_out=m.asum[:, b:b + 1]).then_inc(s["attn_exp"], 1)
            a.wait_ge(s["probs_turned"], 1)
            a.copy(probsT, m.ps[:, 3, :]).then_inc(s["probs_copied"], 1)
            a.wait_ge(s["mixed"], 1)
            a.copy(mixT, m.ps[0:F, 4, :]).then_inc(s["mixed_copied"], 1)

        @block.vector
        def _(v):
            link = chain_of(v, own)
            v.wait_ge(s["scores"], 1)
            for i in range(2 * GS):
                last = v.max(top[:, i, 0:8], scb[:, i // 2, i % 2, :])
            link(last)
            for i in range(2 * GS):
                last = v.match_replace(out=m.rest[:, i, :], in_to_replace=top[:, i, 0:8], in_values=scb[:, i // 2, i % 2, :],
                                       imm_value=LOWEST)
            link(last)
            for i in range(2 * GS):
                last = v.max(top[:, i, 8:16], m.rest[:, i, :])
            link(last)
            at = 0
            for a0, na, nb in stairs():
                for b in range(GS):
                    last = v.tensor_tensor(cand[:, b, at:at + na * nb].rearrange("p (x y) -> p x y", x=na),
                                           spread(top[:, 2 * b, a0:a0 + na], 2, nb),
                                           spread(top[:, 2 * b + 1, 0:nb], 1, na), ALU.add)
                at += na * nb
            link(last)
            for b in range(GS):
                last = v.max(v16[:, b, 0:8], cand[:, b, :])
            link(last)
            for b in range(GS):
                last = v.match_replace(out=m.cand2[:, b, :], in_to_replace=v16[:, b, 0:8], in_values=cand[:, b, :],
                                       imm_value=LOWEST)
            link(last)
            for b in range(GS):
                last = v.max(v16[:, b, 8:16], m.cand2[:, b, :])
            link(last)
            v.tensor_tensor(m.d16[:], v16[:], v16[:, :, 0:1].to_broadcast([128, GS, TOPK]), ALU.subtract).then_inc(s["threshold"], 1)
            v.wait_ge(s["threshold"], 1)
            link(v.tensor_tensor(scb[:, :, 1, :], scb[:, :, 1, :], v16[:, :, 0:1].to_broadcast([128, GS, KEYS]), ALU.subtract))
            link(v.scalar_tensor_tensor(m.mag[:], top[:, :, 0], -1.0, top[:, :, 0], ALU.mult, ALU.max))
            link(v.tensor_reduce(m.mag2[:], m.mag[:].rearrange("p (b s) -> p b s", s=2), AX.X, ALU.add))
            link(v.scalar_tensor_tensor(m.limit[:, 0, :], m.mag2[:], -2.0 ** -20, m.d16[:, :, TOPK - 1], ALU.mult, ALU.add))
            v.wait_ge(s["exp16"], 1)
            link(v.tensor_reduce(m.mag2[:], m.e16[:], AX.X, ALU.add))
            v.reciprocal(m.limit[:, 1, :], m.mag2[:]).then_inc(s["limits"], 1)
            v.wait_ge(s["spread_in_psum"], 1)
            v.tensor_copy(floor, m.ps[:, 0, :]).then_inc(s["scores_copied"], 1)
            v.tensor_copy(rinv, m.ps[:, 1, :]).then_inc(s["scores_copied"], 1)
            v.wait_ge(s["scores_copied"], 3)
            for c in range(CHUNKS):
                v.wait_ge(s["exp"], c + 1)
                if c >= 3:
                    v.wait_ge(s["table_product"], c - 2)
                link(v.tensor_tensor(m.wts[:, c % 3, :], m.ps[:, 4 + c % 4, :], floor, ALU.is_ge))
                v.tensor_tensor(m.wts[:, c % 3, :], m.wts[:, c % 3, :], m.exps[:, c % 3, :], ALU.mult).then_inc(s["weights"], 1)
            v.wait_ge(s["table_product"], CHUNKS)
            v.tensor_tensor(kvT, m.ps[:, 2, :], rinv, ALU.mult).then_inc(s["kv"], 1)
            v.wait_ge(s["attn_scores"], 1)
            v.tensor_copy(m.vals[:], m.ps[:, 0, :].rearrange("p (b c) -> p b c", b=GS)[:, :, F:2 * F]).then_inc(s["values"], 1)
            link(v.tensor_tensor(m.msk[:].rearrange("p (b t) -> p b t", b=GS), m.ps[:, 1, :].rearrange("p (b t) -> p b t", b=GS),
                                 spread(m.w["causal"], 1, GS), ALU.add))
            link(v.tensor_reduce(m.amax[:], m.msk[:].rearrange("p (b t) -> p b t", b=GS), AX.X, ALU.max))
            v.tensor_scalar(m.amax[:], m.amax[:], -scale, None, ALU.mult).then_inc(s["attn_max"], 1)
            v.wait_ge(s["attn_exp"], GS)
            link(v.reciprocal(m.arec[:], m.asum[:]))
            v.wait_ge(s["out"], 1)
            link(v.tensor_tensor(m.outw[:], m.ps[:, 5, 0:GS * F].rearrange("p (b f) -> p b f", b=GS),
                                 spread(m.arec[:], 2, F), ALU.mult))
            state = m.h_all[:, bass.ts(g, GS * F)]
            link(v.tensor_tensor(state, state, m.outw[:].rearrange("p b f -> p (b f)"), ALU.add))


def audio_tower(nc, win, pack, tree_w2, head, table, sel, out, layers=LAYERS, last=True, groups=GROUPS, heads=HEADS):
    with ExitStack() as ctx:
        m = Memory()
        sems = {}

        def sem(name):
            if name not in sems:
                sems[name] = ctx.enter_context(nc.semaphore(name))
            return sems[name]

        def sb(where, name, shape):
            return where.enter_context(nc.sbuf_tensor(name, shape, F32))

        def used():
            nums = [x.num for x in sems.values()]
            assert max(nums) - min(nums) + 1 == len(nums)
            return range(min(nums), max(nums) + 1)

        m.sem = sem
        m.dram = {"win": win, "table": table, "head": head}
        m.ps = ctx.enter_context(nc.psum_tensor("ps", [128, BANKS, 512], F32))
        m.h_all = sb(ctx, "h_all", [128, SEQS * F])
        m.nT_all = sb(ctx, "nT_all", [F, SEQS * T])
        m.big = sb(ctx, "big", [128, 8, TOK])
        cols = pack_columns()
        m.packed = sb(ctx, "packed", [128, sum(c for _, c in cols.values())])
        m.w, at = {}, 0
        for name, (nr, n) in cols.items():
            m.w[name] = m.packed[0:nr, at:at + n]
            at += n

        with ExitStack() as phase:
            m.h = sb(phase, "h", [128, GS, F])
            m.n = sb(phase, "n", [128, GS, F])
            m.n2 = sb(phase, "n2", [128, GS, F])
            m.nT = sb(phase, "nT", [FB, TOK])
            m.mT = sb(phase, "mT", [FB, TOK])
            m.stats = sb(phase, "stats", [128, GS, 6])
            m.moments = sb(phase, "moments", [128, GS, 2])
            m.var = sb(phase, "var", [128, GS])
            m.std = sb(phase, "std", [128, GS])
            m.rstd = sb(phase, "rstd", [128, GS])
            m.small = sb(phase, "small", [128, 64])
            m.window = sb(phase, "window", [128, GS, TAPS * F])
            m.gate = sb(phase, "gate", [128, 4, GS, EXPERTS])
            m.wide = sb(phase, "wide", [128, 2, 512])
            m.ones = sb(phase, "ones", [1, 128])
            m.values = sb(phase, "values", [128, GS, H2 * D2])
            m.l2max = sb(phase, "l2max", [128, 2, 16])
            m.l2sum = sb(phase, "l2sum", [128, 2, 16])
            m.tree = sb(phase, "tree", [128, 3, GS, NODES + 1])
            m.tree_w2 = sb(phase, "tree_w2", [FB, NODES * F])
            m.omega = sb(phase, "omega", [128, 2, 512])
            m.evals = sb(phase, "evals", [128, 2, 512])
            shared = phase.enter_context(nc.sbuf_tensor("shared", [128, 7 * 2 * PER * F], F32))
            m.probs = shared[:, 0:4096].rearrange("p (q r b s t) -> p q r b s t", q=2, r=4, b=2, s=2)
            m.weighted = shared[:, 0:3072].rearrange("p (k n f) -> p k n f", k=3, f=F)
            m.summed = shared[:, 3072:7168].rearrange("p (b n f) -> p b n f", b=GS, f=F)

            loaded = sem("weights_loaded")
            with nc.Block() as block:
                @block.sync
                def _(sp):
                    sp.dma_start(m.packed[:], pack).then_inc(loaded, 16)
                    sp.dma_start(m.tree_w2[:], tree_w2).then_inc(loaded, 16)
                    sp.wait_ge(loaded, 32)

                @block.vector
                def _(v):
                    v.memset(m.nT[F:FB, :], 1.0)
                    v.memset(m.mT[F:FB, :], 1.0)
                    v.memset(m.ones[:], 1.0)

            with nc.Fori(0, groups) as g:
                for layer in layers:
                    layer(nc, m, g)
                layer3_input(nc, m, g)
                nc.all_engine_barrier(sems_to_clear=used())

        if last:
            with ExitStack() as phase:
                m.table = sb(phase, "table", [128, CHUNKS * 2 * F])
                m.head = sb(phase, "head", [F, 320])
                m.sel = sb(phase, "sel", [128, CHUNKS * 128])
                m.top = sb(phase, "top", [128, 2 * GS, TOPK])
                m.rest = sb(phase, "rest", [128, 2 * GS, KEYS])
                m.cand = sb(phase, "cand", [128, GS, 54])
                m.cand2 = sb(phase, "cand2", [128, GS, 54])
                m.v16 = sb(phase, "v16", [128, GS, TOPK])
                m.d16 = sb(phase, "d16", [128, GS, TOPK])
                m.e16 = sb(phase, "e16", [128, GS, TOPK])
                m.mag = sb(phase, "mag", [128, 2 * GS])
                m.mag2 = sb(phase, "mag2", [128, GS])
                m.limit = sb(phase, "limit", [128, 2, GS])
                m.floor = sb(phase, "floor", [128, 2, TOK])
                m.exps = sb(phase, "exps", [128, 3, TOK])
                m.wts = sb(phase, "wts", [128, 3, TOK])
                m.vals = sb(phase, "vals", [128, GS, F])
                m.msk = sb(phase, "msk", [128, TOK])
                m.amax = sb(phase, "amax", [128, GS])
                m.asum = sb(phase, "asum", [128, GS])
                m.arec = sb(phase, "arec", [128, GS])
                m.outw = sb(phase, "outw", [128, GS, F])
                loaded = sem("selectors_loaded")
                with nc.Block() as block:
                    @block.sync
                    def _(sp):
                        sp.dma_start(m.sel[:], sel).then_inc(loaded, 16)
                        sp.wait_ge(loaded, 16)
                with nc.Fori(0, heads) as h:
                    load_head(nc, m, h)
                    with nc.Fori(0, groups) as g:
                        memory_and_attention(nc, m, g)
                        nc.all_engine_barrier(sems_to_clear=used())

        stored = sem("stored")
        with nc.Block() as block:
            @block.sync
            def _(sp):
                n = groups * GS
                sp.dma_start(out[0:n].rearrange("b t f -> t b f"), m.h_all[:, 0:n * F].rearrange("t (b f) -> t b f", f=F)).then_inc(stored, 16)
                sp.wait_ge(stored, 16)


def kernel(**inputs):
    import concourse.bacc as bacc
    from concourse.bass_utils import run_bass_kernel_spmd

    arrays = lay_out({k: np.asarray(v) for k, v in inputs.items()})
    nc = bacc.Bacc("TRN2", target_bir_lowering=False, num_devices=1)
    args = {k: nc.dram_tensor(k + "_dram", a.shape, F32, kind="ExternalInput").ap() for k, a in arrays.items()}
    out = nc.dram_tensor("out_dram", (SEQS, T, F), F32, kind="ExternalOutput").ap()
    audio_tower(nc, **args, out=out)
    r = run_bass_kernel_spmd(nc, [{k + "_dram": a for k, a in arrays.items()}], core_ids=[0])
    return r.results[0]["out_dram"]
```

```python
from contextlib import ExitStack

import numpy as np

import concourse.bass as bass
from concourse import mybir

ALU = mybir.AluOpType
ACT = mybir.ActivationFunctionType
AX = mybir.AxisListType
F32 = mybir.dt.float32
F16 = mybir.dt.float16

SEQS, T_IN, F = 32, 256, 64
T = T_IN // 2
TAPS = 5
GS = 4
GROUPS = SEQS // GS
TOK = GS * T
FB = F + 1
EXPERTS = 8
H2, D2 = 8, 32
NODES = 255
TREE_DEPTH = 7
PER = 8
HEADS = 8
KEYS = 64
TOPK = 16
CHUNKS = KEYS * KEYS // 128
DK = 32
BANKS = 8
LOWEST = -3.0e38
PIECE = 8
SHIFT = 40.0
EXP_ZERO = -87.3
SCORE_MIN = -30000.0
LN_EPS = 1e-5
TOK_EPS = 1e-3


def pack_columns():
    return {
        "ident": (128, 128), "mean128": (128, 128), "off_diag": (128, 128), "upper": (128, 128),
        "causal": (128, 128),
        "tok_w": (128, TAPS * F), "tok_b": (128, F), "tok_gamma": (128, F), "tok_beta": (128, F),
        "tok_alpha": (128, F),
        "wa": (F, F), "wb": (F, F), "wu": (FB, F), "wr": (F, F),
        "m0_router": (FB, EXPERTS), "m0_w1": (FB, EXPERTS * F), "m0_w2": (128, EXPERTS * F),
        "m0_b2": (1, EXPERTS * F),
        "a1_w": (F, F),
        "m1_gamma": (128, F), "m1_beta": (128, F),
        "m1_router": (FB, EXPERTS), "m1_w1": (FB, EXPERTS * 128), "m1_w2": (128, EXPERTS * F),
        "m1_b2": (1, EXPERTS * F),
        "a2_gamma": (128, F), "a2_beta": (128, F),
        "a2_wq": (F, H2 * D2), "a2_wk": (F, H2 * D2), "a2_wv": (F, H2 * D2),
        "a2_wg": (FB, H2 * D2), "a2_wf": (128, 2 * F), "a2_bf": (128, F),
        "tree_w1": (FB, NODES + 1),
        "a3_q": (F, HEADS * F), "a3_e": (F, HEADS * F),
    }


def lay_out(inp):
    f = np.float32
    rows = lambda v: np.broadcast_to(np.asarray(v).reshape(1, -1), (128, np.asarray(v).size))
    below = lambda w, b: np.concatenate([w, np.asarray(b).reshape(1, -1)], 0)
    zero = lambda n: np.zeros((1, n), f)
    r = np.arange(128)
    d = {"ident": np.eye(128, dtype=f), "mean128": np.full((128, 128), 1 / 128, f),
         "off_diag": (1 - np.eye(128, dtype=f)) / f(T),
         "upper": (r[:, None] <= r[None, :]).astype(f),
         "causal": np.where(r[:, None] >= r[None, :], f(0), f(LOWEST)).astype(f)}
    d["tok_w"] = rows(inp["L0_tok_w"][:, 0, :])
    for k in ("b", "gamma", "beta", "alpha"):
        d["tok_" + k] = rows(inp["L0_tok_" + k])
    d["wa"], d["wb"], d["wr"] = inp["L0_attn_W_alpha"].T, inp["L0_attn_W_beta"].T, inp["L0_attn_W_r"].T
    d["wu"] = below(inp["L0_attn_W_unary"].T, inp["L0_attn_b_unary"])
    d["m0_router"] = np.concatenate([inp["L0_ffn_router_w"].T, zero(EXPERTS)], 0)
    d["m0_w1"] = below(inp["L0_ffn_w1"].transpose(1, 0, 2).reshape(F, -1), inp["L0_ffn_b1"])
    w2 = np.zeros((2, F, EXPERTS // 2, 2, F), f)
    for e in range(EXPERTS):
        w2[e % 2, :, e // 2, e % 2, :] = inp["L0_ffn_w2"][e]
    d["m0_w2"] = w2.reshape(128, EXPERTS * F)
    d["m0_b2"] = inp["L0_ffn_b2"].reshape(1, -1)
    d["a1_w"] = inp["L1_attn_W"]
    d["m1_gamma"], d["m1_beta"] = rows(inp["L1_ffn_gamma"]), rows(inp["L1_ffn_beta"])
    d["m1_router"] = below(inp["L1_ffn_Wr"], inp["L1_ffn_br"])
    d["m1_w1"] = below(inp["L1_ffn_W1"].transpose(1, 0, 2).reshape(F, -1), inp["L1_ffn_b1"])
    d["m1_w2"] = inp["L1_ffn_W2"].transpose(1, 0, 2).reshape(128, -1)
    d["m1_b2"] = inp["L1_ffn_b2"].reshape(1, -1)
    d["a2_gamma"], d["a2_beta"] = rows(inp["L2_attn_ln_gamma"]), rows(inp["L2_attn_ln_beta"])
    w = inp["L2_attn_W_qkv"].T
    d["a2_wq"], d["a2_wk"], d["a2_wv"] = w[:, :256], w[:, 256:512], w[:, 512:]
    d["a2_wg"] = below(inp["L2_attn_W_gate"].T, inp["L2_attn_b_gate"])
    d["a2_wf"] = inp["L2_attn_W_final"].T.reshape(2, 128, F).transpose(1, 0, 2).reshape(128, -1)
    d["a2_bf"] = rows(inp["L2_attn_b_final"])
    d["tree_w1"] = np.concatenate([below(inp["L2_ffn_w1s"].T, inp["L2_ffn_b1s"]), np.zeros((FB, 1), f)], 1)
    d["a3_q"] = inp["L3_attn_Q"].transpose(1, 0, 2).reshape(F, -1)
    d["a3_e"] = inp["L3_attn_E"].transpose(2, 0, 1).reshape(F, -1)
    cols = pack_columns()
    pack = np.zeros((128, sum(c for _, c in cols.values())), f)
    at = 0
    for name, (nr, nc_) in cols.items():
        assert d[name].shape == (nr, nc_), (name, d[name].shape)
        pack[:nr, at:at + nc_] = d[name]
        at += nc_

    x = np.concatenate([np.zeros((SEQS, 1, F), f), inp["x"], np.zeros((SEQS, 2, F), f)], 1)
    win = np.stack([x[:, k:k + 2 * T:2, :] for k in range(TAPS)], 2)
    win = win.reshape(GROUPS, GS, T, TAPS * F).transpose(0, 2, 1, 3)
    tree_w2 = np.concatenate([inp["L2_ffn_w2s"].transpose(1, 0, 2).reshape(F, -1),
                              inp["L2_ffn_b2s"].reshape(1, -1)], 0)
    head = np.zeros((HEADS + 1, F, 320), f)
    wq_pk = inp["L3_ffn_Wq_pk"].reshape(F, 2, HEADS, DK)
    for h in range(HEADS):
        head[h, :, 0:64] = wq_pk[:, :, h, :].reshape(F, 64)
        for p in range(2):
            head[h, p * DK:(p + 1) * DK, 64 + p * KEYS:64 + (p + 1) * KEYS] = inp["L3_ffn_pk_keys"][p, :, h, :].T
        head[h, :, 192:256] = inp["L3_ffn_Wq"][:, h * F:(h + 1) * F]
        head[h, :, 256:320] = inp["L3_ffn_Wo"][h * F:(h + 1) * F, :]
    table = np.concatenate([inp["L3_ffn_keys_table"], inp["L3_ffn_values_table"]], 1)
    table = table.reshape(HEADS, CHUNKS, 128, 2 * F).transpose(0, 2, 1, 3).reshape(HEADS, 128, CHUNKS * 2 * F)
    sel = np.zeros((2, KEYS, CHUNKS, 2, KEYS), f)
    for c in range(CHUNKS):
        for j in range(2):
            sel[0, :, c, j, :] = np.eye(KEYS)
            sel[1, 2 * c + j, c, j, :] = 1
    sel = sel.reshape(128, CHUNKS * 128).astype(np.float16)
    arrays = {"pack": pack, "win": win.reshape(GROUPS, T, GS * TAPS * F), "tree_w2": tree_w2, "head": head,
              "table": table, "sel": sel}
    return {k: np.ascontiguousarray(v) for k, v in arrays.items()}


class Memory:
    pass


def spread(ap, axis, n):
    ap = ap.unsqueeze(axis)
    shape = list(ap.shape)
    shape[axis] = n
    return ap.to_broadcast(shape)


def chain_of(eng, sem):
    count = [0]

    def link(ins):
        count[0] += 1
        ins.then_inc(sem, 1)
        eng.wait_ge(sem, count[0])
    return link


class Norm:

    def __init__(self, m, name, src, dst, turned, bank=0, eps=LN_EPS):
        self.m, self.src, self.dst, self.turned, self.bank, self.eps = m, src, dst, turned, bank, eps
        self.var, self.std = m.sem(f"{name}_var"), m.sem(f"{name}_std")
        if turned is not None:
            self.normed, self.inps, self.ready = (m.sem(f"{name}_{x}") for x in ("normed", "turned_in_psum", "turned"))

    def dve_normalize(self, v, link):
        m = self.m
        for b in range(GS):
            last = v.bn_stats(m.stats[:, b, :], self.src[:, b, :])
        link(last)
        for b in range(GS):
            last = v.bn_aggr(m.moments[:, b, :], m.stats[:, b, :])
        link(last)
        v.tensor_scalar(m.var[:], m.moments[:, :, 1], self.eps, None, ALU.add).then_inc(self.var, 1)
        v.wait_ge(self.std, 1)
        link(v.reciprocal(m.rstd[:], m.std[:]))
        for b in range(GS):
            last = v.tensor_scalar(self.dst[:, b, :], self.src[:, b, :], m.moments[:, b, 0:1],
                                   m.rstd[:, b:b + 1], ALU.subtract, ALU.mult)
        return last

    def act_root(self, a):
        a.wait_ge(self.var, 1)
        a.activation(self.m.std[:], self.m.var[:], ACT.Sqrt).then_inc(self.std, 1)

    def pe_turn(self, pe):
        pe.wait_ge(self.normed, 1)
        for b in range(GS):
            last = pe.transpose(self.m.ps[0:F, self.bank, b * T:(b + 1) * T], self.dst[:, b, :], self.m.w["ident"])
        last.then_inc(self.inps, 1)

    def act_copy(self, a):
        a.wait_ge(self.inps, 1)
        a.copy(self.turned[0:F, :], self.m.ps[0:F, self.bank, :]).then_inc(self.ready, 1)


def layer0_tokens(nc, m, g):
    loaded, parts, sums, var, std, own = (m.sem("tok_" + x) for x in (
        "window_loaded", "partial_moments", "moments_in_psum", "var", "std", "dve"))
    with nc.Block() as block:
        @block.sync
        def _(sp):
            sp.dma_start(m.window[:].rearrange("p b k -> p (b k)"), m.dram["win"][g]).then_inc(loaded, 16)

        @block.vector
        def _(v):
            link = chain_of(v, own)
            v.wait_ge(loaded, 16)
            link(v.tensor_tensor(m.window[:], m.window[:], spread(m.w["tok_w"], 1, GS), ALU.mult))
            link(v.tensor_reduce(m.n[:], m.window[:].rearrange("p b (k f) -> p b f k", k=TAPS), AX.X, ALU.add))
            link(v.tensor_tensor(m.n[:], m.n[:], spread(m.w["tok_b"], 1, GS), ALU.add))
            for b in range(GS):
                last = v.bn_stats(m.stats[:, b, :], m.n[:, b, :])
            link(last)
            for b in range(GS):
                last = v.bn_aggr(m.moments[:, b, :], m.stats[:, b, :])
            link(last)
            link(v.tensor_copy(m.small[:, 0:GS], m.moments[:, :, 0]))
            link(v.tensor_tensor(m.small[:, GS:2 * GS], m.small[:, 0:GS], m.small[:, 0:GS], ALU.mult))
            v.tensor_tensor(m.small[:, GS:2 * GS], m.small[:, GS:2 * GS], m.moments[:, :, 1], ALU.add).then_inc(parts, 1)
            v.wait_ge(sums, 1)
            link(v.tensor_copy(m.small[:, 0:2 * GS], m.ps[:, 0, 0:2 * GS]))
            link(v.tensor_tensor(m.small[:, 2 * GS:3 * GS], m.small[:, 0:GS], m.small[:, 0:GS], ALU.mult))
            link(v.tensor_tensor(m.var[:], m.small[:, GS:2 * GS], m.small[:, 2 * GS:3 * GS], ALU.subtract))
            v.tensor_scalar(m.var[:], m.var[:], TOK_EPS, None, ALU.add).then_inc(var, 1)
            v.wait_ge(std, 1)
            link(v.reciprocal(m.rstd[:], m.std[:]))
            for b in range(GS):
                last = v.tensor_scalar(m.n[:, b, :], m.n[:, b, :], m.small[:, b:b + 1], m.rstd[:, b:b + 1],
                                       ALU.subtract, ALU.mult)
            link(last)
            link(v.tensor_tensor(m.n[:], m.n[:], spread(m.w["tok_gamma"], 1, GS), ALU.mult))
            link(v.tensor_tensor(m.n[:], m.n[:], spread(m.w["tok_beta"], 1, GS), ALU.add))
            link(v.scalar_tensor_tensor(m.n2[:], m.n[:], 0.0, spread(m.w["tok_alpha"], 1, GS), ALU.min, ALU.mult))
            link(v.scalar_tensor_tensor(m.h[:], m.n[:], 0.0, m.n2[:], ALU.max, ALU.add))

        @block.tensor
        def _(pe):
            pe.wait_ge(parts, 1)
            pe.matmul(m.ps[:, 0, 0:2 * GS], m.w["mean128"], m.small[:, 0:2 * GS], start=True, stop=True).then_inc(sums, 1)

        @block.scalar
        def _(a):
            a.wait_ge(var, 1)
            a.activation(m.std[:], m.var[:], ACT.Sqrt).then_inc(std, 1)


def layer0_attention(nc, m, g):
    norm = Norm(m, "l0a", m.h, m.n, m.nT)
    proj, copied, scored, masked, mixed, mixed_sb, out, own = (m.sem("l0a_" + x) for x in (
        "projected", "projections_copied", "scores", "scores_masked", "mixed", "mixed_copied", "out", "dve"))
    aT, bT = m.big[0:F, 0, :], m.big[0:F, 1, :]
    un, sT, mixT = m.big[:, 2, 0:GS * F], m.big[:, 3, :], m.big[0:F, 4, :]
    with nc.Block() as block:
        @block.tensor
        def _(pe):
            norm.pe_turn(pe)
            pe.wait_ge(norm.ready, 1)
            pe.matmul(m.ps[0:F, 1, :], m.w["wa"], m.nT[0:F, :], start=True, stop=True)
            pe.matmul(m.ps[0:F, 2, :], m.w["wb"], m.nT[0:F, :], start=True, stop=True)
            for b in range(GS):
                last = pe.matmul(m.ps[:, 3, b * F:(b + 1) * F], m.nT[:, b * T:(b + 1) * T], m.w["wu"], start=True, stop=True)
            last.then_inc(proj, 1)
            pe.wait_ge(copied, 3)
            for b in range(GS):
                at = slice(b * T, (b + 1) * T)
                last = pe.matmul(m.ps[:, 4, at], bT[:, at], aT[:, at], start=True, stop=True)
            last.then_inc(scored, 1)
            pe.wait_ge(masked, 1)
            for b in range(GS):
                at = slice(b * T, (b + 1) * T)
                last = pe.matmul(m.ps[0:F, 5, at], un[:, b * F:(b + 1) * F], sT[:, at], start=True, stop=True)
            last.then_inc(mixed, 1)
            pe.wait_ge(mixed_sb, 1)
            for b in range(GS):
                last = pe.matmul(m.ps[:, 6, b * F:(b + 1) * F], mixT[:, b * T:(b + 1) * T], m.w["wr"], start=True, stop=True)
            last.then_inc(out, 1)

        @block.scalar
        def _(a):
            norm.act_root(a)
            norm.act_copy(a)
            a.wait_ge(proj, 1)
            a.copy(aT, m.ps[0:F, 1, :]).then_inc(copied, 1)
            a.copy(bT, m.ps[0:F, 2, :]).then_inc(copied, 1)
            a.wait_ge(mixed, 1)
            a.copy(mixT, m.ps[0:F, 5, :]).then_inc(mixed_sb, 1)

        @block.vector
        def _(v):
            link = chain_of(v, own)
            norm.dve_normalize(v, link).then_inc(norm.normed, 1)
            v.wait_ge(proj, 1)
            v.tensor_copy(un, m.ps[:, 3, 0:GS * F]).then_inc(copied, 1)
            v.wait_ge(scored, 1)
            v.tensor_tensor(sT.rearrange("p (b t) -> p b t", b=GS), m.ps[:, 4, :].rearrange("p (b t) -> p b t", b=GS),
                            spread(m.w["off_diag"], 1, GS), ALU.mult).then_inc(masked, 1)
            v.wait_ge(norm.normed, 1)
            link(v.tensor_tensor(m.h[:], m.h[:], m.n[:], ALU.add))
            v.wait_ge(out, 1)
            link(v.tensor_tensor(m.h[:], m.h[:], m.ps[:, 6, 0:GS * F].rearrange("p (b f) -> p b f", b=GS), ALU.add))


def mixture(nc, m, which):
    name = f"l{which}m"
    units = (4, 8)[which]
    norm = Norm(m, name, m.h, m.n, m.nT, bank=0)
    if which:
        norm.src, norm.dst = m.n, m.n2
        first = Norm(m, name + "_first", m.h, m.n, None)
    logits, shifted, exped, hidden, acted, out, folded, own = (m.sem(f"{name}_{x}") for x in (
        "logits", "logits_shifted", "exp", "hidden", "gelu", "expert_outputs", "outputs_folded", "dve"))
    w1, w2, b2 = (m.w[f"m{which}_{x}"] for x in ("w1", "w2", "b2"))
    lg, mx, wt, tmp = (m.gate[:, i] for i in range(4))
    act = m.big
    with nc.Block() as block:
        @block.tensor
        def _(pe):
            norm.pe_turn(pe)
            pe.wait_ge(norm.ready, 1)
            for b in range(GS):
                last = pe.matmul(m.ps[:, 1, b * EXPERTS:(b + 1) * EXPERTS], m.nT[:, b * T:(b + 1) * T],
                                 m.w[f"m{which}_router"], start=True, stop=True)
            last.then_inc(logits, 1)
            for u in range(units):
                if u >= 2:
                    pe.wait_ge(acted, u - 1)
                pe.matmul(m.ps[:, 2 + u % 2, :], w1[:, u * 128:(u + 1) * 128], m.nT[:], start=True, stop=True).then_inc(hidden, 1)
            pe.wait_ge(acted, units)
            wide = EXPERTS * F // units
            for b in range(GS):
                pe.matmul(m.ps[:, 4 + b, :], m.ones[0:1, :], b2, start=True, stop=False)
                for u in range(units):
                    last = pe.matmul(m.ps[:, 4 + b, u * wide:(u + 1) * wide], act[:, u, b * T:(b + 1) * T],
                                     w2[:, u * wide:(u + 1) * wide], start=False, stop=u == units - 1)
                last.then_inc(out, 1)

        @block.scalar
        def _(a):
            if which:
                first.act_root(a)
            norm.act_root(a)
            norm.act_copy(a)
            a.wait_ge(shifted, 1)
            a.activation(tmp, tmp, ACT.Exp).then_inc(exped, 1)
            for u in range(units):
                a.wait_ge(hidden, u + 1)
                a.activation(act[:, u, :], m.ps[:, 2 + u % 2, :], ACT.Gelu).then_inc(acted, 1)

        @block.vector
        def _(v):
            link = chain_of(v, own)
            if which:
                link(first.dve_normalize(v, link))
                link(norm.dve_normalize(v, link))
                link(v.tensor_tensor(m.n2[:], m.n2[:], spread(m.w["m1_gamma"], 1, GS), ALU.mult))
                v.tensor_tensor(m.n2[:], m.n2[:], spread(m.w["m1_beta"], 1, GS), ALU.add).then_inc(norm.normed, 1)
            else:
                norm.dve_normalize(v, link).then_inc(norm.normed, 1)
                v.wait_ge(norm.normed, 1)
                link(v.tensor_tensor(m.h[:], m.h[:], m.n[:], ALU.add))
            v.wait_ge(logits, 1)
            link(v.tensor_copy(lg, m.ps[:, 1, 0:GS * EXPERTS].rearrange("p (b e) -> p b e", b=GS)))
            for b in range(GS):
                last = v.max(mx[:, b, :], lg[:, b, :])
            link(last)
            v.tensor_tensor(tmp, lg, mx[:, :, 0:1].to_broadcast([128, GS, EXPERTS]), ALU.subtract).then_inc(shifted, 1)
            link(v.tensor_tensor(wt, lg, mx[:, :, 1:2].to_broadcast([128, GS, EXPERTS]), ALU.is_ge))
            v.wait_ge(exped, 1)
            link(v.tensor_tensor(wt, wt, tmp, ALU.mult))
            link(v.tensor_reduce(m.small[:, 0:GS], wt, AX.X, ALU.add))
            link(v.reciprocal(m.small[:, 0:GS], m.small[:, 0:GS]))
            link(v.tensor_tensor(wt, wt, spread(m.small[:, 0:GS], 2, EXPERTS), ALU.mult))
            for b in range(GS):
                v.wait_ge(out, b + 1)
                link(v.tensor_tensor(m.wide[:, b % 2, :].rearrange("p (e f) -> p e f", e=EXPERTS),
                                     m.ps[:, 4 + b, :].rearrange("p (e f) -> p e f", e=EXPERTS),
                                     spread(wt[:, b, :], 2, F), ALU.mult))
                link(v.tensor_reduce(m.n2[:, b, :], m.wide[:, b % 2, :].rearrange("p (e f) -> p f e", e=EXPERTS),
                                     AX.X, ALU.add))
            link(v.tensor_tensor(m.h[:], m.h[:], m.n2[:], ALU.add))


def layer0_mixture(nc, m, g):
    mixture(nc, m, 0)


def layer1_mixture(nc, m, g):
    mixture(nc, m, 1)


def layer1_attention(nc, m, g):
    norm = Norm(m, "l1a", m.h, m.n, m.nT)
    proj, copied, scored, maxed, exped, turned, turned_sb, out, own = (m.sem("l1a_" + x) for x in (
        "projected", "projection_copied", "scores", "max", "exp", "probs_turned", "probs_copied", "out", "dve"))
    xT, p, pT = m.big[0:F, 0, :], m.big[:, 1, :], m.big[:, 2, :]
    mx, total = m.small[:, 0:GS], m.small[:, GS:2 * GS]
    scale = F ** -0.5
    with nc.Block() as block:
        @block.tensor
        def _(pe):
            norm.pe_turn(pe)
            pe.wait_ge(norm.ready, 1)
            pe.matmul(m.ps[0:F, 1, :], m.w["a1_w"], m.nT[0:F, :], start=True, stop=True).then_inc(proj, 1)
            pe.wait_ge(copied, 1)
            for b in range(GS):
                at = slice(b * T, (b + 1) * T)
                last = pe.matmul(m.ps[:, 2, at], xT[:, at], m.nT[0:F, at], start=True, stop=True)
            last.then_inc(scored, 1)
            for b in range(GS):
                at = slice(b * T, (b + 1) * T)
                pe.wait_ge(exped, b + 1)
                last = pe.transpose(m.ps[:, 3, at], p[:, at], m.w["ident"])
            last.then_inc(turned, 1)
            pe.wait_ge(turned_sb, 1)
            for b in range(GS):
                last = pe.matmul(m.ps[:, 4, b * F:(b + 1) * F], pT[:, b * T:(b + 1) * T], m.n[:, b, :], start=True, stop=True)
            last.then_inc(out, 1)

        @block.scalar
        def _(a):
            norm.act_root(a)
            norm.act_copy(a)
            a.wait_ge(proj, 1)
            a.copy(xT, m.ps[0:F, 1, :]).then_inc(copied, 1)
            a.wait_ge(maxed, 1)
            for b in range(GS):
                at = slice(b * T, (b + 1) * T)
                a.activation(p[:, at], m.ps[:, 2, at], ACT.Exp, bias=mx[:, b:b + 1], scale=scale,
                             accum_out=total[:, b:b + 1]).then_inc(exped, 1)
            a.wait_ge(turned, 1)
            a.copy(pT, m.ps[:, 3, :]).then_inc(turned_sb, 1)

        @block.vector
        def _(v):
            link = chain_of(v, own)
            norm.dve_normalize(v, link).then_inc(norm.normed, 1)
            v.wait_ge(scored, 1)
            link(v.tensor_reduce(mx, m.ps[:, 2, :].rearrange("p (b t) -> p b t", b=GS), AX.X, ALU.max))
            v.tensor_scalar(mx, mx, -scale, None, ALU.mult).then_inc(maxed, 1)
            v.wait_ge(exped, GS)
            link(v.reciprocal(m.rstd[:], total))
            v.wait_ge(out, 1)
            for b in range(GS):
                last = v.scalar_tensor_tensor(m.h[:, b, :], m.ps[:, 4, b * F:(b + 1) * F], m.rstd[:, b:b + 1],
                                              m.h[:, b, :], ALU.mult, ALU.add)
            link(last)


def layer2_attention(nc, m, g):
    norm = Norm(m, "l2a", m.h, m.n, m.nT, bank=0)
    norm2 = Norm(m, "l2a_own", m.n, m.n2, m.mT, bank=1)
    proj, copied, gated, scored, maxed, exped, vready, mixed, ogated, out, own = (m.sem("l2a_" + x) for x in (
        "projected", "projections_copied", "gate_tanh", "scores", "max", "exp", "values_scaled", "mixed", "gated",
        "out", "dve"))
    qT, kT, gT, og = m.big[:, 0:2, :], m.big[:, 2:4, :], m.big[:, 4:6, :], m.big[:, 6:8, :]
    scale = D2 ** -0.5
    pr = m.probs
    mx, total, rinv = (m.small[:, 16 * i:16 * (i + 1)] for i in range(3))
    with nc.Block() as block:
        @block.tensor
        def _(pe):
            norm.pe_turn(pe)
            norm2.pe_turn(pe)
            pe.wait_ge(norm.ready, 1)
            pe.wait_ge(norm2.ready, 1)
            for s in range(2):
                at = slice(s * 128, (s + 1) * 128)
                pe.matmul(m.ps[:, s, :], m.w["a2_wq"][:, at], m.mT[0:F, :], start=True, stop=True)
                pe.matmul(m.ps[:, 2 + s, :], m.w["a2_wk"][:, at], m.mT[0:F, :], start=True, stop=True)
                pe.matmul(m.ps[:, 4 + s, :], m.w["a2_wg"][:, at], m.nT[:], start=True, stop=True)
            for b in range(GS):
                last = pe.matmul(m.ps[:, 6 + b // 2, (b % 2) * 256:(b % 2 + 1) * 256], m.mT[0:F, b * T:(b + 1) * T],
                                 m.w["a2_wv"], start=True, stop=True)
            last.then_inc(proj, 1)
            pe.wait_ge(copied, 3)
            pe.wait_ge(gated, 1)
            for pair in range(2):
                for r in range(4):
                    rows = slice(32 * r, 32 * r + 32)
                    for b in range(2):
                        at = slice((2 * pair + b) * T, (2 * pair + b + 1) * T)
                        for s in range(2):
                            last = pe.matmul(m.ps[:, 4 * pair + r, (2 * b + s) * T:(2 * b + s + 1) * T],
                                             qT[rows, s, at], kT[rows, s, at], start=True, stop=True)
                last.then_inc(scored, 1)
            for pair in range(2):
                pe.wait_ge(exped, 16 * (pair + 1))
                pe.wait_ge(vready, pair + 1)
                for b in range(2):
                    bb = 2 * pair + b
                    for s in range(2):
                        for r in range(4):
                            col = (4 * s + r) * D2
                            last = pe.matmul(m.ps[32 * r:32 * r + 32, s, bb * T:(bb + 1) * T],
                                             m.values[:, bb, col:col + D2], pr[:, pair, r, b, s, :], start=True, stop=True)
                last.then_inc(mixed, 1)
            pe.wait_ge(ogated, 2)
            for b in range(GS):
                for s in range(2):
                    last = pe.matmul(m.ps[:, 2, b * F:(b + 1) * F], og[:, s, b * T:(b + 1) * T],
                                     m.w["a2_wf"][:, s * F:(s + 1) * F], start=s == 0, stop=s == 1)
            last.then_inc(out, 1)

        @block.scalar
        def _(a):
            norm.act_root(a)
            norm.act_copy(a)
            norm2.act_root(a)
            norm2.act_copy(a)
            a.wait_ge(proj, 1)
            a.activation(gT, m.ps[:, 4:6, :], ACT.Tanh, scale=0.5).then_inc(gated, 1)
            a.copy(qT, m.ps[:, 0:2, :]).then_inc(copied, 1)
            for pair in range(2):
                a.wait_ge(maxed, pair + 1)
                for i in range(16):
                    r, b, s = i // 4, i // 2 % 2, i % 2
                    a.activation(pr[:, pair, r, b, s, :], m.ps[:, 4 * pair + r, (i % 4) * T:(i % 4 + 1) * T], ACT.Exp,
                                 bias=m.l2max[:, pair, i:i + 1], scale=scale,
                                 accum_out=m.l2sum[:, pair, i:i + 1]).then_inc(exped, 1)

        @block.vector
        def _(v):
            link = chain_of(v, own)
            norm.dve_normalize(v, link).then_inc(norm.normed, 1)
            v.wait_ge(norm.normed, 1)
            link(norm2.dve_normalize(v, link))
            link(v.tensor_tensor(m.n2[:], m.n2[:], spread(m.w["a2_gamma"], 1, GS), ALU.mult))
            v.tensor_tensor(m.n2[:], m.n2[:], spread(m.w["a2_beta"], 1, GS), ALU.add).then_inc(norm2.normed, 1)
            link(v.tensor_tensor(m.h[:], m.h[:], m.n[:], ALU.add))
            link(v.tensor_tensor(m.h[:], m.h[:], spread(m.w["a2_bf"], 1, GS), ALU.add))
            v.wait_ge(proj, 1)
            v.tensor_copy(kT, m.ps[:, 2:4, :]).then_inc(copied, 1)
            v.tensor_copy(m.values[:].rearrange("p b c -> p (b c)"), m.ps[:, 6:8, :].rearrange("p k c -> p (k c)")).then_inc(copied, 1)
            v.wait_ge(gated, 1)
            link(v.tensor_scalar(gT, gT, 0.5, 0.5, ALU.mult, ALU.add))
            for pair in range(2):
                v.wait_ge(scored, pair + 1)
                link(v.tensor_reduce(m.l2max[:, pair, :],
                                     m.ps[:, 4 * pair:4 * pair + 4, :].rearrange("p r (c t) -> p r c t", t=T), AX.X, ALU.max))
                v.tensor_scalar(m.l2max[:, pair, :], m.l2max[:, pair, :], -scale, None, ALU.mult).then_inc(maxed, 1)
            v.wait_ge(copied, 3)
            for pair in range(2):
                v.wait_ge(exped, 16 * (pair + 1))
                link(v.reciprocal(rinv, m.l2sum[:, pair, :]))
                for b in range(2):
                    vals = m.values[:, 2 * pair + b, :].rearrange("p (s r d) -> p s r d", s=2, r=4)
                    by = rinv.rearrange("p (r b s) -> p b s r", r=4, b=2)[:, b]
                    last = v.tensor_tensor(vals, vals, spread(by, 3, D2), ALU.mult)
                last.then_inc(vready, 1)
                v.wait_ge(vready, pair + 1)
            v.wait_ge(mixed, 2)
            for s in range(2):
                v.tensor_tensor(og[:, s, :], m.ps[:, s, :], gT[:, s, :], ALU.mult).then_inc(ogated, 1)
            v.wait_ge(out, 1)
            link(v.tensor_tensor(m.h[:], m.h[:], m.ps[:, 2, 0:GS * F].rearrange("p (b f) -> p b f", b=GS), ALU.add))


def layer2_tree(nc, m, g):
    norm = Norm(m, "l2t", m.h, m.n, m.nT)
    scored, absed, acted, product, weighted, summed, own = (m.sem("l2t_" + x) for x in (
        "scores", "abs", "gelu", "products", "weighted", "summed", "dve"))
    right, ind, gate = m.tree[:, 0], m.tree[:, 1], m.tree[:, 2]
    scores = m.ps[:, 0:2, :].rearrange("p k (b n) -> p (k b) n", b=2)
    steps = [(b, c) for b in range(GS) for c in range((NODES + 1) // PER // 2)]
    with nc.Block() as block:
        @block.tensor
        def _(pe):
            norm.pe_turn(pe)
            pe.wait_ge(norm.ready, 1)
            for b in range(GS):
                last = pe.matmul(m.ps[:, b // 2, (b % 2) * 256:(b % 2 + 1) * 256], m.nT[:, b * T:(b + 1) * T],
                                 m.w["tree_w1"], start=True, stop=True)
            last.then_inc(scored, 1)
            for i, (b, c) in enumerate(steps):
                if i >= 3:
                    pe.wait_ge(weighted, i - 2)
                for k in range(2):
                    n = min(PER, NODES - (2 * c + k) * PER) * F
                    at = (2 * c + k) * PER * F
                    last = pe.matmul(m.ps[:, 2 + 2 * (i % 3) + k, 0:n], m.nT[:, b * T:(b + 1) * T],
                                     m.tree_w2[:, at:at + n], start=True, stop=True)
                last.then_inc(product, 1)

        @block.scalar
        def _(a):
            norm.act_root(a)
            norm.act_copy(a)
            a.wait_ge(scored, 1)
            a.activation(gate, scores, ACT.Abs).then_inc(absed, 1)
            a.wait_ge(absed, 1)
            a.activation(gate, gate, ACT.Gelu).then_inc(acted, 1)

        @block.vector
        def _(v):
            link = chain_of(v, own)
            norm.dve_normalize(v, link).then_inc(norm.normed, 1)
            v.wait_ge(absed, 1)
            link(v.tensor_scalar(right, scores, 0.0, None, ALU.is_gt))
            link(v.memset(ind[:, :, 0:1], 1.0))
            for level in range(TREE_DEPTH):
                lo, n = 2 ** level - 1, 2 ** level
                kids = ind[:, :, 2 * lo + 1:2 * lo + 1 + 2 * n].rearrange("p b (n k) -> p b n k", k=2)
                link(v.tensor_tensor(kids[:, :, :, 1], ind[:, :, lo:lo + n], right[:, :, lo:lo + n], ALU.mult))
                link(v.tensor_tensor(kids[:, :, :, 0], ind[:, :, lo:lo + n], kids[:, :, :, 1], ALU.subtract))
            v.wait_ge(acted, 1)
            link(v.tensor_tensor(gate[:, :, 0:NODES], gate[:, :, 0:NODES], ind[:, :, 0:NODES], ALU.mult))
            for i, (b, c) in enumerate(steps):
                n = min(2 * PER, NODES - 2 * c * PER)
                v.wait_ge(product, i + 1)
                if i >= 3:
                    v.wait_ge(summed, i - 2)
                v.tensor_tensor(m.weighted[:, i % 3, 0:n, :],
                                m.ps[:, 2 + 2 * (i % 3):4 + 2 * (i % 3), :].rearrange("p k (n f) -> p (k n) f", f=F)[:, 0:n, :],
                                spread(gate[:, b, 2 * c * PER:2 * c * PER + n], 2, F), ALU.mult).then_inc(weighted, 1)
            v.wait_ge(summed, len(steps))
            for b in range(GS):
                last = v.tensor_reduce(m.n2[:, b, :], m.summed[:, b].rearrange("p n f -> p f n"), AX.X, ALU.add)
            link(last)
            link(v.tensor_tensor(m.h[:], m.h[:], m.n2[:], ALU.add))

        @block.gpsimd
        def _(pool):
            for i, (b, c) in enumerate(steps):
                n = min(2 * PER, NODES - 2 * c * PER)
                pool.wait_ge(weighted, i + 1)
                if c:
                    pool.wait_ge(summed, i)
                    pool.tensor_tensor(m.summed[:, b, 0:n, :], m.summed[:, b, 0:n, :], m.weighted[:, i % 3, 0:n, :],
                                       ALU.add).then_inc(summed, 1)
                else:
                    pool.tensor_copy(m.summed[:, b], m.weighted[:, i % 3]).then_inc(summed, 1)


def layer3_attention(nc, m, g):
    norm = Norm(m, "l3a", m.h, m.n, m.nT)
    proj, copied, evals, ecopied, omega, masked, out, own = (m.sem("l3a_" + x) for x in (
        "queries", "queries_copied", "values", "values_copied", "omega", "omega_masked", "out", "dve"))
    qT = m.big
    with nc.Block() as block:
        @block.tensor
        def _(pe):
            norm.pe_turn(pe)
            pe.wait_ge(norm.ready, 1)
            for h in range(HEADS):
                if h >= 2:
                    pe.wait_ge(copied, h - 1)
                pe.matmul(m.ps[0:F, 1 + h % 2, :], m.w["a3_q"][:, h * F:(h + 1) * F], m.nT[0:F, :], start=True, stop=True).then_inc(proj, 1)
            pe.wait_ge(copied, HEADS)
            for b in range(GS):
                nb = m.nT[0:F, b * T:(b + 1) * T]
                if b >= 1:
                    pe.wait_ge(ecopied, b)
                pe.matmul(m.ps[:, 3, :], nb, m.w["a3_e"], start=True, stop=True).then_inc(evals, 1)
                for half in range(2):
                    i = 2 * b + half
                    if i >= 2:
                        pe.wait_ge(masked, i - 1)
                    pe.matmul(m.ps[:, 4 + half, :], nb, qT[0:F, 4 * half:4 * half + 4, b * T:(b + 1) * T], start=True,
                              stop=True).then_inc(omega, 1)
                pe.wait_ge(ecopied, b + 1)
                for half in range(2):
                    pe.wait_ge(masked, 2 * b + half + 1)
                    for k in range(4):
                        h = 4 * half + k
                        last = pe.matmul(m.ps[:, 6, b * F:(b + 1) * F], m.omega[:, half, k * T:(k + 1) * T],
                                         m.evals[:, b % 2, h * F:(h + 1) * F], start=h == 0, stop=h == HEADS - 1)
                last.then_inc(out, 1)

        @block.scalar
        def _(a):
            norm.act_root(a)
            norm.act_copy(a)
            for h in range(HEADS):
                a.wait_ge(proj, h + 1)
                a.copy(qT[0:F, h, :], m.ps[0:F, 1 + h % 2, :]).then_inc(copied, 1)
            for b in range(GS):
                a.wait_ge(evals, b + 1)
                if b >= 2:
                    a.wait_ge(out, b - 1)
                a.copy(m.evals[:, b % 2, :], m.ps[:, 3, :]).then_inc(ecopied, 1)

        @block.vector
        def _(v):
            link = chain_of(v, own)
            norm.dve_normalize(v, link).then_inc(norm.normed, 1)
            for b in range(GS):
                for half in range(2):
                    v.wait_ge(omega, 2 * b + half + 1)
                    if b >= 1:
                        v.wait_ge(out, b)
                    v.tensor_tensor(m.omega[:, half, :].rearrange("p (k t) -> p k t", t=T),
                                    m.ps[:, 4 + half, :].rearrange("p (k t) -> p k t", t=T),
                                    spread(m.w["upper"], 1, 4), ALU.mult).then_inc(masked, 1)
            v.wait_ge(out, GS)
            link(v.tensor_tensor(m.h[:], m.h[:], m.ps[:, 6, 0:GS * F].rearrange("p (b f) -> p b f", b=GS), ALU.add))


def layer3_input(nc, m, g):
    norm = Norm(m, "l3i", m.h, m.n, m.nT)
    own, kept = m.sem("l3i_dve"), m.sem("l3i_kept")
    with nc.Block() as block:
        @block.tensor
        def _(pe):
            norm.pe_turn(pe)

        @block.scalar
        def _(a):
            norm.act_root(a)
            a.wait_ge(norm.inps, 1)
            a.copy(m.nT_all[:, bass.ts(g, TOK)], m.ps[0:F, 0, :]).then_inc(kept, 1)
            a.wait_ge(kept, 1)

        @block.vector
        def _(v):
            link = chain_of(v, own)
            norm.dve_normalize(v, link).then_inc(norm.normed, 1)
            link(v.tensor_copy(m.h_all[:, bass.ts(g, GS * F)], m.h[:].rearrange("p b f -> p (b f)")))


LAYERS = [layer0_tokens, layer0_attention, layer0_mixture, layer1_attention, layer1_mixture,
          layer2_attention, layer2_tree, layer3_attention]


def stairs():
    return [(0, 1, 16), (1, 1, 8), (2, 2, 5), (4, 4, 3), (8, 8, 1)]


class Memory3:

    NAMES = ("weights_loaded", "input", "query_in_psum", "query", "attn_query", "scores_in_psum", "scores", "best16",
             "exp16", "factor", "scores_shifted", "scores_turned", "factor_spread", "high", "low", "factor_copied",
             "sum", "exp", "weights", "product", "kv", "kv_turned", "values", "masked", "attn_max", "attn_exp",
             "probs_turned", "probs_copied", "mixed", "mixed_copied", "out", "out_added", "dve", "output_weights")

    def __init__(self, m, groups, heads):
        self.m, self.groups, self.heads = m, groups, heads
        self.s = {n: m.sem("pk_" + n) for n in self.NAMES}
        self.links = 0

    def pe_queries(self, pe, k):
        m, s = self.m, self.s
        pe.wait_ge(s["weights_loaded"], 16 * k)
        pe.wait_ge(s["input"], k)
        if k > 1 or m.backs:
            pe.wait_ge(s["values"], k)
            pe.wait_ge(s["masked"], k)
        pe.matmul(m.ps[0:F, 6, :], m.front[:, 0:64], m.x[:], start=True, stop=True)
        pe.matmul(m.ps[0:F, 7, :], m.front[:, 192:256], m.x[:], start=True, stop=True).then_inc(s["query_in_psum"], 1)

    def pe_scores(self, pe, k):
        m, s = self.m, self.s
        pe.wait_ge(s["query"], k)
        for b in range(GS):
            last = pe.matmul(m.ps[:, 6, b * 128:(b + 1) * 128], m.qT[:, b * T:(b + 1) * T], m.front[:, 64:192],
                             start=True, stop=True)
        last.then_inc(s["scores_in_psum"], 1)

    def pe_turn_scores(self, pe, k):
        m, s = self.m, self.s
        pe.wait_ge(s["scores_shifted"], k)
        for b in range(GS):
            at = slice(b * T, (b + 1) * T)
            last = pe.transpose(m.ps[:, 6, at], m.sc[:, at], m.w["ident"])
        last.then_inc(s["scores_turned"], 1)
        pe.wait_ge(s["factor"], k)
        if m.backs:
            pe.wait_ge(s["out_added"], k)
        else:
            pe.wait_ge(s["attn_query"], k)
        for b in range(GS):
            at = slice(b * T, (b + 1) * T)
            last = pe.matmul(m.ps[:, 7, at], m.factor[:, b:b + 1].to_broadcast([128, 128]), m.w["ident"],
                             start=True, stop=True)
        last.then_inc(s["factor_spread"], 1)

    def pe_sum(self, pe, u, c):
        m, s = self.m, self.s
        n = u * CHUNKS + c
        if n >= 4:
            pe.wait_ge(s["weights"], n - 3)
        if u == 1 and c == 0:
            pe.wait_ge(s["high"], 1)
            pe.wait_ge(s["low"], 1)
        sel = m.sel[:, c * 128:(c + 1) * 128]
        pe.matmul(m.ps[:, c % 4, :], sel, m.high[:, u, :], start=True, stop=False)
        pe.matmul(m.ps[:, c % 4, :], sel, m.low[:, u, :], start=False, stop=True).then_inc(s["sum"], 1)

    def pe_product(self, pe, u, c):
        m, s = self.m, self.s
        if u == 0 and c % PIECE == 0:
            loaded = m.table_loaded[c // PIECE]
            pe.wait_ge(loaded, 16)
            pe.sem_clear(loaded)
        pe.wait_ge(s["weights"], u * CHUNKS + c + 1)
        if u == 1 and c == 0:
            pe.wait_ge(s["kv"], 1)
        pe.matmul(m.ps[:, 4 + u, :], m.table[:, c * 128:(c + 1) * 128], m.wts[:, (u * CHUNKS + c) % 3, :],
                  start=c == 0, stop=c == CHUNKS - 1).then_inc(s["product"], 1)

    def pe_attention_scores(self, pe, k, q):
        m, s = self.m, self.s
        pe.wait_ge(s["kv"], k)
        if k > 1:
            pe.wait_ge(s["high"], k - 1)
            pe.wait_ge(s["low"], k - 1)
            pe.wait_ge(s["factor_copied"], k - 1)
        for b in range(GS):
            at = slice(b * T, (b + 1) * T)
            pe.transpose(m.ps[:, 6, at], m.kvT[:, at], m.w["ident"])
            last = pe.matmul(m.ps[:, 7, at], m.aT[:, q, at], m.kvT[0:F, at], start=True, stop=True)
        last.then_inc(s["kv_turned"], 1)

    def pe_turn_probs(self, pe, k):
        m, s = self.m, self.s
        pe.wait_ge(s["attn_exp"], GS * k)
        if m.fronts:
            pe.wait_ge(s["attn_query"], k)
        for b in range(GS):
            at = slice(b * T, (b + 1) * T)
            last = pe.transpose(m.ps[:, 7, at], m.probs3[:, at], m.w["ident"])
        last.then_inc(s["probs_turned"], 1)

    def pe_mix(self, pe, k):
        m, s = self.m, self.s
        pe.wait_ge(s["probs_copied"], k)
        for b in range(GS):
            at = slice(b * T, (b + 1) * T)
            last = pe.matmul(m.ps[0:F, 7, at], m.vals[:, b, :], m.probsT[:, at], start=True, stop=True)
        last.then_inc(s["mixed"], 1)

    def pe_out(self, pe, k, q):
        m, s = self.m, self.s
        pe.wait_ge(s["mixed_copied"], k)
        for b in range(GS):
            last = pe.matmul(m.ps[:, 7, b * F:(b + 1) * F], m.mixT[:, b * T:(b + 1) * T], m.wo[:, q, :],
                             start=True, stop=True)
        last.then_inc(s["out"], 1)

    def act_input(self, a, k, group):
        m, s = self.m, self.s
        if k > 1:
            a.wait_ge(s["query_in_psum"], k - 1)
        a.copy(m.x[:], m.nT_all[:, bass.ts(group, TOK)]).then_inc(s["input"], 1)

    def act_queries(self, a, k, q):
        m, s = self.m, self.s
        a.wait_ge(s["query_in_psum"], k)
        a.copy(m.qT[:], m.ps[0:F, 6, :]).then_inc(s["query"], 1)
        a.copy(m.aT[:, q, :], m.ps[0:F, 7, :]).then_inc(s["attn_query"], 1)

    def act_scores(self, a, k):
        m, s = self.m, self.s
        a.wait_ge(s["scores_in_psum"], k)
        a.copy(m.sc[:], m.ps[:, 6, :]).then_inc(s["scores"], 1)

    def act_exp16(self, a, k):
        m, s = self.m, self.s
        a.wait_ge(s["best16"], k)
        a.activation(m.e16[:], m.v16[:], ACT.Exp)
        a.activation(m.efloor[:], m.floor[:], ACT.Exp, bias=m.shift[:, 1:2]).then_inc(s["exp16"], 1)

    def act_high(self, a, k, q):
        m, s = self.m, self.s
        a.wait_ge(s["scores_turned"], k)
        a.copy(m.high[:, q, :], m.ps[:, 6, :]).then_inc(s["high"], 1)

    def act_exp(self, a, u, c):
        m, s = self.m, self.s
        n = u * CHUNKS + c
        a.wait_ge(s["sum"], n + 1)
        if n >= 3:
            a.wait_ge(s["weights"], n - 2)
        a.activation(m.exps[:, n % 3, :], m.ps[:, c % 4, :], ACT.Exp, bias=m.shift[:, 0:1]).then_inc(s["exp"], 1)

    def act_attention(self, a, k):
        m, s = self.m, self.s
        a.wait_ge(s["attn_max"], k)
        for b in range(GS):
            at = slice(b * T, (b + 1) * T)
            a.activation(m.probs3[:, at], m.msk[:, at], ACT.Exp, bias=m.amax[:, b:b + 1], scale=F ** -0.5,
                         accum_out=m.asum[:, b:b + 1]).then_inc(s["attn_exp"], 1)

    def act_probs(self, a, k):
        m, s = self.m, self.s
        a.wait_ge(s["probs_turned"], k)
        a.copy(m.probsT[:], m.ps[:, 7, :]).then_inc(s["probs_copied"], 1)

    def act_mixed(self, a, k):
        m, s = self.m, self.s
        a.wait_ge(s["mixed"], k)
        a.copy(m.mixT[:], m.ps[0:F, 7, :]).then_inc(s["mixed_copied"], 1)

    def link(self, v, ins):
        self.links += 1
        ins.then_inc(self.s["dve"], 1)
        v.wait_ge(self.s["dve"], self.links)

    def dve_weights(self, v, u, c):
        m, s = self.m, self.s
        n = u * CHUNKS + c
        v.wait_ge(s["exp"], n + 1)
        if n >= 3:
            v.wait_ge(s["product"], n - 2)
        v.scalar_tensor_tensor(m.wts[:, n % 3, :], m.ps[:, c % 4, :], 0.0, m.exps[:, n % 3, :], ALU.is_ge,
                               ALU.mult).then_inc(s["weights"], 1)

    def scores_by_half(self):
        return self.m.sc[:].rearrange("p (i k) -> p i k", k=KEYS)

    def dve_first8(self, v, k, half):
        m, s = self.m, self.s
        v.wait_ge(s["scores"], k)
        for i in range(half * GS, (half + 1) * GS):
            last = v.max(m.top[:, i, 0:8], self.scores_by_half()[:, i, :])
        self.link(v, last)

    def dve_strike8(self, v, half):
        m = self.m
        for i in range(half * GS, (half + 1) * GS):
            last = v.match_replace(out=m.rest[:, i, :], in_to_replace=m.top[:, i, 0:8],
                                   in_values=self.scores_by_half()[:, i, :], imm_value=LOWEST)
        self.link(v, last)

    def dve_second8(self, v, half):
        m = self.m
        for i in range(half * GS, (half + 1) * GS):
            last = v.max(m.top[:, i, 8:16], m.rest[:, i, :])
        self.link(v, last)

    def dve_candidates(self, v):
        m = self.m
        self.link(v, v.tensor_tensor(m.topd[:], m.top[:], m.top[:, :, 0:1].to_broadcast([128, 2 * GS, TOPK]), ALU.subtract))
        pairs = m.topd[:].rearrange("p (b s) r -> p b s r", s=2)
        at = 0
        for a0, na, nb in stairs():
            last = v.tensor_tensor(m.cand[:, :, at:at + na * nb].rearrange("p b (x y) -> p b x y", x=na),
                                   spread(pairs[:, :, 0, a0:a0 + na], 3, nb), spread(pairs[:, :, 1, 0:nb], 2, na), ALU.add)
            at += na * nb
        self.link(v, last)

    def dve_best16(self, v, part):
        m = self.m
        for b in range(GS):
            if part == 0:
                last = v.max(m.v16[:, b, 0:8], m.cand[:, b, :])
            elif part == 1:
                last = v.match_replace(out=m.cand2[:, b, :], in_to_replace=m.v16[:, b, 0:8], in_values=m.cand[:, b, :],
                                       imm_value=LOWEST)
            else:
                last = v.max(m.v16[:, b, 8:16], m.cand2[:, b, :])
        self.link(v, last)

    def dve_floor(self, v, k):
        m, s = self.m, self.s
        self.link(v, v.tensor_scalar(m.floor[:], m.v16[:, :, TOPK - 1], 1.0 + 2.0 ** -19, -2.0 ** -22, ALU.mult, ALU.add))
        v.tensor_scalar(m.floor[:], m.floor[:], EXP_ZERO, None, ALU.max).then_inc(s["best16"], 1)
        v.wait_ge(s["best16"], k)

    def dve_shift_scores(self, v, k):
        m, s = self.m, self.s
        byhalf = self.scores_by_half()
        self.link(v, v.tensor_tensor(byhalf, byhalf, m.top[:, :, 0:1].to_broadcast([128, 2 * GS, KEYS]), ALU.subtract))
        second = m.sc[:].rearrange("p (b s k) -> p b s k", s=2, k=KEYS)[:, :, 1, :]
        self.link(v, v.tensor_tensor(second, second, spread(m.floor[:], 2, KEYS), ALU.subtract))
        v.tensor_scalar(m.sc[:], m.sc[:], SCORE_MIN, None, ALU.max).then_inc(s["scores_shifted"], 1)

    def dve_factor(self, v, k):
        m, s = self.m, self.s
        v.wait_ge(s["exp16"], k)
        self.link(v, v.tensor_reduce(m.sum16[:], m.e16[:], AX.X, ALU.add))
        self.link(v, v.reciprocal(m.sum16[:], m.sum16[:]))
        v.tensor_tensor(m.factor[:], m.sum16[:], m.efloor[:], ALU.mult).then_inc(s["factor"], 1)

    def dve_low(self, v, k, q):
        m, s = self.m, self.s
        v.wait_ge(s["high"], k)
        v.tensor_tensor(m.low[:, q, :], m.ps[:, 6, :], m.high[:, q, :], ALU.subtract).then_inc(s["low"], 1)

    def dve_factor_copy(self, v, k, q):
        m, s = self.m, self.s
        v.wait_ge(s["factor_spread"], k)
        v.tensor_copy(m.factorT[:, q, :], m.ps[:, 7, :]).then_inc(s["factor_copied"], 1)

    def dve_kv(self, v, k, q):
        m, s = self.m, self.s
        if k > 1:
            v.wait_ge(s["product"], CHUNKS * (k - 1))
        v.tensor_tensor(m.kvT[:], m.ps[:, 4 + q, :], m.factorT[:, q, :], ALU.mult).then_inc(s["kv"], 1)

    def dve_values(self, v, k):
        m, s = self.m, self.s
        v.wait_ge(s["kv_turned"], k)
        v.tensor_copy(m.vals[:], m.ps[:, 6, :].rearrange("p (b c) -> p b c", b=GS)[:, :, F:2 * F]).then_inc(s["values"], 1)
        v.tensor_tensor(m.msk[:].rearrange("p (b t) -> p b t", b=GS), m.ps[:, 7, :].rearrange("p (b t) -> p b t", b=GS),
                        spread(m.w["causal"], 1, GS), ALU.add).then_inc(s["masked"], 1)

    def dve_attention_max(self, v, k):
        m, s = self.m, self.s
        v.wait_ge(s["masked"], k)
        self.link(v, v.tensor_reduce(m.amax[:], m.msk[:].rearrange("p (b t) -> p b t", b=GS), AX.X, ALU.max))
        v.tensor_scalar(m.amax[:], m.amax[:], -F ** -0.5, None, ALU.mult).then_inc(s["attn_max"], 1)

    def dve_out(self, v, k, group):
        m, s = self.m, self.s
        v.wait_ge(s["attn_exp"], GS * k)
        self.link(v, v.reciprocal(m.arec[:], m.asum[:]))
        v.wait_ge(s["out"], k)
        v.tensor_tensor(m.outw[:], m.ps[:, 7, 0:GS * F].rearrange("p (b f) -> p b f", b=GS),
                        spread(m.arec[:], 2, F), ALU.mult).then_inc(s["out_added"], 1)
        v.wait_ge(s["out_added"], k)
        state = m.h_all[:, bass.ts(group, GS * F)]
        self.link(v, v.tensor_tensor(state, state, m.outw[:].rearrange("p b f -> p (b f)"), ALU.add))


def first_front(nc, m, lay):
    m.fronts, m.backs = True, False
    lay.links = 0
    s = lay.s
    with nc.Block() as block:
        @block.sync
        def _(sp):
            sp.dma_start(m.front[:], m.dram["head"][0, :, 0:256]).then_inc(s["weights_loaded"], 16)
            sp.wait_ge(s["weights_loaded"], 16)
            for i in range(CHUNKS // PIECE):
                at = slice(i * PIECE * 128, (i + 1) * PIECE * 128)
                sp.dma_start(m.table[:, at], m.dram["table"][0, :, at]).then_inc(m.table_loaded[i], 16)

        @block.tensor
        def _(pe):
            lay.pe_queries(pe, 1)
            lay.pe_scores(pe, 1)
            lay.pe_turn_scores(pe, 1)

        @block.scalar
        def _(a):
            lay.act_input(a, 1, 0)
            lay.act_queries(a, 1, 0)
            lay.act_scores(a, 1)
            lay.act_exp16(a, 1)
            lay.act_high(a, 1, 0)

        @block.vector
        def _(v):
            v.memset(m.ps[:, 5, :], 0.0)
            v.memset(m.factorT[:, 1, :], 0.0)
            v.memset(m.aT[:, 1, :], 0.0)
            v.memset(m.wo[:, 1, :], 0.0)
            for half in range(2):
                lay.dve_first8(v, 1, half)
                lay.dve_strike8(v, half)
                lay.dve_second8(v, half)
            lay.dve_candidates(v)
            for part in range(3):
                lay.dve_best16(v, part)
            lay.dve_floor(v, 1)
            lay.dve_shift_scores(v, 1)
            lay.dve_factor(v, 1)
            lay.dve_low(v, 1, 0)
            lay.dve_factor_copy(v, 1, 0)


def two_units(nc, m, lay, j):
    m.fronts, m.backs = True, True
    lay.links = 0
    s = lay.s
    groups, heads = lay.groups, lay.heads
    with nc.Block() as block:
        @block.sync
        def _(sp):
            for u in range(2):
                k = u + 1
                if k > 1:
                    sp.wait_ge(s["scores_in_psum"], k - 1)
                sp.dma_start(m.front[:], m.dram["head"][(j * 2 + (u + 1)) // groups, :, 0:256]).then_inc(s["weights_loaded"], 16)
                if k > 1:
                    sp.wait_ge(s["out"], 1)
                sp.dma_start(m.wo[:, u, :], m.dram["head"][(j * 2 + u) // groups, :, 256:320]).then_inc(s["output_weights"], 16)
            for i in range(CHUNKS // PIECE):
                at = slice(i * PIECE * 128, (i + 1) * PIECE * 128)
                sp.wait_ge(s["product"], CHUNKS + (i + 1) * PIECE)
                sp.dma_start(m.table[:, at], m.dram["table"][(j * 2 + 2) // groups % heads, :, at]).then_inc(m.table_loaded[i], 16)

        @block.tensor
        def _(pe):
            for u in range(2):
                k = u + 1
                for c in range(CHUNKS):
                    lay.pe_sum(pe, u, c)
                    if c >= 2:
                        lay.pe_product(pe, u, c - 2)
                    elif u == 1:
                        lay.pe_product(pe, 0, CHUNKS - 2 + c)
                    if c == 4:
                        lay.pe_attention_scores(pe, k, 1 - u)
                    if c == 7:
                        lay.pe_queries(pe, k)
                    if c == 10:
                        lay.pe_scores(pe, k)
                    if c == 12:
                        lay.pe_turn_probs(pe, k)
                    if c == 15:
                        lay.pe_mix(pe, k)
                    if c == 18:
                        lay.pe_out(pe, k, 1 - u)
                    if c == 27:
                        lay.pe_turn_scores(pe, k)
            for c in range(CHUNKS - 2, CHUNKS):
                lay.pe_product(pe, 1, c)
            pe.wait_ge(s["output_weights"], 32)

        @block.scalar
        def _(a):
            for u in range(2):
                k = u + 1
                for c in range(CHUNKS):
                    lay.act_exp(a, u, c)
                    if c == 0:
                        lay.act_input(a, k, (j * 2 + (u + 1)) % groups)
                    if c == 8:
                        lay.act_queries(a, k, 1 - u)
                    if c == 9:
                        lay.act_attention(a, k)
                    if c == 11:
                        lay.act_scores(a, k)
                    if c == 13:
                        lay.act_probs(a, k)
                    if c == 16:
                        lay.act_mixed(a, k)
                    if c == 24:
                        lay.act_exp16(a, k)
                    if c == 28:
                        lay.act_high(a, k, 1 - u)

        @block.vector
        def _(v):
            for u in range(2):
                k = u + 1
                for c in range(CHUNKS):
                    lay.dve_weights(v, u, c)
                    if c == 2:
                        lay.dve_kv(v, k, 1 - u)
                    if c == 5:
                        lay.dve_values(v, k)
                    if c == 6:
                        lay.dve_attention_max(v, k)
                    if c in (12, 13):
                        lay.dve_first8(v, k, c - 12)
                    if c in (14, 15):
                        lay.dve_strike8(v, c - 14)
                    if c in (16, 17):
                        lay.dve_second8(v, c - 16)
                    if c == 18:
                        lay.dve_candidates(v)
                    if c == 19:
                        lay.dve_out(v, k, (j * 2 + (u + groups - 1)) % groups)
                    if c in (20, 21, 22):
                        lay.dve_best16(v, c - 20)
                    if c == 23:
                        lay.dve_floor(v, k)
                    if c == 24:
                        lay.dve_shift_scores(v, k)
                    if c == 25:
                        lay.dve_factor(v, k)
                    if c == 29:
                        lay.dve_low(v, k, 1 - u)
                    if c == 30:
                        lay.dve_factor_copy(v, k, 1 - u)


def last_back(nc, m, lay):
    m.fronts, m.backs = False, True
    lay.links = 0
    with nc.Block() as block:
        @block.sync
        def _(sp):
            for loaded in m.table_loaded:
                sp.wait_ge(loaded, 16)

        @block.tensor
        def _(pe):
            lay.pe_attention_scores(pe, 1, 1)
            lay.pe_turn_probs(pe, 1)
            pe.wait_ge(lay.s["values"], 1)
            lay.pe_mix(pe, 1)
            lay.pe_out(pe, 1, 1)

        @block.scalar
        def _(a):
            lay.act_attention(a, 1)
            lay.act_probs(a, 1)
            lay.act_mixed(a, 1)

        @block.vector
        def _(v):
            lay.dve_kv(v, 1, 1)
            lay.dve_values(v, 1)
            lay.dve_attention_max(v, 1)
            lay.dve_out(v, 1, lay.groups - 1)


def audio_tower(nc, win, pack, tree_w2, head, table, sel, out, layers=LAYERS, last=True, groups=GROUPS, heads=HEADS):
    with ExitStack() as ctx:
        m = Memory()
        sems = {}

        def sem(name):
            if name not in sems:
                sems[name] = ctx.enter_context(nc.semaphore(name))
            return sems[name]

        def sb(where, name, shape, dtype=F32):
            return where.enter_context(nc.sbuf_tensor(name, shape, dtype))

        def used():
            nums = [x.num for x in sems.values()]
            assert max(nums) - min(nums) + 1 == len(nums)
            return range(min(nums), max(nums) + 1)

        m.table_loaded = [ctx.enter_context(nc.semaphore(f"table_piece_{i}_loaded")) for i in range(CHUNKS // PIECE)]
        m.sem = sem
        m.dram = {"win": win, "table": table, "head": head}
        m.ps = ctx.enter_context(nc.psum_tensor("ps", [128, BANKS, 512], F32))
        m.h_all = sb(ctx, "h_all", [128, SEQS * F])
        m.nT_all = sb(ctx, "nT_all", [F, SEQS * T])
        m.big = sb(ctx, "big", [128, 8, TOK])
        cols = pack_columns()
        m.packed = sb(ctx, "packed", [128, sum(c for _, c in cols.values())])
        m.w, at = {}, 0
        for name, (nr, n) in cols.items():
            m.w[name] = m.packed[0:nr, at:at + n]
            at += n

        with ExitStack() as phase:
            m.h = sb(phase, "h", [128, GS, F])
            m.n = sb(phase, "n", [128, GS, F])
            m.n2 = sb(phase, "n2", [128, GS, F])
            m.nT = sb(phase, "nT", [FB, TOK])
            m.mT = sb(phase, "mT", [FB, TOK])
            m.stats = sb(phase, "stats", [128, GS, 6])
            m.moments = sb(phase, "moments", [128, GS, 2])
            m.var = sb(phase, "var", [128, GS])
            m.std = sb(phase, "std", [128, GS])
            m.rstd = sb(phase, "rstd", [128, GS])
            m.small = sb(phase, "small", [128, 64])
            m.window = sb(phase, "window", [128, GS, TAPS * F])
            m.gate = sb(phase, "gate", [128, 4, GS, EXPERTS])
            m.wide = sb(phase, "wide", [128, 2, 512])
            m.ones = sb(phase, "ones", [1, 128])
            m.values = sb(phase, "values", [128, GS, H2 * D2])
            m.l2max = sb(phase, "l2max", [128, 2, 16])
            m.l2sum = sb(phase, "l2sum", [128, 2, 16])
            m.tree = sb(phase, "tree", [128, 3, GS, NODES + 1])
            m.tree_w2 = sb(phase, "tree_w2", [FB, NODES * F])
            m.omega = sb(phase, "omega", [128, 2, 512])
            m.evals = sb(phase, "evals", [128, 2, 512])
            shared = phase.enter_context(nc.sbuf_tensor("shared", [128, 7 * 2 * PER * F], F32))
            m.probs = shared[:, 0:4096].rearrange("p (q r b s t) -> p q r b s t", q=2, r=4, b=2, s=2)
            m.weighted = shared[:, 0:3072].rearrange("p (k n f) -> p k n f", k=3, f=F)
            m.summed = shared[:, 3072:7168].rearrange("p (b n f) -> p b n f", b=GS, f=F)

            loaded = sem("weights_loaded")
            with nc.Block() as block:
                @block.sync
                def _(sp):
                    sp.dma_start(m.packed[:], pack).then_inc(loaded, 16)
                    sp.dma_start(m.tree_w2[:], tree_w2).then_inc(loaded, 16)
                    sp.wait_ge(loaded, 32)

                @block.vector
                def _(v):
                    v.memset(m.nT[F:FB, :], 1.0)
                    v.memset(m.mT[F:FB, :], 1.0)
                    v.memset(m.ones[:], 1.0)

            with nc.Fori(0, groups) as g:
                for layer in layers:
                    layer(nc, m, g)
                layer3_input(nc, m, g)
                nc.all_engine_barrier(sems_to_clear=used())

        if last:
            with ExitStack() as phase:
                m.table = sb(phase, "table", [128, CHUNKS * 2 * F])
                m.front = sb(phase, "front", [F, 256])
                m.wo = sb(phase, "wo", [F, 2, F])
                m.sel = sb(phase, "sel", [128, CHUNKS * 128], F16)
                m.x = sb(phase, "x", [F, TOK])
                m.qT = sb(phase, "qT", [F, TOK])
                m.aT = sb(phase, "aT", [F, 2, TOK])
                m.sc = sb(phase, "sc", [128, TOK])
                m.top = sb(phase, "top", [128, 2 * GS, TOPK])
                m.topd = sb(phase, "topd", [128, 2 * GS, TOPK])
                m.rest = sb(phase, "rest", [128, 2 * GS, KEYS])
                m.cand = sb(phase, "cand", [128, GS, 54])
                m.cand2 = sb(phase, "cand2", [128, GS, 54])
                m.v16 = sb(phase, "v16", [128, GS, TOPK])
                m.e16 = sb(phase, "e16", [128, GS, TOPK])
                m.floor = sb(phase, "floor", [128, GS])
                m.efloor = sb(phase, "efloor", [128, GS])
                m.sum16 = sb(phase, "sum16", [128, GS])
                m.factor = sb(phase, "factor", [128, GS])
                m.factorT = sb(phase, "factorT", [128, 2, TOK])
                m.high = sb(phase, "high", [128, 2, TOK], F16)
                m.low = sb(phase, "low", [128, 2, TOK], F16)
                m.shift = sb(phase, "shift", [128, 2])
                m.exps = sb(phase, "exps", [128, 3, TOK])
                m.wts = sb(phase, "wts", [128, 3, TOK])
                m.kvT = sb(phase, "kvT", [128, TOK])
                m.vals = sb(phase, "vals", [128, GS, F])
                m.msk = sb(phase, "msk", [128, TOK])
                m.probs3 = sb(phase, "probs3", [128, TOK])
                m.probsT = sb(phase, "probsT", [128, TOK])
                m.mixT = sb(phase, "mixT", [F, TOK])
                m.amax = sb(phase, "amax", [128, GS])
                m.asum = sb(phase, "asum", [128, GS])
                m.arec = sb(phase, "arec", [128, GS])
                m.outw = sb(phase, "outw", [128, GS, F])
                loaded = sem("selectors_loaded")
                with nc.Block() as block:
                    @block.sync
                    def _(sp):
                        sp.dma_start(m.sel[:], sel).then_inc(loaded, 16)
                        sp.wait_ge(loaded, 16)

                    @block.vector
                    def _(v):
                        v.memset(m.shift[:, 0:1], -SHIFT)
                        v.memset(m.shift[:, 1:2], SHIFT)
                lay = Memory3(m, groups, heads)
                first_front(nc, m, lay)
                nc.all_engine_barrier(sems_to_clear=used())
                with nc.Fori(0, heads * groups // 2) as j:
                    two_units(nc, m, lay, j)
                    nc.all_engine_barrier(sems_to_clear=used())
                last_back(nc, m, lay)

        stored = sem("stored")
        with nc.Block() as block:
            @block.sync
            def _(sp):
                n = groups * GS
                sp.dma_start(out[0:n].rearrange("b t f -> t b f"), m.h_all[:, 0:n * F].rearrange("t (b f) -> t b f", f=F)).then_inc(stored, 16)
                sp.wait_ge(stored, 16)


def kernel(**inputs):
    import concourse.bacc as bacc
    from concourse.bass_utils import run_bass_kernel_spmd

    arrays = lay_out({k: np.asarray(v) for k, v in inputs.items()})
    nc = bacc.Bacc("TRN2", target_bir_lowering=False, num_devices=1)
    args = {k: nc.dram_tensor(k + "_dram", a.shape, mybir.dt.from_np(a.dtype), kind="ExternalInput").ap() for k, a in arrays.items()}
    out = nc.dram_tensor("out_dram", (SEQS, T, F), F32, kind="ExternalOutput").ap()
    audio_tower(nc, **args, out=out)
    r = run_bass_kernel_spmd(nc, [{k + "_dram": a for k, a in arrays.items()}], core_ids=[0])
    return r.results[0]["out_dram"]
```

```python
from contextlib import ExitStack

import numpy as np

import concourse.bass as bass
from concourse import mybir

ALU = mybir.AluOpType
ACT = mybir.ActivationFunctionType
AX = mybir.AxisListType
F32 = mybir.dt.float32
F16 = mybir.dt.float16

SEQS, T_IN, F = 32, 256, 64
T = T_IN // 2
TAPS = 5
GS = 4
GROUPS = SEQS // GS
TOK = GS * T
FB = F + 1
EXPERTS = 8
H2, D2 = 8, 32
NODES = 255
TREE_DEPTH = 7
RUN = 4
QUARTERS = 4
QUARTER = 2 ** (TREE_DEPTH - 2) // QUARTERS
WPIECE = 4 * QUARTER
HEADS = 8
KEYS = 64
TOPK = 16
CHUNKS = KEYS * KEYS // 128
DK = 32
PART = KEYS // 2
MIXES = ((0, 0), (1, 1), (0, 1), (1, 0))
SELECTORS = CHUNKS // len(MIXES)
UNITS = GROUPS
PLACES = 4
LAG = 3
BANKS = 8
LOWEST = -3.0e38
PIECE = 8
SHIFT = 40.0
EXP_ZERO = -87.3
WSCALE = 64.0
GSCALE = 8.0
SCORE_MIN = -30000.0
LN_EPS = 1e-5
TOK_EPS = 1e-3


def pack_columns():
    return {
        "ident": (128, 128), "mean128": (128, 128), "off_diag": (128, 128), "upper": (128, 128),
        "causal": (128, 128),
        "tok_w": (128, TAPS * F), "tok_b": (128, F), "tok_gamma": (128, F), "tok_beta": (128, F),
        "tok_alpha": (128, F),
        "wa": (F, F), "wb": (F, F), "wu": (FB, F), "wr": (F, F),
        "m0_router": (FB, EXPERTS), "m0_b1": (128, EXPERTS // 2), "m0_w2": (128, EXPERTS * F),
        "m0_b2": (EXPERTS, F),
        "a1_w": (F, F),
        "m1_gamma": (128, F), "m1_beta": (128, F),
        "m1_router": (FB, EXPERTS), "m1_b1": (128, EXPERTS), "m1_w2": (128, EXPERTS * F),
        "m1_b2": (EXPERTS, F),
        "a2_gamma": (128, F), "a2_beta": (128, F),
        "a2_wg": (FB, H2 * D2), "a2_wf": (128, 2 * F), "a2_bf": (128, F),
        "tree_w1": (FB, NODES + 1), "tree_b2": (128, 2 * F),
    }


def split_columns():
    return {"a2_wq": H2 * D2, "a2_wk": H2 * D2, "a2_wv": H2 * D2, "m0_w1": EXPERTS * F, "m1_w1": EXPERTS * 128, "a3_q": HEADS * 2 * F, "a3_e": HEADS * F}


def lay_out(inp):
    f = np.float32
    rows = lambda v: np.broadcast_to(np.asarray(v).reshape(1, -1), (128, np.asarray(v).size))
    below = lambda w, b: np.concatenate([w, np.asarray(b).reshape(1, -1)], 0)
    zero = lambda n: np.zeros((1, n), f)
    r = np.arange(128)
    d = {"ident": np.eye(128, dtype=f), "mean128": np.full((128, 128), 1 / 128, f),
         "off_diag": (1 - np.eye(128, dtype=f)) / f(T),
         "upper": (r[:, None] <= r[None, :]).astype(f),
         "causal": np.where(r[:, None] >= r[None, :], f(0), f(LOWEST)).astype(f)}
    d["tok_w"] = rows(inp["L0_tok_w"][:, 0, :])
    for k in ("b", "gamma", "beta", "alpha"):
        d["tok_" + k] = rows(inp["L0_tok_" + k])
    d["wa"], d["wb"], d["wr"] = inp["L0_attn_W_alpha"].T, inp["L0_attn_W_beta"].T, inp["L0_attn_W_r"].T
    d["wu"] = below(inp["L0_attn_W_unary"].T, inp["L0_attn_b_unary"])
    d["m0_router"] = np.concatenate([inp["L0_ffn_router_w"].T, zero(EXPERTS)], 0)
    d["m0_b1"] = inp["L0_ffn_b1"].reshape(EXPERTS // 2, 128).T
    w2 = np.zeros((2, F, EXPERTS // 2, 2, F), f)
    for e in range(EXPERTS):
        w2[e % 2, :, e // 2, e % 2, :] = inp["L0_ffn_w2"][e]
    d["m0_w2"] = w2.reshape(128, EXPERTS * F)
    d["m0_b2"] = inp["L0_ffn_b2"]
    d["a1_w"] = inp["L1_attn_W"]
    d["m1_gamma"], d["m1_beta"] = rows(inp["L1_ffn_gamma"]), rows(inp["L1_ffn_beta"])
    d["m1_router"] = below(inp["L1_ffn_Wr"], inp["L1_ffn_br"])
    d["m1_b1"] = inp["L1_ffn_b1"].reshape(EXPERTS, 128).T
    d["m1_w2"] = inp["L1_ffn_W2"].transpose(1, 0, 2).reshape(128, -1)
    d["m1_b2"] = inp["L1_ffn_b2"]
    d["a2_gamma"], d["a2_beta"] = rows(inp["L2_attn_ln_gamma"]), rows(inp["L2_attn_ln_beta"])
    d["a2_wg"] = below(inp["L2_attn_W_gate"].T, inp["L2_attn_b_gate"])
    d["a2_wf"] = inp["L2_attn_W_final"].T.reshape(2, 128, F).transpose(1, 0, 2).reshape(128, -1)
    d["a2_bf"] = rows(inp["L2_attn_b_final"])
    d["tree_w1"] = np.concatenate([below(inp["L2_ffn_w1s"].T, inp["L2_ffn_b1s"]), np.zeros((FB, 1), f)], 1)
    b2 = np.concatenate([inp["L2_ffn_b2s"], zero(F)], 0)
    d["tree_b2"] = b2.reshape(2, 128, F).transpose(1, 0, 2).reshape(128, 2 * F)
    queries = inp["L3_attn_Q"].transpose(1, 0, 2)
    qkv = inp["L2_attn_W_qkv"].T
    wide = {"a2_wq": qkv[:, :256], "a2_wk": qkv[:, 256:512], "a2_wv": qkv[:, 512:],
            "m0_w1": inp["L0_ffn_w1"].transpose(1, 0, 2), "m1_w1": inp["L1_ffn_W1"].transpose(1, 0, 2),
            "a3_q": np.stack([queries, queries], 2), "a3_e": inp["L3_attn_E"].transpose(2, 0, 1)}
    wide = np.concatenate([wide[name].reshape(F, n) for name, n in split_columns().items()], 1)
    wide = np.concatenate([wide, wide], 0)
    cols = pack_columns()
    pack = np.zeros((128, sum(c for _, c in cols.values())), f)
    at = 0
    for name, (nr, nc_) in cols.items():
        assert d[name].shape == (nr, nc_), (name, d[name].shape)
        pack[:nr, at:at + nc_] = d[name]
        at += nc_

    x = np.concatenate([np.zeros((SEQS, 1, F), f), inp["x"], np.zeros((SEQS, 2, F), f)], 1)
    win = np.stack([x[:, k:k + 2 * T:2, :] for k in range(TAPS)], 2)
    win = win.reshape(GROUPS, GS, T, TAPS * F).transpose(0, 2, 1, 3)
    def node(level, place):
        at = 0
        for bit in range(level):
            at = 2 * at + 1 + (place >> bit & 1)
        return at

    last = 2 ** (TREE_DEPTH - 1)
    order = [node(level, j) for level in range(TREE_DEPTH) for j in range(2 ** level)] + [NODES]
    for q in range(QUARTERS):
        for leaf in (0, last):
            for side in (0, last // 2):
                order += [node(TREE_DEPTH, q * QUARTER + j + side + leaf) for j in range(QUARTER)]
    w2s = np.concatenate([inp["L2_ffn_w2s"], np.zeros((1, F, F), f)], 0)
    tree_w2 = w2s[order].transpose(1, 0, 2)
    head = np.zeros((HEADS + 1, 128, 320), f)
    wq_pk = inp["L3_ffn_Wq_pk"].reshape(F, 2, HEADS, DK)
    for h in range(HEADS):
        for half in range(2):
            head[h, half * F:(half + 1) * F, 0:64] = wq_pk[:, :, h, :].reshape(F, 64)
            head[h, half * F:(half + 1) * F, 64:128] = inp["L3_ffn_Wq"][:, h * F:(h + 1) * F]
        for p in range(2):
            head[h, p * DK:(p + 1) * DK, 128 + p * KEYS:128 + (p + 1) * KEYS] = inp["L3_ffn_pk_keys"][p, :, h, :].T
        head[h, 0:F, 256:320] = inp["L3_ffn_Wo"][h * F:(h + 1) * F, :]
    table = np.concatenate([inp["L3_ffn_values_table"], inp["L3_ffn_keys_table"]], 1)
    table = table.reshape(HEADS, KEYS, KEYS, 2 * F)
    chunks = []
    for c in range(CHUNKS):
        (part0, part1), e = MIXES[c // SELECTORS], c % SELECTORS
        chunks.append(table[:, part1 * PART + 4 * e:part1 * PART + 4 * e + 4, part0 * PART:(part0 + 1) * PART])
    table = np.stack(chunks, 1).reshape(HEADS, CHUNKS, 128, 2 * F).transpose(0, 2, 1, 3).reshape(HEADS, 128, -1)
    sel = np.zeros((2, 2, PART, SELECTORS, 4, PART), np.float16)
    for e in range(SELECTORS):
        for j in range(4):
            sel[:, 0, :, e, j, :] = np.eye(PART)
            sel[:, 1, 4 * e + j, e, j, :] = 1
    sel = sel.reshape(128, SELECTORS * 128)
    arrays = {"pack": pack, "win": win.reshape(GROUPS, T, GS * TAPS * F), "tree_w2": tree_w2, "head": head,
              "table": table, "sel": sel, "wide": wide}
    return {k: np.ascontiguousarray(v) for k, v in arrays.items()}


class Memory:
    pass


def spread(ap, axis, n):
    ap = ap.unsqueeze(axis)
    shape = list(ap.shape)
    shape[axis] = n
    return ap.to_broadcast(shape)


def chain_of(eng, sem):
    count = [0]

    def link(ins):
        count[0] += 1
        ins.then_inc(sem, 1)
        eng.wait_ge(sem, count[0])
    return link


class Norm:

    def __init__(self, m, name, src, dst, turned, bank=0, eps=LN_EPS, split=False):
        self.m, self.src, self.dst, self.turned, self.bank, self.eps = m, src, dst, turned, bank, eps
        self.var, self.std = m.sem(f"{name}_var"), m.sem(f"{name}_std")
        if split:
            self.high, self.low = m.sem(f"{name}_high"), m.sem(f"{name}_low")
        if turned is not None:
            self.normed, self.inps, self.ready = (m.sem(f"{name}_{x}") for x in ("normed", "turned_in_psum", "turned"))

    def dve_normalize(self, v, link):
        m = self.m
        for b in range(GS):
            last = v.bn_stats(m.stats[:, b, :], self.src[:, b, :])
        link(last)
        for b in range(GS):
            last = v.bn_aggr(m.moments[:, b, :], m.stats[:, b, :])
        link(last)
        v.tensor_scalar(m.var[:], m.moments[:, :, 1], self.eps, None, ALU.add).then_inc(self.var, 1)
        v.wait_ge(self.std, 1)
        link(v.reciprocal(m.rstd[:], m.std[:]))
        for b in range(GS):
            last = v.tensor_scalar(self.dst[:, b, :], self.src[:, b, :], m.moments[:, b, 0:1],
                                   m.rstd[:, b:b + 1], ALU.subtract, ALU.mult)
        return last

    def act_root(self, a):
        a.wait_ge(self.var, 1)
        a.activation(self.m.std[:], self.m.var[:], ACT.Sqrt).then_inc(self.std, 1)

    def pe_turn(self, pe):
        pe.wait_ge(self.normed, 1)
        for b in range(GS):
            last = pe.transpose(self.m.ps[0:F, self.bank, b * T:(b + 1) * T], self.dst[:, b, :], self.m.w["ident"])
        last.then_inc(self.inps, 1)

    def pe_turn_twice(self, pe):
        pe.wait_ge(self.normed, 1)
        for b in range(GS):
            for half in range(2):
                last = pe.matmul(self.m.ps[half * F:(half + 1) * F, self.bank, b * T:(b + 1) * T], self.dst[:, b, :],
                                 self.m.w["ident"], start=True, stop=True)
        last.then_inc(self.inps, 1)

    def act_high(self, a):
        a.wait_ge(self.inps, 1)
        a.copy(self.m.split, self.m.ps[:, self.bank, :]).then_inc(self.high, 1)

    def dve_low(self, v):
        v.wait_ge(self.high, 1)
        low = self.m.split[F:128, :]
        v.tensor_tensor(low, self.m.ps[F:128, self.bank, :], low, ALU.subtract).then_inc(self.low, 1)

    def act_copy(self, a):
        a.wait_ge(self.inps, 1)
        a.copy(self.turned[0:F, :], self.m.ps[0:F, self.bank, :]).then_inc(self.ready, 1)


def layer0_tokens(nc, m, g):
    parts, sums, var, std, own = (m.sem("tok_" + x) for x in (
        "partial_moments", "moments_in_psum", "var", "std", "dve"))
    with nc.Block() as block:
        @block.vector
        def _(v):
            link = chain_of(v, own)
            v.wait_ge(m.window_loaded, 16)
            v.sem_clear(m.window_loaded)
            link(v.tensor_tensor(m.window[:], m.window[:], spread(m.w["tok_w"], 1, GS), ALU.mult))
            link(v.tensor_reduce(m.n[:], m.window[:].rearrange("p b (k f) -> p b f k", k=TAPS), AX.X, ALU.add))
            link(v.tensor_tensor(m.n[:], m.n[:], spread(m.w["tok_b"], 1, GS), ALU.add))
            for b in range(GS):
                last = v.bn_stats(m.stats[:, b, :], m.n[:, b, :])
            link(last)
            for b in range(GS):
                last = v.bn_aggr(m.moments[:, b, :], m.stats[:, b, :])
            link(last)
            link(v.tensor_copy(m.small[:, 0:GS], m.moments[:, :, 0]))
            link(v.tensor_tensor(m.small[:, GS:2 * GS], m.small[:, 0:GS], m.small[:, 0:GS], ALU.mult))
            v.tensor_tensor(m.small[:, GS:2 * GS], m.small[:, GS:2 * GS], m.moments[:, :, 1], ALU.add).then_inc(parts, 1)
            v.wait_ge(sums, 1)
            link(v.tensor_copy(m.small[:, 0:2 * GS], m.ps[:, 0, 0:2 * GS]))
            link(v.tensor_tensor(m.small[:, 2 * GS:3 * GS], m.small[:, 0:GS], m.small[:, 0:GS], ALU.mult))
            link(v.tensor_tensor(m.var[:], m.small[:, GS:2 * GS], m.small[:, 2 * GS:3 * GS], ALU.subtract))
            v.tensor_scalar(m.var[:], m.var[:], TOK_EPS, None, ALU.add).then_inc(var, 1)
            v.wait_ge(std, 1)
            link(v.reciprocal(m.rstd[:], m.std[:]))
            for b in range(GS):
                last = v.tensor_scalar(m.n[:, b, :], m.n[:, b, :], m.small[:, b:b + 1], m.rstd[:, b:b + 1],
                                       ALU.subtract, ALU.mult)
            link(last)
            link(v.tensor_tensor(m.n[:], m.n[:], spread(m.w["tok_gamma"], 1, GS), ALU.mult))
            link(v.tensor_tensor(m.n[:], m.n[:], spread(m.w["tok_beta"], 1, GS), ALU.add))
            link(v.scalar_tensor_tensor(m.n2[:], m.n[:], 0.0, spread(m.w["tok_alpha"], 1, GS), ALU.min, ALU.mult))
            link(v.scalar_tensor_tensor(m.h[:], m.n[:], 0.0, m.n2[:], ALU.max, ALU.add))

        @block.tensor
        def _(pe):
            pe.wait_ge(parts, 1)
            pe.matmul(m.ps[:, 0, 0:2 * GS], m.w["mean128"], m.small[:, 0:2 * GS], start=True, stop=True).then_inc(sums, 1)

        @block.scalar
        def _(a):
            a.wait_ge(var, 1)
            a.activation(m.std[:], m.var[:], ACT.Sqrt).then_inc(std, 1)


def layer0_attention(nc, m, g):
    norm = Norm(m, "l0a", m.h, m.n, m.nT)
    proj, copied, ucopied, scored, masked, mixed, mixed_sb, out, own = (m.sem("l0a_" + x) for x in (
        "projected", "a_and_b_copied", "u_copied", "scores", "scores_masked", "mixed", "mixed_copied", "out", "dve"))
    aT, bT = m.big[0:F, 0, :], m.big[0:F, 1, :]
    un, sT, mixT = m.big[:, 2, 0:GS * F], m.big[:, 3, :], m.big[0:F, 4, :]
    with nc.Block() as block:
        @block.tensor
        def _(pe):
            norm.pe_turn(pe)
            pe.wait_ge(norm.ready, 1)
            pe.matmul(m.ps[0:F, 1, :], m.w["wa"], m.nT[0:F, :], start=True, stop=True).then_inc(proj, 1)
            pe.matmul(m.ps[0:F, 2, :], m.w["wb"], m.nT[0:F, :], start=True, stop=True).then_inc(proj, 1)
            for b in range(GS):
                last = pe.matmul(m.ps[:, 3, b * F:(b + 1) * F], m.nT[:, b * T:(b + 1) * T], m.w["wu"], start=True, stop=True)
            last.then_inc(proj, 1)
            pe.wait_ge(copied, 2)
            for b in range(GS):
                at = slice(b * T, (b + 1) * T)
                last = pe.matmul(m.ps[:, 4, at], bT[:, at], aT[:, at], start=True, stop=True)
            last.then_inc(scored, 1)
            pe.wait_ge(masked, 1)
            pe.wait_ge(ucopied, 1)
            for b in range(GS):
                at = slice(b * T, (b + 1) * T)
                last = pe.matmul(m.ps[0:F, 5, at], un[:, b * F:(b + 1) * F], sT[:, at], start=True, stop=True)
            last.then_inc(mixed, 1)
            pe.wait_ge(mixed_sb, 1)
            for b in range(GS):
                last = pe.matmul(m.ps[:, 6, b * F:(b + 1) * F], mixT[:, b * T:(b + 1) * T], m.w["wr"], start=True, stop=True)
            last.then_inc(out, 1)

        @block.scalar
        def _(a):
            norm.act_root(a)
            norm.act_copy(a)
            a.wait_ge(proj, 1)
            a.copy(aT, m.ps[0:F, 1, :]).then_inc(copied, 1)
            a.wait_ge(proj, 2)
            a.copy(bT, m.ps[0:F, 2, :]).then_inc(copied, 1)
            a.wait_ge(mixed, 1)
            a.copy(mixT, m.ps[0:F, 5, :]).then_inc(mixed_sb, 1)

        @block.vector
        def _(v):
            link = chain_of(v, own)
            norm.dve_normalize(v, link).then_inc(norm.normed, 1)
            v.wait_ge(proj, 3)
            v.tensor_copy(un, m.ps[:, 3, 0:GS * F]).then_inc(ucopied, 1)
            v.wait_ge(scored, 1)
            v.tensor_tensor(sT.rearrange("p (b t) -> p b t", b=GS), m.ps[:, 4, :].rearrange("p (b t) -> p b t", b=GS),
                            spread(m.w["off_diag"], 1, GS), ALU.mult).then_inc(masked, 1)
            v.wait_ge(norm.normed, 1)
            link(v.tensor_tensor(m.h[:], m.h[:], m.n[:], ALU.add))
            v.wait_ge(out, 1)
            link(v.tensor_tensor(m.h[:], m.h[:], m.ps[:, 6, 0:GS * F].rearrange("p (b f) -> p b f", b=GS), ALU.add))


def mixture(nc, m, which):
    name = f"l{which}m"
    units = (4, 8)[which]
    norm = Norm(m, name, m.h, m.n, m.nT, bank=0, split=True)
    if which:
        norm.src, norm.dst = m.n, m.n2
        first = Norm(m, name + "_first", m.h, m.n, None)
    logits, shifted, exped, hidden, acted, out, weighed, wturned, wcopied, biased, own = (m.sem(f"{name}_{x}") for x in (
        "logits", "logits_shifted", "exp", "hidden", "gelu", "expert_outputs", "expert_weights", "weights_turned",
        "weights_copied", "biases", "dve"))
    w1 = m.wide16[f"m{which}_w1"]
    b1, w2, b2 = (m.w[f"m{which}_{x}"] for x in ("b1", "w2", "b2"))
    lg, mx, wt, tmp = (m.gate[:, i] for i in range(4))
    act = m.big
    with nc.Block() as block:
        @block.tensor
        def _(pe):
            norm.pe_turn_twice(pe)
            pe.wait_ge(norm.ready, 1)
            for b in range(GS):
                last = pe.matmul(m.ps[:, 1, b * EXPERTS:(b + 1) * EXPERTS], m.nT[:, b * T:(b + 1) * T],
                                 m.w[f"m{which}_router"], start=True, stop=True)
            last.then_inc(logits, 1)
            pe.wait_ge(norm.low, 1)
            wide = EXPERTS * F // units

            def hidden_units(u):
                for part in range(2):
                    last = pe.matmul(m.ps[:, 2 + u % 2, :], w1[:, part, u * 128:(u + 1) * 128], m.split,
                                     start=part == 0, stop=part == 1)
                last.then_inc(hidden, 1)

            hidden_units(0)
            hidden_units(1)
            for u in range(units):
                pe.wait_ge(acted, u + 1)
                if u + 2 < units:
                    hidden_units(u + 2)
                if u == 2:
                    pe.wait_ge(weighed, 1)
                    for b in range(GS):
                        last = pe.transpose(m.ps[0:EXPERTS, 0, b * T:(b + 1) * T], wt[:, b, :], m.w["ident"])
                    last.then_inc(wturned, 1)
                half, at = divmod(u * wide, 4 * F)
                for b in range(GS):
                    last = pe.matmul(m.ps[:, 4 + 2 * half + b // 2, (b % 2) * 4 * F + at:(b % 2) * 4 * F + at + wide],
                                     act[:, u, b * T:(b + 1) * T], w2[:, u * wide:(u + 1) * wide], start=True, stop=True)
                    if at + wide == 4 * F and b % 2:
                        last.then_inc(out, 1)
            pe.wait_ge(wcopied, 1)
            for b in range(GS):
                last = pe.matmul(m.ps[:, 1, b * F:(b + 1) * F], m.nT[0:EXPERTS, b * T:(b + 1) * T], b2, start=True, stop=True)
            last.then_inc(biased, 1)

        @block.scalar
        def _(a):
            if which:
                first.act_root(a)
            norm.act_root(a)
            norm.act_copy(a)
            norm.act_high(a)
            a.wait_ge(shifted, 1)
            a.activation(tmp, tmp, ACT.Exp).then_inc(exped, 1)
            for u in range(units):
                a.wait_ge(hidden, u + 1)
                a.activation(act[:, u, :], m.ps[:, 2 + u % 2, :], ACT.Gelu, bias=b1[:, u:u + 1],
                             scale=1.0 / WSCALE).then_inc(acted, 1)
            a.wait_ge(wturned, 1)
            a.copy(m.nT[0:EXPERTS, :], m.ps[0:EXPERTS, 0, :]).then_inc(wcopied, 1)

        @block.vector
        def _(v):
            link = chain_of(v, own)
            if which:
                link(first.dve_normalize(v, link))
                link(norm.dve_normalize(v, link))
                link(v.tensor_tensor(m.n2[:], m.n2[:], spread(m.w["m1_gamma"], 1, GS), ALU.mult))
                v.tensor_tensor(m.n2[:], m.n2[:], spread(m.w["m1_beta"], 1, GS), ALU.add).then_inc(norm.normed, 1)
            else:
                norm.dve_normalize(v, link).then_inc(norm.normed, 1)
                v.wait_ge(norm.normed, 1)
                link(v.tensor_tensor(m.h[:], m.h[:], m.n[:], ALU.add))
            norm.dve_low(v)
            v.wait_ge(logits, 1)
            link(v.tensor_copy(lg, m.ps[:, 1, 0:GS * EXPERTS].rearrange("p (b e) -> p b e", b=GS)))
            for b in range(GS):
                last = v.max(mx[:, b, :], lg[:, b, :])
            link(last)
            v.tensor_tensor(tmp, lg, mx[:, :, 0:1].to_broadcast([128, GS, EXPERTS]), ALU.subtract).then_inc(shifted, 1)
            link(v.tensor_tensor(wt, lg, mx[:, :, 1:2].to_broadcast([128, GS, EXPERTS]), ALU.is_ge))
            v.wait_ge(exped, 1)
            link(v.tensor_tensor(wt, wt, tmp, ALU.mult))
            link(v.tensor_reduce(m.small[:, 0:GS], wt, AX.X, ALU.add))
            link(v.reciprocal(m.small[:, 0:GS], m.small[:, 0:GS]))
            v.tensor_tensor(wt, wt, spread(m.small[:, 0:GS], 2, EXPERTS), ALU.mult).then_inc(weighed, 1)
            v.wait_ge(weighed, 1)
            for i in range(4):
                half, pair = divmod(i, 2)
                seqs, experts = slice(2 * pair, 2 * pair + 2), slice(4 * half, 4 * half + 4)
                v.wait_ge(out, i + 1)
                weighted = m.wide[:, pair, :]
                link(v.tensor_tensor(weighted.rearrange("p (b e f) -> p b e f", b=2, e=4),
                                     m.ps[:, 4 + i, :].rearrange("p (b e f) -> p b e f", b=2, e=4),
                                     spread(wt[:, seqs, experts], 3, F), ALU.mult))
                link(v.tensor_reduce((m.n2, m.n)[half][:, seqs, :], weighted.rearrange("p (b e f) -> p b f e", b=2, e=4),
                                     AX.X, ALU.add))
                if i == 1:
                    link(v.tensor_tensor(m.h[:], m.h[:], m.n2[:], ALU.add))
            link(v.tensor_tensor(m.h[:], m.h[:], m.n[:], ALU.add))
            v.wait_ge(biased, 1)
            link(v.tensor_tensor(m.h[:], m.h[:], m.ps[:, 1, 0:GS * F].rearrange("p (b f) -> p b f", b=GS), ALU.add))


def layer0_mixture(nc, m, g):
    mixture(nc, m, 0)


def layer1_mixture(nc, m, g):
    mixture(nc, m, 1)


def layer1_attention(nc, m, g):
    norm = Norm(m, "l1a", m.h, m.n, m.nT)
    proj, copied, scored, maxed, exped, turned, turned_sb, out, own = (m.sem("l1a_" + x) for x in (
        "projected", "projection_copied", "scores", "max", "exp", "probs_turned", "probs_copied", "out", "dve"))
    xT, p, pT = m.big[0:F, 0, :], m.big[:, 1, :], m.big[:, 2, :]
    mx, total = m.small[:, 0:GS], m.small[:, GS:2 * GS]
    scale = F ** -0.5
    with nc.Block() as block:
        @block.tensor
        def _(pe):
            norm.pe_turn(pe)
            pe.wait_ge(norm.ready, 1)
            pe.matmul(m.ps[0:F, 1, :], m.w["a1_w"], m.nT[0:F, :], start=True, stop=True).then_inc(proj, 1)
            pe.wait_ge(copied, 1)
            for b in range(GS):
                at = slice(b * T, (b + 1) * T)
                last = pe.matmul(m.ps[:, 2, at], xT[:, at], m.nT[0:F, at], start=True, stop=True)
            last.then_inc(scored, 1)
            for b in range(GS):
                at = slice(b * T, (b + 1) * T)
                pe.wait_ge(exped, b + 1)
                last = pe.transpose(m.ps[:, 3, at], p[:, at], m.w["ident"])
            last.then_inc(turned, 1)
            pe.wait_ge(turned_sb, 1)
            for b in range(GS):
                last = pe.matmul(m.ps[:, 4, b * F:(b + 1) * F], pT[:, b * T:(b + 1) * T], m.n[:, b, :], start=True, stop=True)
            last.then_inc(out, 1)

        @block.scalar
        def _(a):
            norm.act_root(a)
            norm.act_copy(a)
            a.wait_ge(proj, 1)
            a.copy(xT, m.ps[0:F, 1, :]).then_inc(copied, 1)
            a.wait_ge(maxed, 1)
            for b in range(GS):
                at = slice(b * T, (b + 1) * T)
                a.activation(p[:, at], m.ps[:, 2, at], ACT.Exp, bias=mx[:, b:b + 1], scale=scale,
                             accum_out=total[:, b:b + 1]).then_inc(exped, 1)
            a.wait_ge(turned, 1)
            a.copy(pT, m.ps[:, 3, :]).then_inc(turned_sb, 1)

        @block.vector
        def _(v):
            link = chain_of(v, own)
            norm.dve_normalize(v, link).then_inc(norm.normed, 1)
            v.wait_ge(scored, 1)
            link(v.tensor_reduce(mx, m.ps[:, 2, :].rearrange("p (b t) -> p b t", b=GS), AX.X, ALU.max))
            v.tensor_scalar(mx, mx, -scale, None, ALU.mult).then_inc(maxed, 1)
            v.wait_ge(exped, GS)
            link(v.reciprocal(m.rstd[:], total))
            v.wait_ge(out, 1)
            for b in range(GS):
                last = v.scalar_tensor_tensor(m.h[:, b, :], m.ps[:, 4, b * F:(b + 1) * F], m.rstd[:, b:b + 1],
                                              m.h[:, b, :], ALU.mult, ALU.add)
            link(last)


def layer2_attention(nc, m, g):
    norm = Norm(m, "l2a", m.h, m.n, m.nT, bank=0)
    norm2 = Norm(m, "l2a_own", m.n, m.n2, m.split, bank=1, split=True)
    proj, qcopied, kcopied, vcopied, gated, scored, maxed, exped, vready, mixed, ogated, out, own = (m.sem("l2a_" + x) for x in (
        "projected", "queries_copied", "keys_copied", "values_copied", "gate_tanh", "scores", "max", "exp", "values_scaled", "mixed", "gated",
        "out", "dve"))
    qT, kT, gT, og = m.big[:, 0:2, :], m.big[:, 2:4, :], m.big[:, 4:6, :], m.big[:, 6:8, :]
    scale = D2 ** -0.5
    pr = m.probs
    mx, total, rinv = (m.small[:, 16 * i:16 * (i + 1)] for i in range(3))
    with nc.Block() as block:
        @block.tensor
        def _(pe):
            norm.pe_turn(pe)
            pe.wait_ge(norm.ready, 1)
            for s in range(2):
                last = pe.matmul(m.ps[:, 4 + s, :], m.w["a2_wg"][:, s * 128:(s + 1) * 128], m.nT[:], start=True, stop=True)
            last.then_inc(proj, 1)
            norm2.pe_turn_twice(pe)
            pe.wait_ge(norm2.low, 1)
            for first_bank, name in ((0, "a2_wq"), (2, "a2_wk")):
                for s in range(2):
                    for part in range(2):
                        last = pe.matmul(m.ps[:, first_bank + s, :], m.wide16[name][:, part, s * 128:(s + 1) * 128], m.split,
                                         start=part == 0, stop=part == 1)
                last.then_inc(proj, 1)
            for b in range(GS):
                for part in range(2):
                    last = pe.matmul(m.ps[:, 6 + b // 2, (b % 2) * 256:(b % 2 + 1) * 256], m.split[:, b * T:(b + 1) * T],
                                     m.wide16["a2_wv"][:, part, :], start=part == 0, stop=part == 1)
            last.then_inc(proj, 1)
            pe.wait_ge(qcopied, 1)
            pe.wait_ge(kcopied, 1)
            for pair in range(2):
                if pair:
                    pe.wait_ge(gated, 1)
                    pe.wait_ge(vcopied, 1)
                for r in range(4):
                    rows = slice(32 * r, 32 * r + 32)
                    for b in range(2):
                        at = slice((2 * pair + b) * T, (2 * pair + b + 1) * T)
                        for s in range(2):
                            last = pe.matmul(m.ps[:, 4 * pair + r, (2 * b + s) * T:(2 * b + s + 1) * T],
                                             qT[rows, s, at], kT[rows, s, at], start=True, stop=True)
                    last.then_inc(scored, 1)
            for pair in range(2):
                pe.wait_ge(exped, 16 * (pair + 1))
                pe.wait_ge(vready, pair + 1)
                for b in range(2):
                    bb = 2 * pair + b
                    for s in range(2):
                        for r in range(4):
                            col = (4 * s + r) * D2
                            last = pe.matmul(m.ps[32 * r:32 * r + 32, s, bb * T:(bb + 1) * T],
                                             m.values[:, bb, col:col + D2], pr[:, pair, r, b, s, :], start=True, stop=True)
                last.then_inc(mixed, 1)
            pe.wait_ge(ogated, 2)
            for b in range(GS):
                for s in range(2):
                    last = pe.matmul(m.ps[:, 2, b * F:(b + 1) * F], og[:, s, b * T:(b + 1) * T],
                                     m.w["a2_wf"][:, s * F:(s + 1) * F], start=s == 0, stop=s == 1)
            last.then_inc(out, 1)

        @block.scalar
        def _(a):
            norm.act_root(a)
            norm.act_copy(a)
            norm2.act_root(a)
            norm2.act_high(a)
            a.wait_ge(proj, 1)
            a.activation(gT, m.ps[:, 4:6, :], ACT.Tanh, scale=0.5).then_inc(gated, 1)
            a.wait_ge(proj, 2)
            a.activation(qT, m.ps[:, 0:2, :], ACT.Copy, scale=1.0 / WSCALE).then_inc(qcopied, 1)
            for pair in range(2):
                for i in range(16):
                    r, b, s = i // 4, i // 2 % 2, i % 2
                    if i % 4 == 0:
                        a.wait_ge(maxed, 4 * pair + r + 1)
                    a.activation(pr[:, pair, r, b, s, :], m.ps[:, 4 * pair + r, (i % 4) * T:(i % 4 + 1) * T], ACT.Exp,
                                 bias=m.l2max[:, pair, i:i + 1], scale=scale,
                                 accum_out=m.l2sum[:, pair, i:i + 1]).then_inc(exped, 1)

        @block.vector
        def _(v):
            link = chain_of(v, own)
            norm.dve_normalize(v, link).then_inc(norm.normed, 1)
            v.wait_ge(norm.normed, 1)
            link(norm2.dve_normalize(v, link))
            link(v.tensor_tensor(m.n2[:], m.n2[:], spread(m.w["a2_gamma"], 1, GS), ALU.mult))
            v.tensor_tensor(m.n2[:], m.n2[:], spread(m.w["a2_beta"], 1, GS), ALU.add).then_inc(norm2.normed, 1)
            norm2.dve_low(v)
            link(v.tensor_tensor(m.h[:], m.h[:], m.n[:], ALU.add))
            link(v.tensor_tensor(m.h[:], m.h[:], spread(m.w["a2_bf"], 1, GS), ALU.add))
            v.wait_ge(proj, 3)
            v.tensor_scalar(kT, m.ps[:, 2:4, :], 1.0 / WSCALE, None, ALU.mult).then_inc(kcopied, 1)
            v.wait_ge(proj, 4)
            v.tensor_scalar(m.values.rearrange("p b c -> p (b c)"), m.ps[:, 6:8, :].rearrange("p k c -> p (k c)"),
                            1.0 / WSCALE, None, ALU.mult).then_inc(vcopied, 1)
            v.wait_ge(gated, 1)
            link(v.tensor_scalar(gT, gT, 0.5, 0.5, ALU.mult, ALU.add))
            for pair in range(2):
                for r in range(4):
                    v.wait_ge(scored, 4 * pair + r + 1)
                    mine = m.l2max[:, pair, 4 * r:4 * r + 4]
                    link(v.tensor_reduce(mine, m.ps[:, 4 * pair + r, :].rearrange("p (c t) -> p c t", t=T), AX.X, ALU.max))
                    v.tensor_scalar(mine, mine, -scale, None, ALU.mult).then_inc(maxed, 1)
            v.wait_ge(vcopied, 1)
            for pair in range(2):
                v.wait_ge(exped, 16 * (pair + 1))
                link(v.reciprocal(rinv, m.l2sum[:, pair, :]))
                for b in range(2):
                    vals = m.values[:, 2 * pair + b, :].rearrange("p (s r d) -> p s r d", s=2, r=4)
                    by = rinv.rearrange("p (r b s) -> p b s r", r=4, b=2)[:, b]
                    last = v.tensor_tensor(vals, vals, spread(by, 3, D2), ALU.mult)
                last.then_inc(vready, 1)
                v.wait_ge(vready, pair + 1)
            v.wait_ge(mixed, 2)
            for s in range(2):
                v.tensor_tensor(og[:, s, :], m.ps[:, s, :], gT[:, s, :], ALU.mult).then_inc(ogated, 1)
            v.wait_ge(out, 1)
            link(v.tensor_tensor(m.h[:], m.h[:], m.ps[:, 2, 0:GS * F].rearrange("p (b f) -> p b f", b=GS), ALU.add))


def load_weights(nc, m, pack, wide, tree_w2):
    loaded, wide_loaded, cleared, high, low, ready = (m.sem("weights_" + x) for x in (
        "packed", "wide", "constants", "high", "low", "differences"))
    columns = sum(split_columns().values())
    stage_wide = m.shared[:, 0:columns]
    buffers = 5
    piece_loaded = [m.sem(f"tree_weights_loaded_{i}") for i in range(buffers)]
    stage = m.shared[:, columns:columns + buffers * WPIECE * F].rearrange("p (k n f) -> p k n f", k=buffers, f=F)
    pieces = 2 ** (TREE_DEPTH + 1) // WPIECE

    def load_piece(queue, i, half):
        queue.dma_start(stage[half * F:(half + 1) * F, i % buffers],
                        tree_w2[:, i * WPIECE:(i + 1) * WPIECE, :]).then_inc(piece_loaded[i % buffers], 16)

    with nc.Block() as block:
        @block.sync
        def _(sp):
            sp.dma_start(stage_wide, wide).then_inc(wide_loaded, 16)
            sp.dma_start(m.packed[:], pack).then_inc(loaded, 16)
            for i in range(pieces):
                if i >= buffers:
                    sp.wait_ge(low, i - buffers + 2)
                    load_piece(sp, i, 1)
                load_piece(sp, i, 0)
            sp.wait_ge(low, 1)
            sp.dma_start(m.window.rearrange("p b k -> p (b k)"), m.dram["win"][0]).then_inc(m.window_loaded, 16)

        @block.scalar
        def _(a):
            for i in range(buffers):
                load_piece(a, i, 1)
            a.wait_ge(wide_loaded, 16)
            a.activation(m.wide_weights[:, 0, :], stage_wide, ACT.Copy, scale=WSCALE).then_inc(high, 1)
            for i in range(pieces):
                if i < pieces // 2:
                    a.wait_ge(piece_loaded[i % buffers], 32 * (i // buffers + 1))
                else:
                    a.wait_ge(ready, i - pieces // 2 + 1)
                a.activation(m.tree_w[:, i * WPIECE:(i + 1) * WPIECE, 0:F], stage[:, i % buffers], ACT.Copy,
                             scale=WSCALE).then_inc(high, 1)

        @block.vector
        def _(v):
            v.memset(m.nT[F:FB, :], 1.0).then_inc(cleared, 1)
            v.wait_ge(high, 1)
            v.scalar_tensor_tensor(m.wide_weights[:, 1, :], stage_wide, WSCALE, m.wide_weights[:, 0, :], ALU.mult,
                                   ALU.subtract).then_inc(low, 1)
            v.wait_ge(loaded, 16)
            v.tensor_copy(m.ident16[:], m.w["ident"]).then_inc(cleared, 1)
            v.tensor_tensor(m.halves[:], m.w["ident"][:, 0:F], m.w["ident"][:, F:2 * F], ALU.add).then_inc(cleared, 1)
            for i in range(pieces):
                at = slice(i * WPIECE, (i + 1) * WPIECE)
                if i >= pieces // 2:
                    v.wait_ge(piece_loaded[i % buffers], 32 * (i // buffers + 1))
                    left, right = stage[:, i % buffers, 0:WPIECE // 2], stage[:, i % buffers, WPIECE // 2:WPIECE]
                    v.tensor_tensor(right, right, left, ALU.subtract).then_inc(ready, 1)
                v.wait_ge(high, i + 2)
                v.scalar_tensor_tensor(m.tree_w[:, at, F:2 * F], stage[:, i % buffers], WSCALE, m.tree_w[:, at, 0:F],
                                       ALU.mult, ALU.subtract).then_inc(low, 1)
            v.wait_ge(cleared, 3)
            v.wait_ge(low, pieces + 1)


def growth():
    steps = []
    for level in range(TREE_DEPTH - 2):
        for kind in ("right", "left"):
            for at in range(0, 2 ** level, RUN):
                steps.append((kind, level, at, min(RUN, 2 ** level - at)))
    for q in range(QUARTERS):
        for side in ("right", "left"):
            for at in range(q * QUARTER, (q + 1) * QUARTER, RUN):
                steps.append((side, TREE_DEPTH - 2, at, RUN))
            for at in range(q * QUARTER, (q + 1) * QUARTER, RUN):
                steps.append(("last", side, at, RUN))
    return steps


def layer2_tree(nc, m, g):
    norm = Norm(m, "l2t", m.h, m.n, m.nT)
    scored, absed, compared, acted, doubled, turned2, high, low, gated, gturned, gcopied = (m.sem("l2t_" + x) for x in (
        "scores", "abs", "turns_of_all_nodes", "gelu", "features_twice", "twice_turned", "high", "low", "gates",
        "gates_turned", "gates_copied"))
    bit, bit_spread, bit_copied, sums, gate_spread, gate_copied = (m.sem("l2t_" + x) for x in (
        "level_turns", "level_turns_spread", "level_turns_copied", "level_gates", "level_gates_spread",
        "level_gates_copied"))
    made, level_done, last_used, level_gated, folded, own = (m.sem("l2t_" + x) for x in (
        "paths", "level_products", "leaves_used", "levels_gated", "levels_folded", "dve"))
    right, ind, gate = m.tree[:, 0], m.tree[:, 1], m.tree[:, 2]
    scores = m.ps[:, 0:2, :].rearrange("p k (b n) -> p (k b) n", b=2)
    n2x = m.big[:, 0:1, :].rearrange("p k (b c) -> p (k b) c", b=GS).rearrange("p b (k f) -> p b k f", k=2)
    gT = m.tree[:, 0].rearrange("p b n -> p (b n)").rearrange("p (k t) -> p k t", k=2)
    weighted = m.tree[:, 1].rearrange("p b n -> p (b n)").rearrange("p (k t) -> p k t", k=2)
    gates_of = m.big
    bank = (5, 6, 7, 0, 1, 5, 6, 7)
    levels = TREE_DEPTH + 1
    steps = growth()
    sides = 2 ** (TREE_DEPTH - 2)

    def places(kind, level, at, n):
        if kind == "last":
            parents = (at, at + n) if level == "left" else (sides + at % (2 * QUARTER), sides + at % (2 * QUARTER) + n)
            chunk = [s for s in steps if s[0] == "last"].index((kind, level, at, n)) % 3
            first = sides + 2 * QUARTER + chunk * RUN
            return slice(first, first + n), slice(*parents)
        if kind == "left":
            return slice(at, at + n), slice(at, at + n)
        first = at + 2 ** level if level < TREE_DEPTH - 2 else sides + at % (2 * QUARTER)
        return slice(first, first + n), slice(at, at + n)

    def count(kind, level, at):
        return 1 + next(i for i, s in enumerate(steps) if s[0] == kind and s[1] == level and s[2] <= at < s[2] + s[3])

    with nc.Block() as block:
        @block.tensor
        def _(pe):
            def spread_turns(d):
                pe.wait_ge(bit, d + 1)
                if d >= 2:
                    pe.wait_ge(bit_copied, d - 1)
                for b in range(GS):
                    last = pe.matmul(m.ps[:, 3 + d % 2, b * T:(b + 1) * T], m.turns[:, d, b:b + 1].to_broadcast([128, 128]),
                                     m.ident16[:], start=True, stop=True)
                last.then_inc(bit_spread, 1)

            def spread_gates(d):
                if d == 0:
                    pe.wait_ge(sums, 1)
                    pe.wait_ge(gcopied, 1)
                if d >= 2:
                    pe.wait_ge(gate_copied, d - 1)
                for b in range(GS):
                    for part in range(2):
                        last = pe.matmul(m.ps[:, 3 + d % 2, b * T:(b + 1) * T],
                                         m.gate16[:, part, d, b:b + 1].to_broadcast([128, 128]), m.ident16[:],
                                         start=part == 0, stop=part == 1)
                last.then_inc(gate_spread, 1)

            def node(d, place, path, first, last):
                ins = pe.matmul(m.ps[:, bank[d], :], m.tree_w[:, place, :], m.path[:, path, :], start=first, stop=last)
                return ins

            def level(d, between=None):
                if d >= 5:
                    pe.wait_ge(level_gated, d - 4)
                for j in range(2 ** d):
                    if d and j % RUN == 0 or j == 2 ** d // 2:
                        half = 2 ** d // 2
                        if d:
                            pe.wait_ge(made, count("left", d - 1, j) if j < half else count("right", d - 1, j - half))
                    ins = node(d, 2 ** d - 1 + j, j, j == 0, j == 2 ** d - 1)
                    if j == 2 ** d - 1:
                        ins.then_inc(level_done, 1)
                    if between and j % RUN == RUN - 1:
                        between(j // RUN)

            def fold(d):
                pe.wait_ge(level_gated, d + 1)
                for b in range(GS):
                    last = pe.matmul(m.ps[:, 2, b * F:(b + 1) * F], weighted[:, d % 2, b * T:(b + 1) * T], m.halves[:],
                                     start=False, stop=d == levels - 1 and b == GS - 1)
                last.then_inc(folded, 1)

            def quarter(q, side):
                d = TREE_DEPTH - 1
                first, final = q == 0 and side == "right", q == QUARTERS - 1 and side == "left"
                if first:
                    pe.wait_ge(level_gated, 3)
                for j in range(QUARTER):
                    at = q * QUARTER + j
                    if j % RUN == 0:
                        pe.wait_ge(made, count(side, d - 1, at))
                    place = 2 ** d - 1 + at + (sides if side == "right" else 0)
                    path = at if side == "left" else sides + at % (2 * QUARTER)
                    ins = node(d, place, path, first and j == 0, final and j == QUARTER - 1)
                if final:
                    ins.then_inc(level_done, 1)
                leaf = 2 ** TREE_DEPTH + q * WPIECE + (QUARTER if side == "right" else 0)
                for j in range(QUARTER):
                    at = q * QUARTER + j
                    path = at if side == "left" else sides + at % (2 * QUARTER)
                    node(d + 1, leaf + j, path, first and j == 0, False)
                for j in range(QUARTER):
                    at = q * QUARTER + j
                    if j % RUN == 0:
                        pe.wait_ge(made, count("last", side, at))
                        where, _ = places("last", side, at, RUN)
                    ins = node(d + 1, leaf + WPIECE // 2 + j, where.start + j % RUN, False, final and j == QUARTER - 1)
                    if j % RUN == RUN - 1:
                        ins.then_inc(last_used, 1)

            norm.pe_turn(pe)
            pe.wait_ge(norm.ready, 1)
            for b in range(GS):
                last = pe.matmul(m.ps[:, b // 2, (b % 2) * 256:(b % 2 + 1) * 256], m.nT[:, b * T:(b + 1) * T],
                                 m.w["tree_w1"], start=True, stop=True)
            last.then_inc(scored, 1)
            pe.wait_ge(doubled, 2)
            for b in range(GS):
                last = pe.transpose(m.ps[:, 2, b * T:(b + 1) * T], n2x[:, b].rearrange("p k f -> p (k f)"), m.w["ident"])
            last.then_inc(turned2, 1)
            for d in range(TREE_DEPTH):
                spread_turns(d)
            pe.wait_ge(high, 1)
            pe.wait_ge(low, 1)
            level(0)
            pe.wait_ge(gated, 1)
            pe.wait_ge(bit_copied, TREE_DEPTH)
            for b in range(GS):
                for half in range(2):
                    last = pe.transpose(m.ps[:, 3 + half, b * T:(b + 1) * T], gate[:, b, half * 128:(half + 1) * 128],
                                        m.w["ident"])
            last.then_inc(gturned, 1)
            level(1)
            spread_gates(0)
            level(2)
            spread_gates(1)
            for b in range(GS):
                for half in range(2):
                    pe.matmul(m.ps[:, 2, b * F:(b + 1) * F], gT[:, half, b * T:(b + 1) * T],
                              m.w["tree_b2"][:, half * F:(half + 1) * F], start=b == half == 0, stop=False)
            pe.wait_ge(compared, 1)
            level(3)
            level(4)
            fold(0)
            level(5, between=lambda i: spread_gates(i + 2) if i + 2 < levels else None)
            fold(1)
            fold(2)
            for q in range(QUARTERS):
                quarter(q, "right")
                if q < 2:
                    fold(3 + 2 * q)
                quarter(q, "left")
                if q == 0:
                    fold(4)
            fold(6)
            fold(7)

        @block.scalar
        def _(a):
            norm.act_root(a)
            norm.act_copy(a)
            a.wait_ge(norm.normed, 1)
            for k in range(2):
                a.copy(n2x[:, :, k, :], m.n[:]).then_inc(doubled, 1)
            a.wait_ge(scored, 1)
            a.activation(gate, scores, ACT.Abs).then_inc(absed, 1)
            a.wait_ge(turned2, 1)
            a.copy(m.path[:, 0, :], m.ps[:, 2, :]).then_inc(high, 1)
            a.wait_ge(absed, 1)
            a.activation(gate, gate, ACT.Gelu).then_inc(acted, 1)
            for d in range(TREE_DEPTH):
                a.wait_ge(bit_spread, d + 1)
                a.copy(m.turn[:, d, :], m.ps[:, 3 + d % 2, :]).then_inc(bit_copied, 1)
            a.wait_ge(gturned, 1)
            a.copy(gT, m.ps[:, 3:5, :]).then_inc(gcopied, 1)
            for d in range(levels):
                a.wait_ge(gate_spread, d + 1)
                a.copy(gates_of[:, d, :], m.ps[:, 3 + d % 2, :]).then_inc(gate_copied, 1)

        @block.vector
        def _(v):
            link = chain_of(v, own)

            def grow(which):
                for i, (kind, level, at, n) in enumerate(steps):
                    if not which(kind, level, at):
                        continue
                    out, parents = places(kind, level, at, n)
                    inner = TREE_DEPTH - 2
                    q = at // QUARTER
                    if i == 0:
                        v.wait_ge(low, 1)
                    elif kind == "last":
                        v.wait_ge(made, count(level, inner, at))
                        k = [s for s in steps if s[0] == "last"].index((kind, level, at, n))
                        if k >= 3:
                            v.wait_ge(last_used, k - 2)
                    elif kind == "left":
                        v.wait_ge(made, count("right", level, at))
                        v.wait_ge(level_done, level + 1)
                    else:
                        half = 2 ** level // 2
                        for j in {at, at + n - 1}:
                            v.wait_ge(made, count("left", level - 1, j) if j < half else count("right", level - 1, j - half))
                        if level == inner and q >= 2:
                            v.wait_ge(last_used, (2 * (q - 2) + 1) * QUARTER // RUN)
                            v.wait_ge(made, count("last", "right", at - 2 * QUARTER))
                    turn = TREE_DEPTH - 1 if kind == "last" else level
                    if kind == "left":
                        rights, _ = places("right", level, at, n)
                        ins = v.tensor_tensor(m.path[:, out, :], m.path[:, parents, :], m.path[:, rights, :], ALU.subtract)
                    else:
                        v.wait_ge(bit_copied, turn + 1)
                        ins = v.tensor_tensor(m.path[:, out, :], m.path[:, parents, :], spread(m.turn[:, turn, :], 1, n), ALU.mult)
                    ins.then_inc(made, 1)

            def gate_level(d):
                if d == TREE_DEPTH:
                    v.wait_ge(last_used, 2 * sides // RUN)
                else:
                    v.wait_ge(level_done, d + 1)
                v.wait_ge(gate_copied, d + 1)
                if d >= 2:
                    v.wait_ge(folded, d - 1)
                v.scalar_tensor_tensor(weighted[:, d % 2, :], m.ps[:, bank[d], :], 1.0 / (WSCALE * GSCALE), gates_of[:, d, :],
                                       ALU.mult, ALU.mult).then_inc(level_gated, 1)

            norm.dve_normalize(v, link).then_inc(norm.normed, 1)
            v.wait_ge(absed, 1)
            v.tensor_scalar(right, scores, 0.0, None, ALU.is_gt).then_inc(compared, 1)
            v.wait_ge(compared, 1)
            v.wait_ge(high, 1)
            v.tensor_tensor(m.path[F:128, 0, :], m.ps[F:128, 2, :], m.path[F:128, 0, :], ALU.subtract).then_inc(low, 1)
            link(v.memset(ind[:, :, 0:1], 1.0))
            for d in range(TREE_DEPTH):
                lo, n = 2 ** d - 1, 2 ** d
                kids = ind[:, :, 2 * lo + 1:2 * lo + 1 + 2 * n].rearrange("p b (n k) -> p b n k", k=2)
                link(v.tensor_tensor(kids[:, :, :, 1], ind[:, :, lo:lo + n], right[:, :, lo:lo + n], ALU.mult))
                link(v.tensor_tensor(kids[:, :, :, 0], ind[:, :, lo:lo + n], kids[:, :, :, 1], ALU.subtract))
                v.tensor_reduce(m.turns[:, d, :], kids[:, :, :, 1], AX.X, ALU.max).then_inc(bit, 1)
            grow(lambda kind, level, at: level == 0)
            link(v.memset(ind[:, :, NODES:NODES + 1], 0.0))
            v.wait_ge(acted, 1)
            v.tensor_tensor(gate, gate, ind, ALU.mult).then_inc(gated, 1)
            v.wait_ge(gated, 1)
            for d in range(levels):
                last = v.tensor_reduce(m.level_gate[:, d, :], gate[:, :, 2 ** d - 1:2 ** (d + 1) - 1], AX.X, ALU.add)
            link(last)
            link(v.tensor_scalar(m.level_gate[:], m.level_gate[:], GSCALE, None, ALU.mult))
            link(v.tensor_copy(m.gate16[:, 0], m.level_gate[:]))
            v.tensor_tensor(m.gate16[:, 1], m.level_gate[:], m.gate16[:, 0], ALU.subtract).then_inc(sums, 1)
            grow(lambda kind, level, at: kind != "last" and level in (1, 2, 3) or (kind, level) == ("right", 4))
            gate_level(0)
            gate_level(1)
            grow(lambda kind, level, at: (kind, level) == ("left", 4))
            gate_level(2)
            for q in range(QUARTERS):
                for side in ("right", "left"):
                    grow(lambda kind, level, at: at // QUARTER == q and (kind, level) in ((side, TREE_DEPTH - 2), ("last", side)))
                    if (q, side) in ((0, "right"), (0, "left"), (1, "right")):
                        gate_level(3 + 2 * q + (side == "left"))
            gate_level(6)
            gate_level(7)
            v.wait_ge(folded, levels)
            link(v.tensor_tensor(m.h[:], m.h[:], m.ps[:, 2, 0:GS * F].rearrange("p (b f) -> p b f", b=GS), ALU.add))


def layer3_attention(nc, m, g):
    norm = Norm(m, "l3a", m.h, m.n, m.nT, split=True)
    proj, high, low, evals, ecopied, omega, masked, out, own = (m.sem("l3a_" + x) for x in (
        "queries", "queries_high", "queries_low", "values", "values_copied", "omega", "omega_masked", "out", "dve"))
    qT = m.big[:].rearrange("p k t -> p (k t)").bitcast(F16).rearrange("p (i h t) -> p i h t", i=2, h=HEADS)
    query_bank = lambda h: (1, 2, 4, 5)[h % 4]
    value_bank = lambda b: (3, 0)[b % 2]
    omega_bank = lambda b, half: ((4, 5), (7, 1))[b % 2][half]
    with nc.Block() as block:
        @block.sync
        def _(sp):
            sp.dma_start(m.window.rearrange("p b k -> p (b k)"), m.dram["win"][(g + 1) % m.groups]).then_inc(m.window_loaded, 16)

        @block.tensor
        def _(pe):
            norm.pe_turn_twice(pe)
            pe.wait_ge(norm.low, 1)
            for h in range(HEADS):
                if h >= 4:
                    pe.wait_ge(low, h - 3)
                for part in range(2):
                    last = pe.matmul(m.ps[:, query_bank(h), :], m.wide16["a3_q"][:, part, h * 2 * F:(h + 1) * 2 * F],
                                     m.split, start=part == 0, stop=part == 1)
                last.then_inc(proj, 1)
            pe.wait_ge(low, HEADS)
            for b in range(GS + 1):
                if b < GS:
                    nb = m.split[:, b * T:(b + 1) * T]
                    if b >= 2:
                        pe.wait_ge(ecopied, b - 1)
                    for part in range(2):
                        last = pe.matmul(m.ps[:, value_bank(b), :], nb, m.wide16["a3_e"][:, part, :], start=part == 0,
                                         stop=part == 1)
                    last.then_inc(evals, 1)
                    for half in range(2):
                        if b >= 2:
                            pe.wait_ge(masked, 2 * (b - 2) + half + 1)
                        for part in range(2):
                            last = pe.matmul(m.ps[:, omega_bank(b, half), :], nb,
                                             qT[:, part, 4 * half:4 * half + 4, b * T:(b + 1) * T], start=part == 0,
                                             stop=part == 1)
                        last.then_inc(omega, 1)
                if b:
                    d = b - 1
                    pe.wait_ge(ecopied, d + 1)
                    for half in range(2):
                        pe.wait_ge(masked, 2 * d + half + 1)
                        for k in range(4):
                            h = 4 * half + k
                            last = pe.matmul(m.ps[:, 6, d * F:(d + 1) * F],
                                             m.omega[:, 2 * (d % 2) + half, k * T:(k + 1) * T],
                                             m.evals[:, d % 2, h * F:(h + 1) * F], start=h == 0, stop=h == HEADS - 1)
                    last.then_inc(out, 1)

        @block.scalar
        def _(a):
            norm.act_root(a)
            norm.act_high(a)
            for h in range(HEADS):
                a.wait_ge(proj, h + 1)
                a.activation(qT[:, 0, h, :], m.ps[:, query_bank(h), :], ACT.Copy, scale=1.0 / WSCALE).then_inc(high, 1)
            for b in range(GS):
                a.wait_ge(evals, b + 1)
                if b >= 2:
                    a.wait_ge(out, b - 1)
                a.activation(m.evals[:, b % 2, :], m.ps[:, value_bank(b), :], ACT.Copy, scale=1.0 / WSCALE).then_inc(ecopied, 1)

        @block.vector
        def _(v):
            link = chain_of(v, own)
            norm.dve_normalize(v, link).then_inc(norm.normed, 1)
            norm.dve_low(v)
            for h in range(HEADS):
                v.wait_ge(high, h + 1)
                v.scalar_tensor_tensor(qT[:, 1, h, :], m.ps[:, query_bank(h), :], 1.0 / WSCALE, qT[:, 0, h, :], ALU.mult,
                                       ALU.subtract).then_inc(low, 1)
            for b in range(GS):
                for half in range(2):
                    v.wait_ge(omega, 2 * b + half + 1)
                    if b >= 2:
                        v.wait_ge(out, b - 1)
                    v.tensor_tensor(m.omega[:, 2 * (b % 2) + half, :].rearrange("p (k t) -> p k t", t=T),
                                    m.ps[:, omega_bank(b, half), :].rearrange("p (k t) -> p k t", t=T),
                                    spread(m.w["upper"], 1, 4), ALU.mult).then_inc(masked, 1)
            v.wait_ge(out, GS)
            link(v.tensor_tensor(m.h_all[:, bass.ts(g, GS * F)], m.h[:].rearrange("p b f -> p (b f)"), m.ps[:, 6, 0:GS * F],
                                 ALU.add))


def layer3_input(nc, m, g):
    norm = Norm(m, "l3i", m.h, m.n, m.nT, split=True)
    own = m.sem("l3i_dve")
    mine = m.input_all[:, bass.ts(g, TOK)]
    with nc.Block() as block:
        @block.tensor
        def _(pe):
            norm.pe_turn_twice(pe)

        @block.scalar
        def _(a):
            norm.act_root(a)
            a.wait_ge(norm.inps, 1)
            a.copy(mine, m.ps[:, 0, :]).then_inc(norm.high, 1)

        @block.vector
        def _(v):
            link = chain_of(v, own)
            link(v.tensor_copy(m.h[:].rearrange("p b f -> p (b f)"), m.h_all[:, bass.ts(g, GS * F)]))
            norm.dve_normalize(v, link).then_inc(norm.normed, 1)
            v.wait_ge(norm.high, 1)
            low = m.input_all[F:128, bass.ts(g, TOK)]
            v.tensor_tensor(low, m.ps[F:128, 0, :], low, ALU.subtract).then_inc(norm.low, 1)
            v.wait_ge(norm.low, 1)


LAYERS = [layer0_tokens, layer0_attention, layer0_mixture, layer1_attention, layer1_mixture,
          layer2_attention, layer2_tree, layer3_attention]


def stairs():
    return [(0, 1, 16), (1, 1, 8), (2, 2, 5), (4, 4, 3), (8, 8, 1)]


class Memory3:

    NAMES = ("weights_loaded", "weights_scaled", "weights_high", "weights_split", "input", "query_in_psum", "query", "scores_in_psum", "scores", "best16",
             "exp16", "factor", "scores_shifted", "scores_turned", "factor_spread", "high", "low", "mixes", "factor_copied",
             "sum", "exp", "weights", "product", "kv", "kv_turned", "values", "masked", "attn_max", "attn_exp",
             "probs_turned", "probs_copied", "mixed", "mixed_copied", "out", "out_added", "dve", "output_weights")

    def __init__(self, m, groups, heads):
        self.m, self.groups, self.heads = m, groups, heads
        self.s = {n: m.sem("pk_" + n) for n in self.NAMES}
        self.links = 0

    def pe_queries(self, pe, k):
        m, s = self.m, self.s
        pe.wait_ge(s["weights_split"], k)
        pe.wait_ge(s["input"], k)
        if k > 1:
            pe.wait_ge(s["low"], 2 * (k - 1))
        for part in range(2):
            last = pe.matmul(m.ps[:, 6, :], m.front16[:, part, :], m.x[:], start=part == 0, stop=part == 1)
        last.then_inc(s["query_in_psum"], 1)

    def pe_scores(self, pe, k, place):
        m, s = self.m, self.s
        pe.wait_ge(s["query"], k)
        pe.wait_ge(s["weights_loaded"], 16 * k)
        for b in range(GS):
            last = pe.matmul(m.ps[:, 6, b * 128:(b + 1) * 128], m.queries[0:F, place, b * T:(b + 1) * T],
                             m.front[0:F, 128:256], start=True, stop=True)
        last.then_inc(s["scores_in_psum"], 1)

    def pe_turn_scores(self, pe, k, part):
        m, s = self.m, self.s
        pe.wait_ge(s["scores_shifted"], k)
        if part:
            pe.wait_ge(s["low"], 2 * k - 1)
        elif m.backs:
            pe.wait_ge(s["values"], k)
        for b in range(GS):
            last = pe.transpose(m.ps[:, 6, b * T:(b + 1) * T], m.twice[:, part, b, :], m.w["ident"])
        last.then_inc(s["scores_turned"], 1)

    def pe_spread_factor(self, pe, k):
        m, s = self.m, self.s
        pe.wait_ge(s["factor"], k)
        if m.backs:
            pe.wait_ge(s["out_added"], k)
        for b in range(GS):
            at = slice(b * T, (b + 1) * T)
            last = pe.matmul(m.ps[:, 7, at], m.factor[:, b:b + 1].to_broadcast([128, 128]), m.w["ident"],
                             start=True, stop=True)
        last.then_inc(s["factor_spread"], 1)

    def pe_sum(self, pe, u, c):
        m, s = self.m, self.s
        n = u * CHUNKS + c
        if n >= 4:
            pe.wait_ge(s["weights"], n - 3)
        if u and c in (0, SELECTORS):
            pe.wait_ge(s["low"], 2 * u - 1 + c // SELECTORS)
        if u and c in (2 * SELECTORS, 3 * SELECTORS):
            pe.wait_ge(s["mixes"], 2 * u - 3 + c // SELECTORS)
        e = c % SELECTORS
        pe.matmul(m.ps[:, c % 4, :], m.sel[:, e * 128:(e + 1) * 128], m.mixes[:, u % 2, c // SELECTORS, :], start=True,
                  stop=True).then_inc(s["sum"], 1)

    def pe_product(self, pe, u, c):
        m, s = self.m, self.s
        if u == 0 and c % PIECE == 0:
            loaded = m.table_loaded[c // PIECE]
            pe.wait_ge(loaded, 16)
            pe.sem_clear(loaded)
        pe.wait_ge(s["weights"], u * CHUNKS + c + 1)
        if u and c == 0:
            pe.wait_ge(s["kv"], u)
        pe.matmul(m.ps[:, 4 + u % 2, :], m.table[:, c * 128:(c + 1) * 128], m.wts[:, (u * CHUNKS + c) % 4, :],
                  start=c == 0, stop=c == CHUNKS - 1).then_inc(s["product"], 1)

    def pe_attention_scores(self, pe, k, q):
        m, s = self.m, self.s
        pe.wait_ge(s["kv"], k)
        if m.fronts:
            pe.wait_ge(s["scores"], k)
            if k > 1:
                pe.wait_ge(s["factor_copied"], k - 1)
        for b in range(GS):
            at = slice(b * T, (b + 1) * T)
            pe.transpose(m.ps[:, 6, at], m.kvT[:, at], m.w["ident"])
            last = pe.matmul(m.ps[:, 7, at], m.queries[F:128, q, at], m.kvT[F:128, at], start=True, stop=True)
        last.then_inc(s["kv_turned"], 1)

    def pe_turn_probs(self, pe, k):
        m, s = self.m, self.s
        pe.wait_ge(s["attn_exp"], GS * k)
        for b in range(GS):
            at = slice(b * T, (b + 1) * T)
            last = pe.transpose(m.ps[:, 7, at], m.probs3[:, at], m.w["ident"])
        last.then_inc(s["probs_turned"], 1)

    def pe_mix(self, pe, k):
        m, s = self.m, self.s
        pe.wait_ge(s["probs_copied"], k)
        for b in range(GS):
            at = slice(b * T, (b + 1) * T)
            last = pe.matmul(m.ps[0:F, 7, at], m.vals[:, b, :], m.probsT[:, at], start=True, stop=True)
        last.then_inc(s["mixed"], 1)

    def pe_out(self, pe, k, q):
        m, s = self.m, self.s
        pe.wait_ge(s["mixed_copied"], k)
        if k > 1:
            pe.wait_ge(s["output_weights"], 16 * (k - 1))
        for b in range(GS):
            last = pe.matmul(m.ps[:, 7, b * F:(b + 1) * F], m.mixT[:, b * T:(b + 1) * T], m.wo[:, q, :],
                             start=True, stop=True)
        last.then_inc(s["out"], 1)

    def act_queries(self, a, k, place):
        m, s = self.m, self.s
        a.wait_ge(s["query_in_psum"], k)
        a.activation(m.queries[:, place, :], m.ps[:, 6, :], ACT.Copy, scale=1.0 / WSCALE).then_inc(s["query"], 1)

    def act_scores(self, a, k):
        m, s = self.m, self.s
        a.wait_ge(s["scores_in_psum"], k)
        a.copy(m.sc[:], m.ps[:, 6, :]).then_inc(s["scores"], 1)

    def act_exp16(self, a, k):
        m, s = self.m, self.s
        a.wait_ge(s["best16"], k)
        a.activation(m.e16[:], m.v16[:], ACT.Exp)
        a.activation(m.efloor[:], m.floor[:], ACT.Exp, bias=m.shift[:, 1:2]).then_inc(s["exp16"], 1)

    def act_high(self, a, k, q, part):
        m, s = self.m, self.s
        a.wait_ge(s["scores_turned"], 2 * k - 1 + part)
        a.copy(m.mixes[:, q, part, :], m.ps[:, 6, :]).then_inc(s["high"], 1)

    def act_factor(self, a, k, q):
        m, s = self.m, self.s
        a.wait_ge(s["factor_spread"], k)
        a.copy(m.factorT[:, q, :], m.ps[:, 7, :]).then_inc(s["factor_copied"], 1)

    def act_exp(self, a, u, c):
        m, s = self.m, self.s
        n = u * CHUNKS + c
        a.wait_ge(s["sum"], n + 1)
        if n >= 4:
            a.wait_ge(s["weights"], n - 3)
        a.activation(m.exps[:, n % 4, :], m.ps[:, c % 4, :], ACT.Exp, bias=m.shift[:, 0:1]).then_inc(s["exp"], 1)

    def act_attention(self, a, k):
        m, s = self.m, self.s
        a.wait_ge(s["attn_max"], k)
        for b in range(GS):
            at = slice(b * T, (b + 1) * T)
            a.activation(m.probs3[:, at], m.msk[:, at], ACT.Exp, bias=m.amax[:, b:b + 1], scale=F ** -0.5,
                         accum_out=m.asum[:, b:b + 1]).then_inc(s["attn_exp"], 1)

    def act_probs(self, a, k):
        m, s = self.m, self.s
        a.wait_ge(s["probs_turned"], k)
        a.copy(m.probsT[:], m.ps[:, 7, :]).then_inc(s["probs_copied"], 1)

    def act_mixed(self, a, k):
        m, s = self.m, self.s
        a.wait_ge(s["mixed"], k)
        a.copy(m.mixT[:], m.ps[0:F, 7, :]).then_inc(s["mixed_copied"], 1)

    def pool_front(self, pool, k, group):
        m, s = self.m, self.s
        if k > 1:
            pool.wait_ge(s["query_in_psum"], k - 1)
        pool.tensor_copy(m.x[:], m.input_all[:, bass.ts(group, TOK)]).then_inc(s["input"], 1)
        pool.wait_ge(s["weights_loaded"], 16 * k)
        pool.tensor_scalar(m.scaled[:], m.front[:, 0:128], WSCALE, None, ALU.mult).then_inc(s["weights_scaled"], 1)
        pool.wait_ge(s["weights_scaled"], k)
        pool.tensor_copy(m.front16[:, 0, :], m.scaled[:]).then_inc(s["weights_high"], 1)
        pool.wait_ge(s["weights_high"], k)
        pool.tensor_tensor(m.front16[:, 1, :], m.scaled[:], m.front16[:, 0, :], ALU.subtract).then_inc(s["weights_split"], 1)

    def link(self, v, ins):
        self.links += 1
        ins.then_inc(self.s["dve"], 1)
        v.wait_ge(self.s["dve"], self.links)

    def dve_weights(self, v, u, c):
        m, s = self.m, self.s
        n = u * CHUNKS + c
        v.wait_ge(s["exp"], n + 1)
        if n >= 4:
            v.wait_ge(s["product"], n - 3)
        v.scalar_tensor_tensor(m.wts[:, n % 4, :], m.ps[:, c % 4, :], 0.0, m.exps[:, n % 4, :], ALU.is_ge,
                               ALU.mult).then_inc(s["weights"], 1)

    def scores_by_half(self):
        return self.m.sc[:].rearrange("p (i k) -> p i k", k=KEYS)

    def dve_first8(self, v, k, half):
        m, s = self.m, self.s
        v.wait_ge(s["scores"], k)
        for i in range(half * GS, (half + 1) * GS):
            last = v.max(m.top[:, i, 0:8], self.scores_by_half()[:, i, :])
        self.link(v, last)

    def dve_strike8(self, v, half):
        m = self.m
        for i in range(half * GS, (half + 1) * GS):
            last = v.match_replace(out=m.rest[:, i, :], in_to_replace=m.top[:, i, 0:8],
                                   in_values=self.scores_by_half()[:, i, :], imm_value=LOWEST)
        self.link(v, last)

    def dve_second8(self, v, half):
        m = self.m
        for i in range(half * GS, (half + 1) * GS):
            last = v.max(m.top[:, i, 8:16], m.rest[:, i, :])
        self.link(v, last)

    def dve_candidates(self, v):
        m = self.m
        self.link(v, v.tensor_tensor(m.topd[:], m.top[:], m.top[:, :, 0:1].to_broadcast([128, 2 * GS, TOPK]), ALU.subtract))
        pairs = m.topd[:].rearrange("p (b s) r -> p b s r", s=2)
        at = 0
        for a0, na, nb in stairs():
            last = v.tensor_tensor(m.cand[:, :, at:at + na * nb].rearrange("p b (x y) -> p b x y", x=na),
                                   spread(pairs[:, :, 0, a0:a0 + na], 3, nb), spread(pairs[:, :, 1, 0:nb], 2, na), ALU.add)
            at += na * nb
        self.link(v, last)

    def dve_best16(self, v, part):
        m = self.m
        for b in range(GS):
            if part == 0:
                last = v.max(m.v16[:, b, 0:8], m.cand[:, b, :])
            elif part == 1:
                last = v.match_replace(out=m.cand2[:, b, :], in_to_replace=m.v16[:, b, 0:8], in_values=m.cand[:, b, :],
                                       imm_value=LOWEST)
            else:
                last = v.max(m.v16[:, b, 8:16], m.cand2[:, b, :])
        self.link(v, last)

    def dve_floor(self, v, k):
        m, s = self.m, self.s
        self.link(v, v.tensor_scalar(m.floor[:], m.v16[:, :, TOPK - 1], 1.0 + 2.0 ** -19, -2.0 ** -22, ALU.mult, ALU.add))
        v.tensor_scalar(m.floor[:], m.floor[:], EXP_ZERO, None, ALU.max).then_inc(s["best16"], 1)
        v.wait_ge(s["best16"], k)

    def dve_less_largest(self, v):
        byhalf = self.scores_by_half()
        top = self.m.top[:, :, 0:1].to_broadcast([128, 2 * GS, KEYS])
        self.link(v, v.tensor_tensor(byhalf, byhalf, top, ALU.subtract))

    def dve_less_threshold(self, v):
        m = self.m
        second = m.sc[:].rearrange("p (b s k) -> p b s k", s=2, k=KEYS)[:, :, 1, :]
        self.link(v, v.tensor_tensor(second, second, spread(m.floor[:], 2, KEYS), ALU.subtract))

    def dve_scores_twice(self, v):
        m, s = self.m, self.s
        scores = m.sc[:].rearrange("p (b s k) -> p b s k", s=2, k=KEYS)
        for part in range(2):
            for twice in range(2):
                out = m.twice[:, part, :, twice * KEYS:(twice + 1) * KEYS].rearrange("p b (s i) -> p b s i", s=2)
                last = v.tensor_scalar(out, scores[:, :, :, part * PART:(part + 1) * PART], SCORE_MIN, None, ALU.max)
        last.then_inc(s["scores_shifted"], 1)

    def dve_factor(self, v, k):
        m, s = self.m, self.s
        v.wait_ge(s["exp16"], k)
        self.link(v, v.tensor_reduce(m.sum16[:], m.e16[:], AX.X, ALU.add))
        self.link(v, v.reciprocal(m.sum16[:], m.sum16[:]))
        v.tensor_tensor(m.factor[:], m.sum16[:], m.efloor[:], ALU.mult).then_inc(s["factor"], 1)

    def dve_low(self, v, k, q, part):
        m, s = self.m, self.s
        v.wait_ge(s["high"], 2 * k - 1 + part)
        low = m.mixes[2 * PART:128, q, part, :]
        v.tensor_tensor(low, m.ps[2 * PART:128, 6, :], low, ALU.subtract).then_inc(s["low"], 1)

    def dve_mixes(self, v, k, q, mix):
        m, s = self.m, self.s
        v.wait_ge(s["low"], 2 * k)
        for row in range(4):
            rows = slice(row * PART, (row + 1) * PART)
            last = v.tensor_copy(m.mixes[rows, q, mix, :], m.mixes[rows, q, MIXES[mix][row % 2], :])
        last.then_inc(s["mixes"], 1)

    def dve_kv(self, v, k, q):
        m, s = self.m, self.s
        if k > 1:
            v.wait_ge(s["product"], CHUNKS * (k - 1))
            v.wait_ge(s["factor_copied"], k - 1)
        v.tensor_tensor(m.kvT[:], m.ps[:, 4 + q, :], m.factorT[:, q, :], ALU.mult).then_inc(s["kv"], 1)

    def dve_values(self, v, k):
        m, s = self.m, self.s
        v.wait_ge(s["kv_turned"], k)
        v.tensor_copy(m.vals[:], m.ps[:, 6, :].rearrange("p (b c) -> p b c", b=GS)[:, :, 0:F]).then_inc(s["values"], 1)
        v.tensor_tensor(m.msk[:].rearrange("p (b t) -> p b t", b=GS), m.ps[:, 7, :].rearrange("p (b t) -> p b t", b=GS),
                        spread(m.w["causal"], 1, GS), ALU.add).then_inc(s["masked"], 1)

    def dve_attention_max(self, v, k):
        m, s = self.m, self.s
        v.wait_ge(s["masked"], k)
        self.link(v, v.tensor_reduce(m.amax[:], m.msk[:].rearrange("p (b t) -> p b t", b=GS), AX.X, ALU.max))
        v.tensor_scalar(m.amax[:], m.amax[:], -F ** -0.5, None, ALU.mult).then_inc(s["attn_max"], 1)

    def dve_out(self, v, k, group):
        m, s = self.m, self.s
        v.wait_ge(s["attn_exp"], GS * k)
        self.link(v, v.reciprocal(m.arec[:], m.asum[:]))
        v.wait_ge(s["out"], k)
        v.tensor_tensor(m.outw[:], m.ps[:, 7, 0:GS * F].rearrange("p (b f) -> p b f", b=GS),
                        spread(m.arec[:], 2, F), ALU.mult).then_inc(s["out_added"], 1)
        v.wait_ge(s["out_added"], k)
        state = m.h_all[:, bass.ts(group, GS * F)]
        self.link(v, v.tensor_tensor(state, state, m.outw[:].rearrange("p b f -> p (b f)"), ALU.add))


def first_front(nc, m, lay):
    m.fronts, m.backs = True, False
    lay.links = 0
    s = lay.s
    with nc.Block() as block:
        @block.sync
        def _(sp):
            sp.dma_start(m.front[:], m.dram["head"][0, :, 0:256]).then_inc(s["weights_loaded"], 16)
            sp.wait_ge(s["weights_loaded"], 16)
            for i in range(CHUNKS // PIECE):
                at = slice(i * PIECE * 128, (i + 1) * PIECE * 128)
                sp.dma_start(m.table[:, at], m.dram["table"][0, :, at]).then_inc(m.table_loaded[i], 16)

        @block.gpsimd
        def _(pool):
            lay.pool_front(pool, 1, 0)

        @block.tensor
        def _(pe):
            lay.pe_queries(pe, 1)
            lay.pe_scores(pe, 1, 0)
            lay.pe_turn_scores(pe, 1, 0)
            lay.pe_spread_factor(pe, 1)
            lay.pe_turn_scores(pe, 1, 1)

        @block.scalar
        def _(a):
            lay.act_queries(a, 1, 0)
            lay.act_scores(a, 1)
            lay.act_exp16(a, 1)
            lay.act_high(a, 1, 0, 0)
            lay.act_factor(a, 1, 0)
            lay.act_high(a, 1, 0, 1)

        @block.vector
        def _(v):
            v.memset(m.ps[:, 5, :], 0.0)
            v.memset(m.factorT[:, 1, :], 0.0)
            v.memset(m.queries[:, PLACES - 1, :], 0.0)
            v.memset(m.wo[:, 1, :], 0.0)
            for half in range(2):
                lay.dve_first8(v, 1, half)
                lay.dve_strike8(v, half)
                lay.dve_second8(v, half)
            lay.dve_candidates(v)
            for part in range(3):
                lay.dve_best16(v, part)
            lay.dve_floor(v, 1)
            lay.dve_less_largest(v)
            lay.dve_less_threshold(v)
            lay.dve_scores_twice(v)
            lay.dve_factor(v, 1)
            lay.dve_low(v, 1, 0, 0)
            lay.dve_low(v, 1, 0, 1)
            for mix in (2, 3):
                lay.dve_mixes(v, 1, 0, mix)


def some_units(nc, m, lay, j):
    m.fronts, m.backs = True, True
    lay.links = 0
    s = lay.s
    groups, heads = lay.groups, lay.heads
    with nc.Block() as block:
        @block.sync
        def _(sp):
            for u in range(UNITS):
                k = u + 1
                if k > 1:
                    sp.wait_ge(s["scores_in_psum"], k - 1)
                    sp.wait_ge(s["weights_split"], k - 1)
                sp.dma_start(m.front[:], m.dram["head"][(j * UNITS + k) // groups, :, 0:256]).then_inc(s["weights_loaded"], 16)
                if k > 1:
                    sp.wait_ge(s["out"], k - 1)
                    sp.wait_ge(s["output_weights"], 16 * (k - 1))
                sp.dma_start(m.wo[:, u % 2, :], m.dram["head"][(j * UNITS + u) // groups, 0:F, 256:320]).then_inc(s["output_weights"], 16)
            for i in range(CHUNKS // PIECE):
                at = slice(i * PIECE * 128, (i + 1) * PIECE * 128)
                sp.wait_ge(s["product"], (UNITS - 1) * CHUNKS + (i + 1) * PIECE)
                sp.dma_start(m.table[:, at], m.dram["table"][(j * UNITS + UNITS) // groups % heads, :, at]).then_inc(m.table_loaded[i], 16)

        @block.tensor
        def _(pe):
            for u in range(UNITS):
                k, other = u + 1, (u + 1) % 2
                for c in range(CHUNKS):
                    lay.pe_sum(pe, u, c)
                    if c >= LAG:
                        lay.pe_product(pe, u, c - LAG)
                    elif u:
                        lay.pe_product(pe, u - 1, CHUNKS - LAG + c)
                    if c == 3:
                        lay.pe_queries(pe, k)
                    if c == 4:
                        lay.pe_scores(pe, k, k % PLACES)
                    if c == 6:
                        lay.pe_attention_scores(pe, k, (u + PLACES - 1) % PLACES)
                    if c == 12:
                        lay.pe_turn_probs(pe, k)
                    if c == 15:
                        lay.pe_mix(pe, k)
                    if c == 18:
                        lay.pe_out(pe, k, other)
                    if c in (25, 28):
                        lay.pe_turn_scores(pe, k, int(c == 28))
                    if c == 26:
                        lay.pe_spread_factor(pe, k)
            for c in range(CHUNKS - LAG, CHUNKS):
                lay.pe_product(pe, UNITS - 1, c)
            pe.wait_ge(s["output_weights"], 16 * UNITS)

        @block.scalar
        def _(a):
            for u in range(UNITS):
                k, other = u + 1, (u + 1) % 2
                for c in range(CHUNKS):
                    lay.act_exp(a, u, c)
                    if c == 3:
                        lay.act_queries(a, k, k % PLACES)
                    if c == 5:
                        lay.act_scores(a, k)
                    if c == 9:
                        lay.act_attention(a, k)
                    if c == 13:
                        lay.act_probs(a, k)
                    if c == 16:
                        lay.act_mixed(a, k)
                    if c == 19:
                        lay.act_exp16(a, k)
                    if c in (26, 29):
                        lay.act_high(a, k, other, int(c == 29))
                    if c == 27:
                        lay.act_factor(a, k, other)

        @block.gpsimd
        def _(pool):
            for u in range(UNITS):
                lay.pool_front(pool, u + 1, (j * UNITS + u + 1) % groups)

        @block.vector
        def _(v):
            for u in range(UNITS):
                k, other = u + 1, (u + 1) % 2
                for c in range(CHUNKS):
                    lay.dve_weights(v, u, c)
                    if c == 3:
                        lay.dve_kv(v, k, other)
                    if c == 7:
                        lay.dve_values(v, k)
                    if c == 8:
                        lay.dve_attention_max(v, k)
                    if c in (6, 9):
                        lay.dve_first8(v, k, int(c == 9))
                    if c in (10, 11):
                        lay.dve_strike8(v, c - 10)
                    if c in (12, 13):
                        lay.dve_second8(v, c - 12)
                    if c == 14:
                        lay.dve_candidates(v)
                    if c in (15, 16, 17):
                        lay.dve_best16(v, c - 15)
                    if c == 18:
                        lay.dve_floor(v, k)
                    if c == 19:
                        lay.dve_less_largest(v)
                    if c == 20:
                        lay.dve_less_threshold(v)
                    if c == 21:
                        lay.dve_out(v, k, (j * UNITS + (u + groups - 1)) % groups)
                    if c == 22:
                        lay.dve_scores_twice(v)
                    if c == 23:
                        lay.dve_factor(v, k)
                    if c in (27, 30):
                        lay.dve_low(v, k, other, int(c == 30))
                    if c == 31:
                        for mix in (2, 3):
                            lay.dve_mixes(v, k, other, mix)


def last_back(nc, m, lay):
    m.fronts, m.backs = False, True
    lay.links = 0
    with nc.Block() as block:
        @block.sync
        def _(sp):
            for loaded in m.table_loaded:
                sp.wait_ge(loaded, 16)

        @block.tensor
        def _(pe):
            lay.pe_attention_scores(pe, 1, PLACES - 1)
            lay.pe_turn_probs(pe, 1)
            pe.wait_ge(lay.s["values"], 1)
            lay.pe_mix(pe, 1)
            lay.pe_out(pe, 1, 1)

        @block.scalar
        def _(a):
            lay.act_attention(a, 1)
            lay.act_probs(a, 1)
            lay.act_mixed(a, 1)

        @block.vector
        def _(v):
            lay.dve_kv(v, 1, 1)
            lay.dve_values(v, 1)
            lay.dve_attention_max(v, 1)
            lay.dve_out(v, 1, lay.groups - 1)


def audio_tower(nc, win, pack, tree_w2, head, table, sel, wide, out, layers=LAYERS, last=True, groups=GROUPS, heads=HEADS):
    with ExitStack() as ctx:
        m = Memory()
        sems = {}

        def sem(name):
            if name not in sems:
                sems[name] = sems_of.enter_context(nc.semaphore(name))
            return sems[name]

        def sb(where, name, shape, dtype=F32):
            return where.enter_context(nc.sbuf_tensor(name, shape, dtype))

        def used():
            nums = [x.num for x in sems.values()]
            assert max(nums) - min(nums) + 1 == len(nums)
            return range(min(nums), max(nums) + 1)

        m.table_loaded = [ctx.enter_context(nc.semaphore(f"table_piece_{i}_loaded")) for i in range(CHUNKS // PIECE)]
        m.window_loaded = ctx.enter_context(nc.semaphore("window_loaded"))
        m.groups = groups
        m.sem = sem
        m.dram = {"win": win, "table": table, "head": head}
        m.ps = ctx.enter_context(nc.psum_tensor("ps", [128, BANKS, 512], F32))
        m.h_all = sb(ctx, "h_all", [128, SEQS * F])
        m.big = sb(ctx, "big", [128, 8, TOK])
        m.h = sb(ctx, "h", [128, GS, F])
        m.n = sb(ctx, "n", [128, GS, F])
        m.nT = sb(ctx, "nT", [FB, TOK])
        m.stats = sb(ctx, "stats", [128, GS, 6])
        m.moments = sb(ctx, "moments", [128, GS, 2])
        m.var = sb(ctx, "var", [128, GS])
        m.std = sb(ctx, "std", [128, GS])
        m.rstd = sb(ctx, "rstd", [128, GS])
        cols = pack_columns()
        m.packed = sb(ctx, "packed", [128, sum(c for _, c in cols.values())])
        m.w, at = {}, 0
        for name, (nr, n) in cols.items():
            m.w[name] = m.packed[0:nr, at:at + n]
            at += n

        with ExitStack() as phase:
            sems_of = phase
            m.n2 = sb(phase, "n2", [128, GS, F])
            m.small = sb(phase, "small", [128, 64])
            m.gate = sb(phase, "gate", [128, 4, GS, EXPERTS])
            m.l2max = sb(phase, "l2max", [128, 2, 16])
            m.l2sum = sb(phase, "l2sum", [128, 2, 16])
            m.tree = sb(phase, "tree", [128, 3, GS, NODES + 1])
            by_bank = m.tree[:].rearrange("p i b n -> p (i b n)").rearrange("p (k c) -> p k c", c=512)
            m.wide, m.omega, m.evals = by_bank[:, 0:2], by_bank[:, 0:4], by_bank[:, 4:6]
            m.tree_w = sb(phase, "tree_w", [128, 2 ** (TREE_DEPTH + 1), 2 * F], F16)
            m.wide_weights = sb(phase, "wide_weights", [128, 2, sum(split_columns().values())], F16)
            m.wide16, at = {}, 0
            for name, n in split_columns().items():
                m.wide16[name] = m.wide_weights[:, :, at:at + n]
                at += n
            m.ident16 = sb(phase, "ident16", [128, 128], F16)
            m.halves = sb(phase, "halves", [128, F])
            m.turns = sb(phase, "turns", [128, TREE_DEPTH, GS], F16)
            m.turn = sb(phase, "turn", [128, TREE_DEPTH, TOK], F16)
            m.split = m.turn[:, 2, :]
            m.gate16 = sb(phase, "gate16", [128, 2, TREE_DEPTH + 1, GS], F16)
            m.level_gate = sb(phase, "level_gate", [128, TREE_DEPTH + 1, GS])
            paths = 6 * QUARTER + 3 * RUN
            m.path = sb(phase, "path", [128, paths, TOK], F16)
            m.shared = m.path[:].rearrange("p n t -> p (n t)").bitcast(F32)
            m.window = m.shared[:, 0:GS * TAPS * F].rearrange("p (b k) -> p b k", b=GS)
            m.probs = m.shared[:, 0:4096].rearrange("p (q r b s t) -> p q r b s t", q=2, r=4, b=2, s=2)
            m.values = m.shared[:, 4096:4096 + GS * H2 * D2].rearrange("p (b c) -> p b c", b=GS)

            load_weights(nc, m, pack, wide, tree_w2)

            with nc.Fori(0, groups) as g:
                for layer in layers:
                    layer(nc, m, g)
                nc.all_engine_barrier(sems_to_clear=used())

            with nc.Block() as block:
                @block.sync
                def _(sp):
                    sp.wait_ge(m.window_loaded, 16)

        if last:
            sems.clear()
            with ExitStack() as phase:
                sems_of = phase
                m.input_all = sb(phase, "input_all", [128, SEQS * T], F16)
                m.table = sb(phase, "table", [128, CHUNKS * 2 * F])
                m.front = sb(phase, "front", [128, 256])
                m.scaled = sb(phase, "scaled", [128, 128])
                m.front16 = sb(phase, "front16", [128, 2, 128], F16)
                m.wo = sb(phase, "wo", [F, 2, F])
                m.sel = sb(phase, "sel", [128, SELECTORS * 128], F16)
                m.x = sb(phase, "x", [128, TOK], F16)
                m.queries = sb(phase, "queries", [128, PLACES, TOK])
                m.sc = sb(phase, "sc", [128, TOK])
                m.twice = sb(phase, "twice", [128, 2, GS, 128])
                m.top = sb(phase, "top", [128, 2 * GS, TOPK])
                m.topd = sb(phase, "topd", [128, 2 * GS, TOPK])
                m.rest = sb(phase, "rest", [128, 2 * GS, KEYS])
                m.cand = sb(phase, "cand", [128, GS, 54])
                m.cand2 = sb(phase, "cand2", [128, GS, 54])
                m.v16 = sb(phase, "v16", [128, GS, TOPK])
                m.e16 = sb(phase, "e16", [128, GS, TOPK])
                m.floor = sb(phase, "floor", [128, GS])
                m.efloor = sb(phase, "efloor", [128, GS])
                m.sum16 = sb(phase, "sum16", [128, GS])
                m.factor = sb(phase, "factor", [128, GS])
                m.factorT = sb(phase, "factorT", [128, 2, TOK])
                m.mixes = sb(phase, "mixes", [128, 2, len(MIXES), TOK], F16)
                m.shift = sb(phase, "shift", [128, 2])
                m.exps = sb(phase, "exps", [128, 4, TOK])
                m.wts = sb(phase, "wts", [128, 4, TOK])
                m.kvT = sb(phase, "kvT", [128, TOK])
                m.vals = sb(phase, "vals", [128, GS, F])
                m.msk = sb(phase, "msk", [128, TOK])
                m.probs3 = sb(phase, "probs3", [128, TOK])
                m.probsT = sb(phase, "probsT", [128, TOK])
                m.mixT = sb(phase, "mixT", [F, TOK])
                m.amax = sb(phase, "amax", [128, GS])
                m.asum = sb(phase, "asum", [128, GS])
                m.arec = sb(phase, "arec", [128, GS])
                m.outw = sb(phase, "outw", [128, GS, F])
                loaded = sem("selectors_loaded")
                with nc.Block() as block:
                    @block.sync
                    def _(sp):
                        sp.dma_start(m.sel[:], sel).then_inc(loaded, 16)
                        sp.wait_ge(loaded, 16)

                    @block.vector
                    def _(v):
                        v.memset(m.shift[:, 0:1], -SHIFT)
                        v.memset(m.shift[:, 1:2], SHIFT)
                with nc.Fori(0, groups) as g:
                    layer3_input(nc, m, g)
                    nc.all_engine_barrier(sems_to_clear=used())
                lay = Memory3(m, groups, heads)
                first_front(nc, m, lay)
                nc.all_engine_barrier(sems_to_clear=used())
                with nc.Fori(0, heads * groups // UNITS) as j:
                    some_units(nc, m, lay, j)
                    nc.all_engine_barrier(sems_to_clear=used())
                last_back(nc, m, lay)

        stored = ctx.enter_context(nc.semaphore("stored"))
        with nc.Block() as block:
            @block.sync
            def _(sp):
                n = groups * GS
                sp.dma_start(out[0:n].rearrange("b t f -> t b f"), m.h_all[:, 0:n * F].rearrange("t (b f) -> t b f", f=F)).then_inc(stored, 16)
                sp.wait_ge(stored, 16)


def kernel(**inputs):
    import concourse.bacc as bacc
    from concourse.bass_utils import run_bass_kernel_spmd

    arrays = lay_out({k: np.asarray(v) for k, v in inputs.items()})
    nc = bacc.Bacc("TRN2", target_bir_lowering=False, num_devices=1)
    args = {k: nc.dram_tensor(k + "_dram", a.shape, mybir.dt.from_np(a.dtype), kind="ExternalInput").ap() for k, a in arrays.items()}
    out = nc.dram_tensor("out_dram", (SEQS, T, F), F32, kind="ExternalOutput").ap()
    audio_tower(nc, **args, out=out)
    r = run_bass_kernel_spmd(nc, [{k + "_dram": a for k, a in arrays.items()}], core_ids=[0])
    return r.results[0]["out_dram"]
```
